# Optimizing a Trainium2 kernel written in Bass

```python
import numpy as np
import jax
import jax.numpy as jnp

def _softmax(x, axis=-1):
    return jax.nn.softmax(x, axis=axis)

def _gelu(x):
    return jax.nn.gelu(x, approximate=True)

def _silu(x):
    return jax.nn.silu(x)

def _sigmoid(x):
    return jax.nn.sigmoid(x)

def _layernorm(x, axis=-1, eps=1e-05):
    m = jnp.mean(x, axis=axis, keepdims=True)
    v = jnp.var(x, axis=axis, keepdims=True)
    return (x - m) / jnp.sqrt(v + eps)

def _scatter_add(tgt, idx, src, axis=0):
    return tgt.at[idx].add(src)

def _segment_sum(src, seg, n):
    return jax.ops.segment_sum(src, seg, n)
kernel_name = 'mk_perceiver_d1_seqx_r2_d92c35'

def setup_inputs(seed: int=0):
    np.random.seed(seed)
    _w = jnp.asarray

    def _rec_inputs():
        import jax
        import jax.numpy as jnp
        _rk = jax.random.key(seed)
        x = 7.22e-05 + 1 * jax.random.normal(jax.random.fold_in(_rk, 1), (16, 64, 512), jnp.float32)
        _lenS = 64 - jax.random.randint(jax.random.fold_in(_rk, 7), (16,), 0, max(1, 64 // 4) + 1, jnp.int32)
        _lenS2 = 1601 - jax.random.randint(jax.random.fold_in(_rk, 8), (16,), 0, max(1, 1601 // 4) + 1, jnp.int32)
        _ctx_1024P = jax.random.normal(jax.random.fold_in(_rk, 11), (16, 16, 512), jnp.float32)
        _ctx_1024c = jax.random.dirichlet(jax.random.fold_in(_rk, 511), 0.3 * jnp.ones((16,), jnp.float32), (16, 1601))
        _ctx_1024t = jnp.einsum('bsk,bkd->bsd', _ctx_1024c, _ctx_1024P)
        _ctx_1024t = _ctx_1024t * jax.lax.rsqrt(jnp.mean(jnp.square(_ctx_1024t)) + 1e-12) * 0.953939
        ctx_1024 = 4.13588e-05 + 0.999923 * (_ctx_1024t + 0.3 * jax.random.normal(jax.random.fold_in(_rk, 611), (16, 1601, 512), jnp.float32))
        return (x, ctx_1024)
    x, ctx_1024 = _rec_inputs()

    def _L0_xattn_setup():
        import jax, jax.numpy as jnp
        import numpy as np
        DIM = 512
        NUM_HEADS = 16
        HEAD_DIM = DIM // NUM_HEADS
        SCALE = HEAD_DIM ** (-0.5)
        key = jax.random.key(seed)
        ks = jax.random.split(key, 11)
        B, N = (4, 1024)
        init = 1.0 / np.sqrt(DIM)
        return {'q': jax.random.normal(ks[0], (B, N, DIM), jnp.float32), 'k': jax.random.normal(ks[1], (B, N, DIM), jnp.float32), 'v': jax.random.normal(ks[2], (B, N, DIM), jnp.float32), 'wq': jax.random.normal(ks[3], (DIM, DIM), jnp.float32) * init, 'bq': jax.random.normal(ks[4], (DIM,), jnp.float32) * init, 'wk': jax.random.normal(ks[5], (DIM, DIM), jnp.float32) * init, 'bk': jax.random.normal(ks[6], (DIM,), jnp.float32) * init, 'wv': jax.random.normal(ks[7], (DIM, DIM), jnp.float32) * init, 'bv': jax.random.normal(ks[8], (DIM,), jnp.float32) * init, 'wo': jax.random.normal(ks[9], (DIM, DIM), jnp.float32) * init, 'bo': jax.random.normal(ks[10], (DIM,), jnp.float32) * init}
    _L0_xattn_all = _L0_xattn_setup()
    _L0_xattn_in = {k: v for k, v in _L0_xattn_all.items() if k in ('wq', 'bq', 'wk', 'bk', 'wv', 'bv', 'wo', 'bo')}
    del _L0_xattn_all

    def _L0_attn_setup():
        import jax, jax.numpy as jnp
        import numpy as np
        from functools import partial
        B, S, D = (8, 1024, 512)
        HEADS, DIM_HEAD = (16, 64)
        MAX_ALLOWABLE = 512 * 512 * 8

        def _max_pow2_divides(n):
            i = 1
            while n % 2 == 0:
                i *= 2
                n //= 2
            return i

        def _n_splits(bh, sq, sk):
            dimprod = bh * sq * sk
            true_divisor = dimprod / MAX_ALLOWABLE
            if true_divisor < 1:
                return 1
            if true_divisor >= bh:
                return bh
            nearest_pow2 = 2 ** np.round(np.log2(true_divisor))
            return int(min(_max_pow2_divides(bh), nearest_pow2))

        def _sdp_attention(q, k, v, scale):
            scores = jnp.einsum('bid,bjd->bij', q, k) * scale
            probs = jax.nn.softmax(scores, axis=2)
            return jnp.einsum('bij,bjd->bid', probs, v)

        def _scan_attention(q, k, v, scale, n_splits):
            bh = q.shape[0]
            nq, nk, nv = [h.reshape(n_splits, bh // n_splits, h.shape[-2], h.shape[-1]) for h in (q, k, v)]

            def body(carry, args):
                cq, ck, cv = args
                return (None, _sdp_attention(cq, ck, cv, scale))
            outs = jax.lax.scan(body, None, (nq, nk, nv))[1]
            return outs.reshape(-1, outs.shape[-2], outs.shape[-1])

        def _heads_to_batch(t, heads):
            b, s, d = t.shape
            return t.reshape(b, s, heads, d // heads).transpose(0, 2, 1, 3).reshape(b * heads, s, d // heads)

        def _batch_to_heads(t, heads):
            bh, s, d = t.shape
            return t.reshape(bh // heads, heads, s, d).transpose(0, 2, 1, 3).reshape(bh // heads, s, d * heads)
        key = jax.random.key(seed)
        k1, k2, k3, k4 = jax.random.split(key, 4)
        inner = HEADS * DIM_HEAD
        return {'hidden_states': jax.random.normal(k1, (B, S, D), jnp.float32), 'Wq': jax.random.normal(k2, (D, inner), jnp.float32) * D ** (-0.5), 'Wkv': jax.random.normal(k3, (D, 2 * inner), jnp.float32) * D ** (-0.5), 'Wo': jax.random.normal(k4, (inner, D), jnp.float32) * inner ** (-0.5), 'bo': jnp.zeros((D,), jnp.float32)}
    _L0_attn_all = _L0_attn_setup()
    _L0_attn_in = {k: v for k, v in _L0_attn_all.items() if k in ('Wq', 'Wkv', 'Wo', 'bo')}
    del _L0_attn_all

    def _L0_ffn_setup():
        import jax, jax.numpy as jnp
        import numpy as np
        B, L, M = (4, 1024, 512)
        G, E = (8, 8)
        CAP_FACTOR = 2.0

        def _ffn_size(m, widening=8.0):
            f = int(widening * m) * 2 // 3
            return f + (8 - f) % 8
        H = _ffn_size(M)

        def _gating_top2(logits, C):
            Gd, Sd, Ed = logits.shape
            raw = jax.nn.softmax(logits, axis=-1)
            idx1 = jnp.argmax(raw, axis=-1)
            m1 = jax.nn.one_hot(idx1, Ed, dtype=logits.dtype)
            gate1 = jnp.sum(raw * m1, axis=-1)
            rest = raw * (1.0 - m1)
            idx2 = jnp.argmax(rest, axis=-1)
            m2 = jax.nn.one_hot(idx2, Ed, dtype=logits.dtype)
            gate2 = jnp.sum(rest * m2, axis=-1)
            p1 = jnp.cumsum(m1, axis=-2) - m1
            m1 = m1 * (p1 < C).astype(m1.dtype)
            p1 = jnp.sum(p1 * m1, axis=-1)
            m1_flat = jnp.sum(m1, axis=-1)
            m1_count = jnp.sum(m1, axis=-2)
            p2 = jnp.cumsum(m2, axis=-2) - m2 + m1_count[:, None, :]
            m2 = m2 * (p2 < C).astype(m2.dtype)
            p2 = jnp.sum(p2 * m2, axis=-1)
            m2_flat = jnp.sum(m2, axis=-1)
            gate1 = gate1 * m1_flat
            gate2 = gate2 * m2_flat
            c1 = (gate1[..., None] * jax.nn.one_hot(idx1, Ed, dtype=jnp.float32))[..., None] * jax.nn.one_hot(p1.astype(jnp.int32), C, dtype=jnp.float32)[:, :, None, :]
            c2 = (gate2[..., None] * jax.nn.one_hot(idx2, Ed, dtype=jnp.float32))[..., None] * jax.nn.one_hot(p2.astype(jnp.int32), C, dtype=jnp.float32)[:, :, None, :]
            combine = (c1 + c2).astype(logits.dtype)
            dispatch = (combine != 0).astype(logits.dtype)
            return (dispatch, combine)
        key = jax.random.key(seed)
        k0, k1, k2, k3, k4 = jax.random.split(key, 5)
        return {'inputs': jax.random.normal(k0, (B, L, M), jnp.float32), 'router_w': jax.random.normal(k1, (M, E), jnp.float32) * 0.02, 'w0_kernel': jax.random.normal(k2, (E, M, H), jnp.float32) * 0.02, 'w1_kernel': jax.random.normal(k3, (E, M, H), jnp.float32) * 0.02, 'wo_kernel': jax.random.normal(k4, (E, H, M), jnp.float32) * 0.02}
    _L0_ffn_all = _L0_ffn_setup()
    _L0_ffn_in = {k: v for k, v in _L0_ffn_all.items() if k in ('router_w', 'w0_kernel', 'w1_kernel', 'wo_kernel')}
    del _L0_ffn_all
    return {'x': x, 'ctx_1024': ctx_1024, 'L0_xattn_wq': _L0_xattn_in['wq'], 'L0_xattn_bq': _L0_xattn_in['bq'], 'L0_xattn_wk': _L0_xattn_in['wk'], 'L0_xattn_bk': _L0_xattn_in['bk'], 'L0_xattn_wv': _L0_xattn_in['wv'], 'L0_xattn_bv': _L0_xattn_in['bv'], 'L0_xattn_wo': _L0_xattn_in['wo'], 'L0_xattn_bo': _L0_xattn_in['bo'], 'L0_attn_Wq': _L0_attn_in['Wq'], 'L0_attn_Wkv': _L0_attn_in['Wkv'], 'L0_attn_Wo': _L0_attn_in['Wo'], 'L0_attn_bo': _L0_attn_in['bo'], 'L0_ffn_router_w': _L0_ffn_in['router_w'], 'L0_ffn_w0_kernel': _L0_ffn_in['w0_kernel'], 'L0_ffn_w1_kernel': _L0_ffn_in['w1_kernel'], 'L0_ffn_wo_kernel': _L0_ffn_in['wo_kernel']}

def reference(x, ctx_1024, L0_xattn_wq, L0_xattn_bq, L0_xattn_wk, L0_xattn_bk, L0_xattn_wv, L0_xattn_bv, L0_xattn_wo, L0_xattn_bo, L0_attn_Wq, L0_attn_Wkv, L0_attn_Wo, L0_attn_bo, L0_ffn_router_w, L0_ffn_w0_kernel, L0_ffn_w1_kernel, L0_ffn_wo_kernel):
    import jax
    import jax.numpy as jnp

    def _L0_xattn_ref(q, k, v, wq, bq, wk, bk, wv, bv, wo, bo):
        import jax, jax.numpy as jnp
        import numpy as np
        DIM = 512
        NUM_HEADS = 16
        HEAD_DIM = DIM // NUM_HEADS
        SCALE = HEAD_DIM ** (-0.5)
        B, Nq, C = q.shape
        Nk = k.shape[1]
        qh = (q @ wq.T + bq).reshape(B, Nq, NUM_HEADS, HEAD_DIM).transpose(0, 2, 1, 3)
        kh = (k @ wk.T + bk).reshape(B, Nk, NUM_HEADS, HEAD_DIM).transpose(0, 2, 1, 3)
        vh = (v @ wv.T + bv).reshape(B, Nk, NUM_HEADS, HEAD_DIM).transpose(0, 2, 1, 3)
        attn = jnp.einsum('bhqd,bhkd->bhqk', qh * SCALE, kh)
        attn = jax.nn.softmax(attn, axis=-1)
        out = jnp.einsum('bhqk,bhkd->bhqd', attn, vh)
        out = out.transpose(0, 2, 1, 3).reshape(B, Nq, C)
        return out @ wo.T + bo

    def _L0_attn_ref(hidden_states, Wq, Wkv, Wo, bo):
        import jax, jax.numpy as jnp
        import numpy as np
        from functools import partial
        B, S, D = (8, 1024, 512)
        HEADS, DIM_HEAD = (16, 64)
        MAX_ALLOWABLE = 512 * 512 * 8

        def _max_pow2_divides(n):
            i = 1
            while n % 2 == 0:
                i *= 2
                n //= 2
            return i

        def _n_splits(bh, sq, sk):
            dimprod = bh * sq * sk
            true_divisor = dimprod / MAX_ALLOWABLE
            if true_divisor < 1:
                return 1
            if true_divisor >= bh:
                return bh
            nearest_pow2 = 2 ** np.round(np.log2(true_divisor))
            return int(min(_max_pow2_divides(bh), nearest_pow2))

        def _sdp_attention(q, k, v, scale):
            scores = jnp.einsum('bid,bjd->bij', q, k) * scale
            probs = jax.nn.softmax(scores, axis=2)
            return jnp.einsum('bij,bjd->bid', probs, v)

        def _scan_attention(q, k, v, scale, n_splits):
            bh = q.shape[0]
            nq, nk, nv = [h.reshape(n_splits, bh // n_splits, h.shape[-2], h.shape[-1]) for h in (q, k, v)]

            def body(carry, args):
                cq, ck, cv = args
                return (None, _sdp_attention(cq, ck, cv, scale))
            outs = jax.lax.scan(body, None, (nq, nk, nv))[1]
            return outs.reshape(-1, outs.shape[-2], outs.shape[-1])

        def _heads_to_batch(t, heads):
            b, s, d = t.shape
            return t.reshape(b, s, heads, d // heads).transpose(0, 2, 1, 3).reshape(b * heads, s, d // heads)

        def _batch_to_heads(t, heads):
            bh, s, d = t.shape
            return t.reshape(bh // heads, heads, s, d).transpose(0, 2, 1, 3).reshape(bh // heads, s, d * heads)
        scale = DIM_HEAD ** (-0.5)
        q = hidden_states @ Wq
        kv = hidden_states @ Wkv
        k, v = jnp.split(kv, 2, axis=-1)
        q = _heads_to_batch(q, HEADS)
        k = _heads_to_batch(k, HEADS)
        v = _heads_to_batch(v, HEADS)
        n_splits = _n_splits(q.shape[0], q.shape[1], k.shape[1])
        out = _scan_attention(q, k, v, scale, n_splits)
        out = _batch_to_heads(out, HEADS)
        return out @ Wo + bo

    def _L0_ffn_ref(inputs, router_w, w0_kernel, w1_kernel, wo_kernel):
        import jax, jax.numpy as jnp
        import numpy as np
        B, L, M = (4, 1024, 512)
        G, E = (8, 8)
        CAP_FACTOR = 2.0

        def _ffn_size(m, widening=8.0):
            f = int(widening * m) * 2 // 3
            return f + (8 - f) % 8
        H = _ffn_size(M)

        def _gating_top2(logits, C):
            Gd, Sd, Ed = logits.shape
            raw = jax.nn.softmax(logits, axis=-1)
            idx1 = jnp.argmax(raw, axis=-1)
            m1 = jax.nn.one_hot(idx1, Ed, dtype=logits.dtype)
            gate1 = jnp.sum(raw * m1, axis=-1)
            rest = raw * (1.0 - m1)
            idx2 = jnp.argmax(rest, axis=-1)
            m2 = jax.nn.one_hot(idx2, Ed, dtype=logits.dtype)
            gate2 = jnp.sum(rest * m2, axis=-1)
            p1 = jnp.cumsum(m1, axis=-2) - m1
            m1 = m1 * (p1 < C).astype(m1.dtype)
            p1 = jnp.sum(p1 * m1, axis=-1)
            m1_flat = jnp.sum(m1, axis=-1)
            m1_count = jnp.sum(m1, axis=-2)
            p2 = jnp.cumsum(m2, axis=-2) - m2 + m1_count[:, None, :]
            m2 = m2 * (p2 < C).astype(m2.dtype)
            p2 = jnp.sum(p2 * m2, axis=-1)
            m2_flat = jnp.sum(m2, axis=-1)
            gate1 = gate1 * m1_flat
            gate2 = gate2 * m2_flat
            c1 = (gate1[..., None] * jax.nn.one_hot(idx1, Ed, dtype=jnp.float32))[..., None] * jax.nn.one_hot(p1.astype(jnp.int32), C, dtype=jnp.float32)[:, :, None, :]
            c2 = (gate2[..., None] * jax.nn.one_hot(idx2, Ed, dtype=jnp.float32))[..., None] * jax.nn.one_hot(p2.astype(jnp.int32), C, dtype=jnp.float32)[:, :, None, :]
            combine = (c1 + c2).astype(logits.dtype)
            dispatch = (combine != 0).astype(logits.dtype)
            return (dispatch, combine)
        Bb, Ll, Mm = inputs.shape
        S = Bb * Ll // G
        x = inputs.reshape(G, S, Mm)
        logits = jnp.einsum('GSM,ME->GSE', x, router_w)
        cap = int(CAP_FACTOR * S / E)
        C = (cap + 3) // 4 * 4
        dispatch, combine = _gating_top2(logits, C)
        expert_inputs = jnp.einsum('GSEC,GSM->EGCM', dispatch, x)
        layer_w0 = jnp.einsum('EGCM,EMH->EGCH', expert_inputs, w0_kernel)
        layer_w1 = jnp.einsum('EGCM,EMH->EGCH', expert_inputs, w1_kernel)
        hidden = jax.nn.gelu(layer_w0, approximate=True) * layer_w1
        expert_outputs = jnp.einsum('EGCH,EHM->EGCM', hidden, wo_kernel)
        out = jnp.einsum('EGCM,GSEC->GSM', expert_outputs, combine)
        return out.reshape(Bb, Ll, Mm)
    x = x + _L0_xattn_ref(_layernorm(x, axis=-1), ctx_1024, ctx_1024, L0_xattn_wq, L0_xattn_bq, L0_xattn_wk, L0_xattn_bk, L0_xattn_wv, L0_xattn_bv, L0_xattn_wo, L0_xattn_bo)
    x = x + _L0_attn_ref(_layernorm(x, axis=-1), L0_attn_Wq, L0_attn_Wkv, L0_attn_Wo, L0_attn_bo)
    x = x + _L0_ffn_ref(_layernorm(x, axis=-1), L0_ffn_router_w, L0_ffn_w0_kernel, L0_ffn_w1_kernel, L0_ffn_wo_kernel)
    return x

_drawn_inputs = setup_inputs


def setup_inputs(seed=0):
    import zlib

    import numpy as np

    out = dict(_drawn_inputs(seed))
    spreads = {'L0_attn_bo': (0.0, 0.1)}
    factors = {'L0_xattn_bq': 5.913, 'L0_xattn_bk': 8.0}
    for name, (base, spread) in spreads.items():
        noise = np.random.default_rng([zlib.crc32(name.encode()), seed]).standard_normal(out[name].shape)
        drawn = base * np.exp(spread * noise) if base else spread * noise
        out[name] = jnp.asarray(drawn.astype(out[name].dtype))
    for name, factor in factors.items():
        out[name] = (out[name] * factor).astype(out[name].dtype)
    return out
```

```python
from contextlib import ExitStack

import concourse.bass as bass
from concourse import mybir
import numpy as np

P = 128
D = 512
KC = D // P
NQ = 64
H = 16
DH = D // H
NK = 1601
CH = 402
NC = 4
LAST = NK - (NC - 1) * CH
KT = -(-NK // P)
HW = 256
EPS = 1e-5
SCALE = DH ** -0.5

SH = 64
SI = H * SH
SSCALE = SH ** -0.5

E = 8
CAP = 32
ROWS = 256
FC = 22

F32 = mybir.dt.float32
F32R = mybir.dt.float32r
ALU = mybir.AluOpType
ACT = mybir.ActivationFunctionType
AX = mybir.AxisListType


def tile_rows(t):
    return min(P, NK - P * t)


def tile_chunk(t):
    return (min(P * t + P, NK) - 1) // CH


CROSS_STEPS = [("S", 0), ("V", 0), ("S", 1), ("K", 1), ("S", 2), ("T", 0), ("S", 3), ("K", 2),
               ("S", 4), ("T", 1), ("S", 5), ("K", 3), ("V", 1), ("S", 6), ("T", 2), ("S", 7),
               ("Q", 0), ("Ka", 0), ("T", 3), ("N", 0), ("Kb", 0)]
CHUNKS_OF = {"K": range(NC), "Ka": range(2), "Kb": range(2, NC)}
TU = (KT + 1) // 2
UNITS_OF = {"S": 0, "Q": 0, "V": KT, "K": NC, "Ka": 2, "Kb": NC - 2, "T": TU, "N": 2}
UNITS = sum(UNITS_OF[kind] for kind, _ in CROSS_STEPS)
HIS = UNITS - UNITS_OF["N"]
BANKS = 3
assert UNITS % BANKS == 0


def cross_steps(last):
    at = hi = 0
    for kind, n in CROSS_STEPS:
        if last and kind in ("Ka", "Kb", "Q"):
            continue
        yield kind, n, at, hi
        at += UNITS_OF[kind]
        hi += 0 if kind == "N" else UNITS_OF[kind]


def freed_by(t):
    return [c for c in range(NC) if min(CH * (c + 1) - 1, NK - 1) // P == t]


def cross_attention(nc, x, ctx, wq, bq, wk, bk, wv, bv, ident_in, sel_in, q_scr, o_scr, batches):
    rows = batches * NQ
    tiles = rows // P
    QN = min(512, rows)
    with ExitStack() as es:
        def sb(name, shape, dt=F32):
            return es.enter_context(nc.sbuf_tensor(name, shape, dt))

        def sem(name):
            return es.enter_context(nc.semaphore(name))

        raw = sb("xa_raw", [P, 2, KC, CH])
        cxh = sb("xa_cxh", [P, KC, NC * CH], F32R)
        cxl = sb("xa_cxl", [P, KC, NC * CH], F32R)
        wkh = sb("xa_wkh", [P, KC, D], F32R)
        wkl = sb("xa_wkl", [P, KC, D], F32R)
        wvh = sb("xa_wvh", [P, KC, D], F32R)
        wvl = sb("xa_wvl", [P, KC, D], F32R)
        kth = sb("xa_kth", [P, 2, NC * CH], F32R)
        ktl = sb("xa_ktl", [P, 2, NC * CH], F32R)
        vh = sb("xa_vh", [P, KT, HW], F32R)
        vl = sb("xa_vl", [P, KT, HW], F32R)
        probs = sb("xa_probs", [P, 3, NC * CH])
        pth = sb("xa_pth", [P, 2, 512], F32R)
        ptl = sb("xa_ptl", [P, 2, 512], F32R)
        qraw = sb("xa_qraw", [P, 4, NQ])
        qbh = sb("xa_qbh", [P, 4, 2, P], F32R)
        qbl = sb("xa_qbl", [P, 4, 2, P], F32R)
        xnT = sb("xa_xnT", [P, KC, 1024])
        ident = sb("xa_ident", [P, P])
        sel = sb("xa_sel", [P, 2, P])
        eye2 = sb("xa_eye2", [P, NQ])
        bqs = sb("xa_bqs", [P, 4])
        bias = sb("xa_bias", [P, 3, 4])
        mx = sb("xa_mx", [P, 2, 2])
        negmax = sb("xa_negmax", [P, 2])
        rowsum = sb("xa_rowsum", [P, 2, 8])
        total = sb("xa_total", [P, 8])
        inv = sb("xa_inv", [P, 8])
        diag = sb("xa_diag", [P, 8, NQ])
        outT = sb("xa_outT", [P, 4, NQ])
        outn = sb("xa_outn", [P, 4, NQ])
        stat = sb("xa_stat", [P, 2, 6])
        mv = sb("xa_mv", [P, 2, 2])
        rstd = sb("xa_rstd", [P, 2, 1])
        pf = probs[:, :, :].rearrange("p a n -> p (a n)")
        wq_sb = pf[:, 0:2048].rearrange("p (k n) -> p k n", k=KC)
        xt = pf[:, 2048:3072].rearrange("p (a n) -> p a n", a=2)
        xn = pf[:, 3072:4096].rearrange("p (a n) -> p a n", a=2)
        qst = pf[:, 4096:4096 + 512]
        wkv_raw = xnT[:, :, :].rearrange("p k n -> p (k n)").rearrange("p (a k n) -> p a k n", a=2, k=KC)

        sps = es.enter_context(nc.psum_tensor("xa_sps", [P, 4, 512], F32))
        work = es.enter_context(nc.psum_tensor("xa_work", [P, 3, 512], F32))
        ops = es.enter_context(nc.psum_tensor("xa_ops", [P, 512], F32))

        s_const = sem("xa_const")
        s_wkv = sem("xa_wkv")
        s_x = [sem("xa_x0"), sem("xa_x1")]
        s_raw = [sem("xa_raw0"), sem("xa_raw1")]
        s_qin = sem("xa_qin")
        s_qout = sem("xa_qout")
        s_oout = sem("xa_oout")
        s_zero = sem("xa_zero")
        s_whi = sem("xa_whi")
        s_wlo = sem("xa_wlo")
        s_ln = sem("xa_ln")
        s_var = sem("xa_var")
        s_std = sem("xa_std")
        s_xn = sem("xa_xn")
        s_xT = sem("xa_xT")
        s_xTc = sem("xa_xTc")
        s_bqs = sem("xa_bqs_ready")
        s_q = sem("xa_q")
        s_qs = sem("xa_qs")
        s_cxh = sem("xa_cxh_ready")
        s_cx = sem("xa_cx_ready")
        s_full = sem("xa_full")
        s_hi = sem("xa_hi")
        s_evac = sem("xa_evac")
        s_scores = sem("xa_scores")
        s_mx = sem("xa_mx_part")
        s_negmax = sem("xa_negmax_ready")
        s_exp = sem("xa_exp")
        s_pv = sem("xa_pv")
        s_out = sem("xa_out")
        s_tot = sem("xa_tot")
        s_diag = sem("xa_diag_ready")
        s_outr = sem("xa_outn_ready")
        s_qh = sem("xa_qh")
        s_qb = sem("xa_qb")

        KPRO = NC
        QU = 4 * (rows // QN)
        CONSTS = 7 * 16

        def unit(b, u):
            return b * UNITS + KPRO + u

        def hi_part(b, h):
            return b * HIS + KPRO + h

        def bank(u):
            return (KPRO + u) % BANKS

        def prob_slot(n):
            return n // 2 % 2 if n % 2 == 0 else 2

        block = es.enter_context(nc.Block())

        @block.sync
        def _(sp):
            def chunk(b, c):
                sp.dma_start(raw[:, c % 2, :, :], ctx[b, c, :, :, :]).then_inc(s_raw[c % 2], 16)

            sp.dma_start(wkv_raw[:, 0, :, :], wk).then_inc(s_wkv, 16)
            sp.dma_start(wkv_raw[:, 1, :, :], wv).then_inc(s_wkv, 16)
            chunk(0, 0)
            chunk(0, 1)
            for t in range(tiles):
                if t >= 2:
                    sp.wait_ge(s_xn, t - 1)
                sp.dma_start(xt[:, t % 2, :], x[t, :, :]).then_inc(s_x[t % 2], 16)
            for c in range(2, NC):
                sp.wait_ge(s_cx, c - 1)
                chunk(0, c)
            sp.sem_inc(s_oout, 16)
            sp.wait_ge(s_qout, 16 * QU)
            sp.dma_start(qraw[:, :, :], q_scr[0, :, :, :]).then_inc(s_qin, 16)

            def batch(b, last):
                if not last:
                    for c in range(NC):
                        sp.wait_ge(s_cx, b * NC + c + 3)
                        chunk(b + 1, c)
                        if c == 1:
                            sp.wait_ge(s_qb, b + 1)
                            sp.dma_start(qraw[:, :, :], q_scr[b + 1, :, :, :]).then_inc(s_qin, 16)
                sp.wait_ge(s_outr, 2 * b + 2)
                sp.dma_start(o_scr[b, :, :, :], outn[:, :, :]).then_inc(s_oout, 16)

            if batches > 1:
                with sp.Fori(0, batches - 1) as b:
                    batch(b, False)
            batch(batches - 1, True)
            sp.wait_ge(s_oout, 16 * batches + 16)

        @block.gpsimd
        def _(pool):
            pool.dma_start(ident[:, :], ident_in).then_inc(s_const, 16)
            pool.dma_start(sel[:, :, :], sel_in[:, 0:2 * P].rearrange("p (a n) -> p a n", a=2)).then_inc(s_const, 16)
            pool.dma_start(eye2[:, :], sel_in[:, 2 * P:2 * P + NQ]).then_inc(s_const, 16)
            for n, v in enumerate((bq, bk, bv)):
                pool.dma_start(bias[:, n, :], v).then_inc(s_const, 16)
            pool.dma_start(wq_sb, wq).then_inc(s_const, 16)
            nc.gpsimd.memset(qbh[:, :, :, :].bitcast(F32), 0.0).then_inc(s_zero, 1)
            nc.gpsimd.memset(qbl[:, :, :, :].bitcast(F32), 0.0).then_inc(s_zero, 1)

        @block.scalar
        def _(act):
            def split_chunk(b, c):
                act.wait_ge(s_raw[c % 2], 16 * (2 * b + c // 2 + 1))
                nc.scalar.activation(cxh[:, :, CH * c:CH * (c + 1)], raw[:, c % 2, :, :], ACT.Copy).then_inc(s_cxh, 1)

            def queries(b):
                act.wait_ge(s_qin, 16 * b + 16)
                for r in range(4):
                    ins = nc.scalar.activation(qbh[32 * r:32 * r + 32, :, r // 2, NQ * (r % 2):NQ * (r % 2 + 1)],
                                               qraw[32 * r:32 * r + 32, :, :], ACT.Copy)
                ins.then_inc(s_qh, 1)

            def k_units(b, j, chunks, u0):
                for n, c in enumerate(chunks):
                    act.wait_ge(s_full, unit(b, u0 + n) + 1)
                    nc.scalar.activation(kth[:, j % 2, CH * c:CH * (c + 1)], work[:, bank(u0 + n), 0:CH],
                                         ACT.Identity, bias=bias[:, 1, j:j + 1]).then_inc(s_hi, 1)

            act.sem_inc(s_exp, 1)
            act.sem_inc(s_out, 1)
            act.wait_ge(s_wkv, 32)
            for n, w in enumerate((wkh, wvh)):
                nc.scalar.activation(w[:, :, :], wkv_raw[:, n, :, :], ACT.Copy).then_inc(s_whi, 1)
            split_chunk(0, 0)
            split_chunk(0, 1)
            act.wait_ge(s_const, CONSTS)
            nc.scalar.mul(bqs[:, :], bias[:, 0, :], SCALE).then_inc(s_bqs, 1)
            act.wait_ge(s_wlo, 2)
            for t in range(tiles):
                act.wait_ge(s_var, t + 1)
                nc.scalar.activation(rstd[:, t % 2, :], rstd[:, t % 2, :], ACT.Sqrt).then_inc(s_std, 1)
                act.wait_ge(s_xT, t + 1)
                nc.scalar.activation(xnT[:, :, P * t:P * (t + 1)],
                                     sps[:, t % 4, :].rearrange("p (k n) -> p k n", k=KC), ACT.Copy).then_inc(s_xTc, 1)
            for c in range(2, NC):
                split_chunk(0, c)
            act.wait_ge(s_bqs, 1)
            for u in range(QU):
                act.wait_ge(s_q, u + 1)
                if u:
                    act.wait_ge(s_qout, 16 * u)
                nc.scalar.activation(qst[:, 0:QN], sps[:, u % 4, 0:QN], ACT.Identity, bias=bqs[:, u % 4:u % 4 + 1],
                                     scale=SCALE).then_inc(s_qs, 1)
                act.wait_ge(s_qs, u + 1)
                b0 = (u // 4) * (QN // NQ)
                act.dma_start(q_scr[b0:b0 + QN // NQ, :, u % 4, :].rearrange("b p n -> p b n"),
                              qst[:, 0:QN].rearrange("p (b n) -> p b n", n=NQ)).then_inc(s_qout, 16)
            act.wait_ge(s_zero, 2)
            queries(0)
            k_units(0, 0, range(NC), -KPRO)

            def batch(b, last):
                for kind, n, u0, _ in cross_steps(last):
                    if kind == "S":
                        act.wait_ge(s_negmax, 8 * b + n + 1)
                        nc.scalar.activation(probs[:, prob_slot(n), 0:3 * CH].rearrange("p (c n) -> p c n", c=3),
                                             sps[:, 0:3, 0:CH], ACT.Exp, bias=negmax[:, n % 2:n % 2 + 1],
                                             accum_out=rowsum[:, 0, n:n + 1])
                        nc.scalar.activation(probs[:, prob_slot(n), 3 * CH:NK], sps[:, 3, 0:LAST], ACT.Exp,
                                             bias=negmax[:, n % 2:n % 2 + 1],
                                             accum_out=rowsum[:, 1, n:n + 1]).then_inc(s_exp, 1)
                    elif kind in CHUNKS_OF:
                        k_units(b, n, CHUNKS_OF[kind], u0)
                    elif kind == "V":
                        for t in range(KT):
                            m = tile_rows(t)
                            act.wait_ge(s_full, unit(b, u0 + t) + 1)
                            nc.scalar.activation(vh[0:m, t, :], work[0:m, bank(u0 + t), 0:HW], ACT.Copy)\
                              .then_inc(s_hi, 1)
                            if n and not last:
                                for c in freed_by(t):
                                    split_chunk(b + 1, c)
                    elif kind == "T":
                        for d in range(TU):
                            m, w = tile_rows(2 * d), 256 * min(2, KT - 2 * d)
                            tn = TU * n + d
                            act.wait_ge(s_pv, 4 * TU * b + tn + 1)
                            act.wait_ge(s_full, unit(b, u0 + d) + 1)
                            nc.scalar.activation(pth[0:m, tn % 2, 0:w], work[0:m, bank(u0 + d), 0:w], ACT.Copy)\
                              .then_inc(s_hi, 1)
                        act.wait_ge(s_pv, 4 * TU * b + TU * (n + 1) + 2)
                        for r in range(4):
                            ins = nc.scalar.activation(outT[32 * r:32 * r + 32, n, :],
                                                       ops[32 * r:32 * r + 32, NQ * r:NQ * (r + 1)], ACT.Copy)
                        ins.then_inc(s_out, 1)
                    elif kind == "Q":
                        queries(b + 1)

            if batches > 1:
                with act.Fori(0, batches - 1) as b:
                    batch(b, False)
            batch(batches - 1, True)

        @block.vector
        def _(dve):
            def split_chunk(b, c):
                dve.wait_ge(s_cxh, NC * b + c + 1)
                nc.vector.tensor_tensor(cxl[:, :, CH * c:CH * (c + 1)], raw[:, c % 2, :, :],
                                        cxh[:, :, CH * c:CH * (c + 1)], ALU.subtract).then_inc(s_cx, 1)

            def queries(b):
                dve.wait_ge(s_qh, b + 1)
                for r in range(4):
                    at = (slice(32 * r, 32 * r + 32), slice(None), r // 2, slice(NQ * (r % 2), NQ * (r % 2 + 1)))
                    ins = nc.vector.tensor_tensor(qbl[at], qraw[32 * r:32 * r + 32, :, :], qbh[at], ALU.subtract)
                ins.then_inc(s_qb, 1)

            def k_units(b, j, chunks, u0, h0):
                for n, c in enumerate(chunks):
                    dve.wait_ge(s_hi, hi_part(b, h0 + n) + 1)
                    at = (slice(None), j % 2, slice(CH * c, CH * (c + 1)))
                    nc.vector.scalar_tensor_tensor(ktl[at], work[:, bank(u0 + n), 0:CH], bias[:, 1, j:j + 1],
                                                   kth[at], ALU.add, ALU.subtract).then_inc(s_evac, 1)

            for n, (wh, wl) in enumerate(((wkh, wkl), (wvh, wvl))):
                dve.wait_ge(s_whi, n + 1)
                nc.vector.tensor_tensor(wl[:, :, :], wkv_raw[:, n, :, :], wh[:, :, :], ALU.subtract).then_inc(s_wlo, 1)
            split_chunk(0, 0)
            split_chunk(0, 1)
            for t in range(tiles):
                a = t % 2
                dve.wait_ge(s_x[a], 16 * (t // 2 + 1))
                nc.vector.bn_stats(stat[:, a, :], xt[:, a, :]).then_inc(s_ln, 1)
                dve.wait_ge(s_ln, 3 * t + 1)
                nc.vector.bn_aggr(mv[:, a, :], stat[:, a, :]).then_inc(s_ln, 1)
                dve.wait_ge(s_ln, 3 * t + 2)
                nc.vector.tensor_scalar(rstd[:, a, :], mv[:, a, 1:2], EPS, None, ALU.add).then_inc(s_var, 1)
                dve.wait_ge(s_std, t + 1)
                nc.vector.reciprocal(rstd[:, a, :], rstd[:, a, :]).then_inc(s_ln, 1)
                dve.wait_ge(s_ln, 3 * t + 3)
                if t >= 2:
                    dve.wait_ge(s_xT, t - 1)
                nc.vector.tensor_scalar(xn[:, a, :], xt[:, a, :], mv[:, a, 0:1], rstd[:, a, :],
                                        ALU.subtract, ALU.mult).then_inc(s_xn, 1)
            for c in range(2, NC):
                split_chunk(0, c)
            dve.wait_ge(s_zero, 2)
            queries(0)
            dve.wait_ge(s_const, CONSTS)
            k_units(0, 0, range(NC), -KPRO, -KPRO)

            def batch(b, last):
                for kind, n, u0, h0 in cross_steps(last):
                    if kind == "S":
                        a = n % 2
                        dve.wait_ge(s_scores, 8 * b + n + 1)
                        nc.vector.tensor_reduce(mx[:, a, 0:1], sps[:, 0:3, 0:CH], AX.XY, ALU.max).then_inc(s_mx, 1)
                        nc.vector.tensor_reduce(mx[:, a, 1:2], sps[:, 3, 0:LAST], AX.X, ALU.max).then_inc(s_mx, 1)
                        dve.wait_ge(s_mx, 16 * b + 2 * n + 2)
                        nc.vector.tensor_scalar(negmax[:, a:a + 1], mx[:, a, 0:1], mx[:, a, 1:2], -1.0,
                                                ALU.max, ALU.mult).then_inc(s_negmax, 1)
                    elif kind in CHUNKS_OF:
                        k_units(b, n, CHUNKS_OF[kind], u0, h0)
                    elif kind == "V":
                        for t in range(KT):
                            m = tile_rows(t)
                            dve.wait_ge(s_hi, hi_part(b, h0 + t) + 1)
                            nc.vector.tensor_tensor(vl[0:m, t, :], work[0:m, bank(u0 + t), 0:HW], vh[0:m, t, :],
                                                    ALU.subtract).then_inc(s_evac, 1)
                            if n and not last:
                                for c in freed_by(t):
                                    split_chunk(b + 1, c)
                    elif kind == "T":
                        if n == 3:
                            dve.wait_ge(s_exp, 8 * b + 9)
                            nc.vector.tensor_tensor(total[:, :], rowsum[:, 0, :], rowsum[:, 1, :], ALU.add).then_inc(s_tot, 1)
                            dve.wait_ge(s_tot, 2 * b + 1)
                            nc.vector.reciprocal(inv[:, :], total[:, :]).then_inc(s_tot, 1)
                            dve.wait_ge(s_tot, 2 * b + 2)
                            nc.vector.tensor_tensor(diag[:, :, :], eye2[:, :].unsqueeze(1).to_broadcast([P, 8, NQ]),
                                                    inv[:, :].unsqueeze(2).to_broadcast([P, 8, NQ]), ALU.mult)\
                              .then_inc(s_diag, 1)
                        for d in range(TU):
                            m, w = tile_rows(2 * d), 256 * min(2, KT - 2 * d)
                            a = (TU * n + d) % 2
                            dve.wait_ge(s_hi, hi_part(b, h0 + d) + 1)
                            nc.vector.tensor_tensor(ptl[0:m, a, 0:w], work[0:m, bank(u0 + d), 0:w], pth[0:m, a, 0:w],
                                                    ALU.subtract).then_inc(s_evac, 1)
                    elif kind == "Q":
                        queries(b + 1)
                    elif kind == "N":
                        dve.wait_ge(s_oout, 16 * b + 16)
                        for rr in range(2):
                            at = (slice(None), slice(2 * rr, 2 * rr + 2), slice(None))
                            dve.wait_ge(s_out, 4 * b + 2 * rr + 3)
                            dve.wait_ge(s_full, unit(b, u0 + rr) + 1)
                            nc.vector.tensor_tensor(outn[at], outT[at],
                                                    work[:, bank(u0 + rr), 0:P].rearrange("p (g n) -> p g n", g=2),
                                                    ALU.mult).then_inc(s_evac, 1)
                            dve.wait_ge(s_evac, unit(b, u0 + rr) + 1)
                            nc.vector.tensor_tensor(outn[at], outn[at],
                                                    bias[:, 2, 2 * rr:2 * rr + 2].unsqueeze(2).to_broadcast([P, 2, NQ]),
                                                    ALU.add).then_inc(s_outr, 1)

            if batches > 1:
                with dve.Fori(0, batches - 1) as b:
                    batch(b, False)
            batch(batches - 1, True)

        @block.tensor
        def _(pe):
            def product3(out, lh, ll, rh, rl, start, stop):
                nc.tensor.matmul(out, lh, rh, start=start, stop=False)
                nc.tensor.matmul(out, lh, rl, start=False, stop=False)
                return nc.tensor.matmul(out, ll, rh, start=False, stop=stop)

            def free_bank(b, u):
                if not (isinstance(b, int) and unit(b, u) < BANKS):
                    pe.wait_ge(s_evac, unit(b, u) - BANKS + 1)

            def k_units(b, b_ctx, j, chunks, u0):
                for n, c in enumerate(chunks):
                    free_bank(b, u0 + n)
                    pe.wait_ge(s_cx, NC * b_ctx + c + 1)
                    for k in range(KC):
                        w = (slice(None), k, slice(P * j, P * (j + 1)))
                        at = (slice(None), k, slice(CH * c, CH * (c + 1)))
                        ins = product3(work[:, bank(u0 + n), 0:CH], wkh[w], wkl[w], cxh[at], cxl[at],
                                       k == 0, k == KC - 1)
                    ins.then_inc(s_full, 1)

            pe.sem_inc(s_pv, 2)
            pe.wait_ge(s_const, CONSTS)
            for t in range(tiles):
                pe.wait_ge(s_xn, t + 1)
                if t >= 4:
                    pe.wait_ge(s_xTc, t - 3)
                for k in range(KC):
                    ins = nc.tensor.transpose(sps[:, t % 4, P * k:P * (k + 1)], xn[:, t % 2, P * k:P * (k + 1)],
                                              ident[:, :])
                ins.then_inc(s_xT, 1)
            pe.wait_ge(s_xTc, tiles)
            for u in range(QU):
                if u >= 4:
                    pe.wait_ge(s_qs, u - 3)
                for k in range(KC):
                    ins = nc.tensor.matmul(sps[:, u % 4, 0:QN], wq_sb[:, k, P * (u % 4):P * (u % 4 + 1)],
                                           xnT[:, k, QN * (u // 4):QN * (u // 4 + 1)],
                                           start=(k == 0), stop=(k == KC - 1))
                ins.then_inc(s_q, 1)
            pe.wait_ge(s_wlo, 2)
            k_units(0, 0, 0, range(NC), -KPRO)
            pe.wait_ge(s_qs, QU)

            def batch(b, last):
                for kind, n, u0, _ in cross_steps(last):
                    j = n // 2
                    if kind == "S":
                        if n == 0:
                            pe.wait_ge(s_qb, b + 1)
                        if n % 2 == 0:
                            pe.wait_ge(s_evac, unit(b, k_end[j] if j else 0))
                        pe.wait_ge(s_exp, 8 * b + n + 1)
                        for c in range(NC):
                            at = (slice(None), j % 2, slice(CH * c, CH * (c + 1)))
                            ins = product3(sps[:, c, 0:CH], qbh[:, j, n % 2, :], qbl[:, j, n % 2, :],
                                           kth[at], ktl[at], True, True)
                        ins.then_inc(s_scores, 1)
                    elif kind in CHUNKS_OF:
                        k_units(b, b + 1 if n == 0 else b, n, CHUNKS_OF[kind], u0)
                    elif kind == "V":
                        for t in range(KT):
                            m = tile_rows(t)
                            free_bank(b, u0 + t)
                            pe.wait_ge(s_cx, NC * b + tile_chunk(t) + 1)
                            for k in range(KC):
                                at = (slice(None), k, slice(P * t, P * t + m))
                                w = (slice(None), k, slice(HW * n, HW * (n + 1)))
                                ins = product3(work[0:m, bank(u0 + t), 0:HW], cxh[at], cxl[at], wvh[w], wvl[w],
                                               k == 0, k == KC - 1)
                            ins.then_inc(s_full, 1)
                    elif kind == "T":
                        def turn(d):
                            free_bank(b, u0 + d)
                            for tt in range(min(2, KT - 2 * d)):
                                t = 2 * d + tt
                                m = tile_rows(t)
                                for pp in range(2):
                                    at = 256 * tt + P * pp
                                    ins = nc.tensor.transpose(work[0:m, bank(u0 + d), at:at + P],
                                                              probs[:, prob_slot(2 * n + pp), P * t:P * t + m],
                                                              ident[:, :])
                            ins.then_inc(s_full, 1)

                        def meet(d):
                            pe.wait_ge(s_evac, unit(b, u0 + d) + 1)
                            for tt in range(min(2, KT - 2 * d)):
                                t = 2 * d + tt
                                m = tile_rows(t)
                                v = (slice(0, m), t, slice(P * (n % 2), P * (n % 2 + 1)))
                                at = (slice(0, m), (TU * n + d) % 2, slice(256 * tt, 256 * (tt + 1)))
                                ins = product3(ops[:, 0:256], vh[v], vl[v], pth[at], ptl[at], t == 0, t == KT - 1)
                            ins.then_inc(s_pv, 1)

                        pe.wait_ge(s_exp, 8 * b + 2 * n + 3)
                        turn(0)
                        pe.wait_ge(s_out, 4 * b + n + 1)
                        for d in range(1, TU):
                            turn(d)
                            meet(d - 1)
                        meet(TU - 1)
                    elif kind == "N":
                        pe.wait_ge(s_diag, b + 1)
                        for rr in range(2):
                            free_bank(b, u0 + rr)
                            for pp in range(2):
                                ins = nc.tensor.matmul(work[:, bank(u0 + rr), 0:P], sel[:, pp, :],
                                                       diag[:, 4 * rr + pp:4 * rr + pp + 3:2, :],
                                                       start=(pp == 0), stop=(pp == 1))
                            ins.then_inc(s_full, 1)

            k_end = {n: u0 + NC for kind, n, u0, _ in cross_steps(False) if kind == "K"}

            if batches > 1:
                with pe.Fori(0, batches - 1) as b:
                    batch(b, False)
            batch(batches - 1, True)


SELF_STEPS = [("TQ", 0), ("TL", -1), ("O1", 1), ("LG", -1), ("S", 0), ("TX", 1), ("QK", 1), ("TP", 0),
              ("PR", 1), ("O2", 0)]
SELF_UNITS = {"TQ": 0, "TL": 1, "O1": 1, "LG": 1, "S": 0, "TX": 1, "QK": 4, "TP": 4, "PR": 2, "O2": 1}
RING = 3
SELF_PER = sum(SELF_UNITS.values())
assert SELF_PER % RING == 0


def numbered(kinds, at):
    first = {}
    for kind in kinds:
        first[kind] = at
        at += SELF_UNITS[kind]
    return first, at


SELF_PROLOGUE, _n = numbered(["O1", "TX", "QK", "PR"], 0)
SELF_BODY, _n = numbered([kind for kind, _ in SELF_STEPS], _n - SELF_UNITS["TL"] - SELF_UNITS["LG"])
SELF_LAST, _n = numbered([kind for kind, shift in SELF_STEPS if shift < 1], SELF_BODY["TL"])
SELF_TAIL, _n = numbered(["TL", "LG"], _n)


def self_attention(nc, x, o_scr, wo1, bo1, wqkv, wo2, bo2, router, ident_in, x2_scr, xn_scr, lg_scr, tiles):
    with ExitStack() as es:
        def sb(name, shape, dt=F32):
            return es.enter_context(nc.sbuf_tensor(name, shape, dt))

        def sem(name):
            return es.enter_context(nc.semaphore(name))

        KI = SI // P
        wqh = sb("sa_wqh", [P, KC, 3 * SI], F32R)
        wql = sb("sa_wql", [P, KC, 3 * SI], F32R)
        woh = sb("sa_woh", [P, KI, D], F32R)
        wol = sb("sa_wol", [P, KI, D], F32R)
        wo1_sb = sb("sa_wo1", [P, KC, D])
        router_sb = sb("sa_router", [P, KC, E])
        stage = sb("sa_stage", [P, 4096])
        kbd = stage[:, 0:2048].rearrange("p (r n) -> p r n", r=KI)
        qT = stage[:, 2048:3072].rearrange("p (r n) -> p r n", r=KI)
        pT = stage[:, 3072:4096].rearrange("p (a h n) -> p a h n", a=2, h=4)
        ident = sb("sa_ident", [P, P])
        bos = sb("sa_bos", [P, 2, D])
        oin = sb("sa_oin", [P, KC, P])
        xin = sb("sa_xin", [P, D])
        xb = sb("sa_xb", [P, D])
        x1 = sb("sa_x1", [P, D])
        x1b = sb("sa_x1b", [P, D])
        xn = sb("sa_xn", [P, D])
        xTh = sb("sa_xTh", [P, KC, P], F32R)
        xTl = sb("sa_xTl", [P, KC, P], F32R)
        rows = sb("sa_rows", [P, 3, SI])
        prob = sb("sa_prob", [P, H, P])
        aTh = sb("sa_aTh", [P, KI, P], F32R)
        aTl = sb("sa_aTl", [P, KI, P], F32R)
        x2 = sb("sa_x2", [P, D])
        xn3 = sb("sa_xn3", [P, D])
        xn3T = sb("sa_xn3T", [P, KC, P])
        lg = sb("sa_lg", [P, E])
        stat = sb("sa_stat", [P, 2, 6])
        mv = sb("sa_mv", [P, 2, 2])
        rstd = sb("sa_rstd", [P, 2, 1])
        idle = sb("sa_idle", [P, 2])
        mx = sb("sa_mx", [P, H])
        tot = sb("sa_tot", [P, 2, H])

        big = es.enter_context(nc.psum_tensor("sa_big", [P, 4, 512], F32))
        ring = es.enter_context(nc.psum_tensor("sa_ring", [P, RING, 512], F32))

        s_const = sem("sa_const")
        s_stage = [sem("sa_stage0"), sem("sa_stage1")]
        s_whi = sem("sa_whi")
        s_wlo = sem("sa_wlo")
        s_zero = sem("sa_zero")
        s_oin = sem("sa_oin_ready")
        s_xin = sem("sa_xin_ready")
        s_xb = sem("sa_xb_ready")
        s_x1b = sem("sa_x1b_ready")
        s_ln = [sem("sa_ln1"), sem("sa_ln3")]
        s_var = [sem("sa_var1"), sem("sa_var3")]
        s_std = [sem("sa_std1"), sem("sa_std3")]
        s_xn = sem("sa_xn_ready")
        s_xn3 = sem("sa_xn3_ready")
        s_xTh = sem("sa_xTh_ready")
        s_full = sem("sa_full")
        s_free = [sem(f"sa_free{i}") for i in range(RING)]
        s_tq = sem("sa_tq")
        s_qT = sem("sa_qT_ready")
        s_kbd = sem("sa_kbd_ready")
        s_s = sem("sa_scores")
        s_sm = sem("sa_softmax")
        s_sub = sem("sa_sub")
        s_exp = sem("sa_exp")
        s_prob = sem("sa_prob_ready")
        s_pv = sem("sa_pv")
        s_aTh = sem("sa_aTh_ready")
        s_aTl = sem("sa_aTl_ready")
        s_x2o = sem("sa_x2_out")
        s_xno = sem("sa_xn_out")
        s_lgo = sem("sa_lg_out")

        CONSTS = 5 * 16
        PROLOGUE, TAIL = -1, tiles

        def steps(t, last):
            for kind, shift in SELF_STEPS:
                if not ((shift < 0 and isinstance(t, int) and t == 0) or (shift > 0 and last)):
                    yield kind, shift

        def first(kind, tb):
            if isinstance(tb, int) and tb == PROLOGUE:
                return SELF_PROLOGUE[kind], 0
            if isinstance(tb, int) and tb >= tiles - 1:
                return (SELF_TAIL if tb == TAIL else SELF_LAST)[kind], tiles - 1
            if isinstance(tb, int) and tb == 0 and kind == "O1":
                return SELF_BODY[kind] + SELF_UNITS["LG"], 0
            return SELF_BODY[kind], tb

        def number(kind, tb, i=0):
            c, n = first(kind, tb)
            return n * SELF_PER + c + i

        def bank(kind, tb, i=0):
            return (first(kind, tb)[0] + i) % RING

        def uses(kind, tb, i=0):
            c, n = first(kind, tb)
            return n * (SELF_PER // RING) + (c + i) // RING

        def filled(eng, kind, tb, i=0):
            eng.wait_ge(s_full, number(kind, tb, i) + 1)

        def emptied(eng, kind, tb, i=0):
            eng.wait_ge(s_free[bank(kind, tb, i)], uses(kind, tb, i) + 1)

        def run(eng, body):
            body(0, tiles == 1)
            if tiles > 2:
                with eng.Fori(1, tiles - 1) as t:
                    body(t, False)
            if tiles > 1:
                body(tiles - 1, True)

        def half(b):
            return slice(NQ * b, NQ * b + NQ)

        block = es.enter_context(nc.Block())

        @block.sync
        def _(sp):
            def inputs(t):
                sp.dma_start(oin[:, :, 0:NQ], o_scr[2 * t, :, :, :]).then_inc(s_oin, 16)
                sp.dma_start(oin[:, :, NQ:P], o_scr[2 * t + 1, :, :, :]).then_inc(s_oin, 16)
                sp.dma_start(xin[:, :], x[t, :, :]).then_inc(s_xin, 16)

            for s in (s_x2o, s_xno, s_lgo):
                sp.sem_inc(s, 16)
            sp.dma_start(wo1_sb[:, :, :], wo1).then_inc(s_const, 16)
            inputs(0)
            sp.dma_start(ident[:, :], ident_in).then_inc(s_const, 16)
            sp.dma_start(bos[:, 0, :], bo1.to_broadcast([P, D])).then_inc(s_const, 16)
            sp.dma_start(bos[:, 1, :], bo2.to_broadcast([P, D])).then_inc(s_const, 16)
            sp.dma_start(router_sb[:, :, :], router).then_inc(s_const, 16)
            for n in range(8):
                if n >= 2:
                    sp.wait_ge(s_wlo, n - 1)
                dst = stage[:, 2048 * (n % 2):2048 * (n % 2 + 1)].rearrange("p (k n) -> p k n", k=KC)
                src = wqkv[:, :, D * n:D * (n + 1)] if n < 6 else wo2[:, KC * (n - 6):KC * (n - 5), :]
                sp.dma_start(dst, src).then_inc(s_stage[n % 2], 16)

            def logits_out(t, tb):
                emptied(sp, "LG", tb)
                sp.dma_start(lg_scr[t, :, :], lg[:, :]).then_inc(s_lgo, 16)

            def body(t, last):
                if not last:
                    sp.wait_ge(s_var[0], t + 1)
                    inputs(t + 1)
                if not (isinstance(t, int) and t == 0):
                    logits_out(t - 1, t)
                emptied(sp, "O2", t)
                sp.dma_start(x2_scr[t, :, :], x2[:, :]).then_inc(s_x2o, 16)
                sp.wait_ge(s_xn3, t + 1)
                sp.dma_start(xn_scr[t, :, :], xn3[:, :]).then_inc(s_xno, 16)

            run(sp, body)
            logits_out(tiles - 1, TAIL)
            for s in (s_x2o, s_xno, s_lgo):
                sp.wait_ge(s, 16 * tiles + 16)

        @block.scalar
        def _(act):
            def root(a, t):
                act.wait_ge(s_var[a], t + 1)
                nc.scalar.activation(rstd[:, a, :], rstd[:, a, :], ACT.Sqrt).then_inc(s_std[a], 1)

            def step(kind, t, tb):
                if kind == "O1":
                    root(0, t)
                elif kind == "TX":
                    filled(act, kind, tb)
                    nc.scalar.activation(xTh[:, :, :], ring[:, bank(kind, tb), :].rearrange("p (k n) -> p k n", k=KC),
                                         ACT.Copy).then_inc(s_xTh, 1)
                elif kind in ("QK", "PR"):
                    n0 = 0 if kind == "QK" else 4
                    for i in range(SELF_UNITS[kind]):
                        n = n0 + i
                        filled(act, kind, tb, i)
                        nc.scalar.activation(rows[:, n // 2, D * (n % 2):D * (n % 2 + 1)],
                                             ring[:, bank(kind, tb, i), :], ACT.Copy).then_inc(s_free[bank(kind, tb, i)], 1)
                elif kind == "TQ":
                    for i in range(2):
                        act.wait_ge(s_tq, 4 * t + i + 1)
                        nc.scalar.activation(qT[:, 4 * i:4 * i + 4, :],
                                             big[:, i, :].rearrange("p (r n) -> p r n", r=4), ACT.Copy).then_inc(s_qT, 1)
                elif kind == "S":
                    for b in range(2):
                        act.wait_ge(s_sub, 2 * t + b + 1)
                        pr = prob[half(b), :, half(b)]
                        nc.scalar.activation(pr, pr, ACT.Exp, scale=SSCALE).then_inc(s_exp, 1)
                elif kind == "TP":
                    for i in range(4):
                        filled(act, kind, tb, i)
                        if i >= 2:
                            act.wait_ge(s_pv, 4 * t + i - 1)
                        nc.scalar.activation(pT[:, i % 2, :, :], ring[:, bank(kind, tb, i), :]
                                             .rearrange("p (h n) -> p h n", h=4), ACT.Copy).then_inc(s_free[bank(kind, tb, i)], 1)
                        if i >= 1:
                            heads_hi(t, i - 1)
                    heads_hi(t, 3)
                elif kind == "O2":
                    root(1, t)
                elif kind == "TL":
                    filled(act, kind, tb)
                    nc.scalar.activation(xn3T[:, :, :], ring[:, bank(kind, tb), :].rearrange("p (k n) -> p k n", k=KC),
                                         ACT.Copy).then_inc(s_free[bank(kind, tb)], 1)

            def heads_hi(t, i):
                act.wait_ge(s_pv, 4 * t + i + 1)
                for hh in range(2):
                    src = big[half(hh), i, :].rearrange("p (r n) -> p r n", r=2)
                    ins = nc.scalar.activation(aTh[half(hh), 2 * i:2 * i + 2, :], src[:, :, P * hh:P * (hh + 1)], ACT.Copy)
                ins.then_inc(s_aTh, 1)

            for n in range(8):
                act.wait_ge(s_stage[n % 2], 16 * (n // 2 + 1))
                src = stage[:, 2048 * (n % 2):2048 * (n % 2 + 1)].rearrange("p (k n) -> p k n", k=KC)
                dst = wqh[:, :, D * n:D * (n + 1)] if n < 6 else woh[:, KC * (n - 6):KC * (n - 5), :]
                nc.scalar.activation(dst, src, ACT.Copy).then_inc(s_whi, 1)
                if n == 0:
                    step("O1", 0, PROLOGUE)
                if n == 1:
                    step("TX", 0, PROLOGUE)
            step("QK", 0, PROLOGUE)
            step("PR", 0, PROLOGUE)

            act.wait_ge(s_wlo, 8)

            def body(t, last):
                for kind, shift in steps(t, last):
                    step(kind, t + shift, t)

            run(act, body)
            step("TL", tiles - 1, TAIL)

        @block.vector
        def _(dve):
            def layer_norm(a, t, src, dst, s_dst, out_wait=None):
                nc.vector.bn_stats(stat[:, a, :], src).then_inc(s_ln[a], 1)
                dve.wait_ge(s_ln[a], 3 * t + 1)
                nc.vector.memset(idle[:, a:a + 1], 0.0)
                nc.vector.bn_aggr(mv[:, a, :], stat[:, a, :]).then_inc(s_ln[a], 1)
                dve.wait_ge(s_ln[a], 3 * t + 2)
                nc.vector.tensor_scalar(rstd[:, a, :], mv[:, a, 1:2], EPS, None, ALU.add).then_inc(s_var[a], 1)
                dve.wait_ge(s_std[a], t + 1)
                nc.vector.reciprocal(rstd[:, a, :], rstd[:, a, :]).then_inc(s_ln[a], 1)
                dve.wait_ge(s_ln[a], 3 * t + 3)
                if out_wait is not None:
                    dve.wait_ge(*out_wait)
                nc.vector.tensor_scalar(dst, src, mv[:, a, 0:1], rstd[:, a, :], ALU.subtract, ALU.mult).then_inc(s_dst, 1)

            def step(kind, t, tb):
                if kind == "O1":
                    dve.wait_ge(s_xin, 16 * t + 16)
                    nc.vector.tensor_tensor(xb[:, :], xin[:, :], bos[:, 0, :], ALU.add).then_inc(s_xb, 1)
                    dve.wait_ge(s_xb, t + 1)
                    if not (isinstance(t, int) and t == 0):
                        dve.wait_ge(s_x1b, t)
                    filled(dve, kind, tb)
                    nc.vector.tensor_tensor(x1[:, :], ring[:, bank(kind, tb), :], xb[:, :], ALU.add).then_inc(s_free[bank(kind, tb)], 1)
                    emptied(dve, kind, tb)
                    layer_norm(0, t, x1[:, :], xn[:, :], s_xn)
                elif kind == "TX":
                    dve.wait_ge(s_xTh, t + 1)
                    nc.vector.tensor_tensor(xTl[:, :, :], ring[:, bank(kind, tb), :].rearrange("p (k n) -> p k n", k=KC),
                                            xTh[:, :, :], ALU.subtract).then_inc(s_free[bank(kind, tb)], 1)
                elif kind == "TQ":
                    for i in range(2):
                        dve.wait_ge(s_tq, 4 * t + i + 3)
                        for hh in range(2):
                            ins = nc.vector.tensor_copy(kbd[half(hh), 4 * i:4 * i + 4, P * hh:P * (hh + 1)],
                                                        big[half(hh), 2 + i, :].rearrange("p (r n) -> p r n", r=4))
                        ins.then_inc(s_kbd, 1)
                    nc.vector.tensor_tensor(x1b[:, :], x1[:, :], bos[:, 1, :], ALU.add).then_inc(s_x1b, 1)
                elif kind == "S":
                    dve.wait_ge(s_s, t + 1)
                    for b in range(2):
                        sc = big[half(b), :, :].rearrange("p a (h n) -> p (a h) n", h=4)[:, :, half(b)]
                        nc.vector.tensor_reduce(mx[half(b), :], sc, AX.X, ALU.max).then_inc(s_sm, 1)
                        dve.wait_ge(s_sm, 5 * t + b + 1)
                        nc.vector.tensor_tensor(prob[half(b), :, half(b)], sc,
                                                mx[half(b), :].unsqueeze(2).to_broadcast([NQ, H, NQ]),
                                                ALU.subtract).then_inc(s_sub, 1)
                    for b in range(2):
                        dve.wait_ge(s_exp, 2 * t + b + 1)
                        nc.vector.tensor_reduce(tot[half(b), 0, :], prob[half(b), :, half(b)], AX.X, ALU.add).then_inc(s_sm, 1)
                    dve.wait_ge(s_sm, 5 * t + 4)
                    nc.vector.reciprocal(tot[:, 1, :], tot[:, 0, :]).then_inc(s_sm, 1)
                    dve.wait_ge(s_sm, 5 * t + 5)
                    for b in range(2):
                        nc.vector.tensor_tensor(prob[half(b), :, half(b)], prob[half(b), :, half(b)],
                                                tot[half(b), 1, :].unsqueeze(2).to_broadcast([NQ, H, NQ]),
                                                ALU.mult).then_inc(s_prob, 1)
                elif kind == "TP":
                    for i in range(4):
                        dve.wait_ge(s_aTh, 4 * t + i + 1)
                        for hh in range(2):
                            src = big[half(hh), i, :].rearrange("p (r n) -> p r n", r=2)
                            at = (half(hh), slice(2 * i, 2 * i + 2), slice(None))
                            ins = nc.vector.tensor_tensor(aTl[at], src[:, :, P * hh:P * (hh + 1)], aTh[at], ALU.subtract)
                        ins.then_inc(s_aTl, 1)
                elif kind == "O2":
                    filled(dve, kind, tb)
                    dve.wait_ge(s_x2o, 16 * t + 16)
                    dve.wait_ge(s_x1b, t + 1)
                    nc.vector.tensor_tensor(x2[:, :], ring[:, bank(kind, tb), :], x1b[:, :], ALU.add).then_inc(s_free[bank(kind, tb)], 1)
                    emptied(dve, kind, tb)
                    layer_norm(1, t, x2[:, :], xn3[:, :], s_xn3, (s_xno, 16 * t + 16))
                elif kind == "LG":
                    filled(dve, kind, tb)
                    dve.wait_ge(s_lgo, 16 * t + 16)
                    nc.vector.tensor_copy(lg[:, :], ring[:, bank(kind, tb), 0:E]).then_inc(s_free[bank(kind, tb)], 1)

            nc.vector.memset(prob[:, :, :], 0.0).then_inc(s_zero, 1)
            dve.wait_ge(s_const, CONSTS)
            for n in range(8):
                dve.wait_ge(s_whi, n + 1)
                src = stage[:, 2048 * (n % 2):2048 * (n % 2 + 1)].rearrange("p (k n) -> p k n", k=KC)
                at = (slice(None), slice(None), slice(D * n, D * (n + 1))) if n < 6 else \
                    (slice(None), slice(KC * (n - 6), KC * (n - 5)), slice(None))
                wh, wl = (wqh, wql) if n < 6 else (woh, wol)
                nc.vector.tensor_tensor(wl[at], src, wh[at], ALU.subtract).then_inc(s_wlo, 1)
                if n == 0:
                    step("O1", 0, PROLOGUE)
                if n == 1:
                    step("TX", 0, PROLOGUE)
            dve.wait_ge(s_wlo, 8)
            nc.vector.memset(stage[:, 0:2048], 0.0).then_inc(s_zero, 1)
            dve.wait_ge(s_zero, 2)

            def body(t, last):
                for kind, shift in steps(t, last):
                    step(kind, t + shift, t)

            run(dve, body)
            step("LG", tiles - 1, TAIL)

        @block.tensor
        def _(pe):
            def product3(out, lh, ll, rh, rl, start, stop):
                nc.tensor.matmul(out, lh, rh, start=start, stop=False)
                nc.tensor.matmul(out, lh, rl, start=False, stop=False)
                return nc.tensor.matmul(out, ll, rh, start=False, stop=stop)

            def free_bank(kind, tb, i=0):
                n = uses(kind, tb, i)
                if not (isinstance(n, int) and n == 0):
                    pe.wait_ge(s_free[bank(kind, tb, i)], n)

            def turn4(dst, src):
                for k in range(KC):
                    ins = nc.tensor.transpose(dst[:, P * k:P * (k + 1)], src[:, P * k:P * (k + 1)], ident[:, :])
                return ins

            def step(kind, t, tb):
                if SELF_UNITS[kind]:
                    dst = ring[:, bank(kind, tb), :]
                if kind == "O1":
                    free_bank(kind, tb)
                    pe.wait_ge(s_oin, 32 * t + 32)
                    for k in range(KC):
                        ins = nc.tensor.matmul(dst, oin[:, k, :], wo1_sb[:, k, :], start=(k == 0), stop=(k == KC - 1))
                    ins.then_inc(s_full, 1)
                elif kind == "TX":
                    free_bank(kind, tb)
                    pe.wait_ge(s_xn, t + 1)
                    turn4(dst, xn).then_inc(s_full, 1)
                elif kind in ("QK", "PR"):
                    emptied(pe, "TX", tb)
                    n0 = 0 if kind == "QK" else 4
                    for i in range(SELF_UNITS[kind]):
                        free_bank(kind, tb, i)
                        n = n0 + i
                        if isinstance(t, int) and t == 0:
                            pe.wait_ge(s_wlo, n + 1)
                        for k in range(KC):
                            w = (slice(None), k, slice(D * n, D * (n + 1)))
                            ins = product3(ring[:, bank(kind, tb, i), :], xTh[:, k, :], xTl[:, k, :], wqh[w], wql[w],
                                           k == 0, k == KC - 1)
                        ins.then_inc(s_full, 1)
                elif kind == "TQ":
                    for i in range(4):
                        emptied(pe, "QK", tb - 1, i)
                        turn4(big[:, i, :], rows[:, i // 2, D * (i % 2):D * (i % 2 + 1)]).then_inc(s_tq, 1)
                elif kind == "S":
                    pe.wait_ge(s_qT, 2 * t + 2)
                    pe.wait_ge(s_kbd, 2 * t + 2)
                    for i in range(4):
                        for r in range(2):
                            ins = nc.tensor.matmul(big[:, i, 256 * r:256 * (r + 1)], qT[:, 2 * i + r, :],
                                                   kbd[:, 2 * i + r, :], start=True, stop=True)
                    ins.then_inc(s_s, 1)
                elif kind == "TP":
                    def turn(i):
                        free_bank(kind, tb, i)
                        turn4(ring[:, bank(kind, tb, i), :],
                              prob[:, 4 * i:4 * i + 4, :].rearrange("p h n -> p (h n)")).then_inc(s_full, 1)

                    def meet(i):
                        emptied(pe, kind, tb, i)
                        for r in range(2):
                            pr = 2 * i + r
                            ins = nc.tensor.matmul(big[:, i, 256 * r:256 * (r + 1)], rows[:, 2, P * pr:P * (pr + 1)],
                                                   pT[:, i % 2, 2 * r:2 * r + 2, :], start=True, stop=True)
                        ins.then_inc(s_pv, 1)

                    pe.wait_ge(s_prob, 2 * t + 2)
                    emptied(pe, "PR", tb - 1, 1)
                    turn(0)
                    for i in range(1, 4):
                        turn(i)
                        meet(i - 1)
                    meet(3)
                elif kind == "O2":
                    if isinstance(t, int) and t == 0:
                        pe.wait_ge(s_wlo, 8)
                    free_bank(kind, tb)
                    pe.wait_ge(s_aTl, 4 * t + 4)
                    for k in range(KI):
                        ins = product3(dst, aTh[:, k, :], aTl[:, k, :], woh[:, k, :], wol[:, k, :], k == 0, k == KI - 1)
                    ins.then_inc(s_full, 1)
                elif kind == "TL":
                    free_bank(kind, tb)
                    pe.wait_ge(s_xn3, t + 1)
                    turn4(dst, xn3).then_inc(s_full, 1)
                elif kind == "LG":
                    free_bank(kind, tb)
                    emptied(pe, "TL", tb)
                    for k in range(KC):
                        ins = nc.tensor.matmul(dst[:, 0:E], xn3T[:, k, :], router_sb[:, k, :], start=(k == 0),
                                               stop=(k == KC - 1))
                    ins.then_inc(s_full, 1)

            pe.wait_ge(s_const, CONSTS)
            for kind in ("O1", "TX", "QK", "PR"):
                step(kind, 0, PROLOGUE)

            def body(t, last):
                for kind, shift in steps(t, last):
                    step(kind, t + shift, t)

            run(pe, body)
            step("TL", tiles - 1, TAIL)
            step("LG", tiles - 1, TAIL)


G = 8
SLOTS = E * CAP


def experts(nc, x2_scr, xn_scr, lg_scr, w01, wout, tri_in, rowc_in, ident_in, eo_scr, out):
    with ExitStack() as es:
        def sb(name, shape, dt=F32):
            return es.enter_context(nc.sbuf_tensor(name, shape, dt))

        xeh = sb("mo_xeh", [P, KC, E, ROWS], F32R)
        xel = sb("mo_xel", [P, KC, E, ROWS], F32R)
        combT = sb("mo_combT", [P, 2, G, P])
        route(nc, xn_scr, lg_scr, tri_in, rowc_in, ident_in, xeh, xel, combT)
        run_experts(nc, x2_scr, w01, wout, eo_scr, xeh, xel, combT, out)


def route(nc, xn_scr, lg_scr, tri_in, rowc_in, ident_in, xeh, xel, combT):
    with ExitStack() as es:
        def sb(name, shape, dt=F32):
            return es.enter_context(nc.sbuf_tensor(name, shape, dt))

        def sem(name):
            return es.enter_context(nc.semaphore(name))

        GE = [P, G, E]
        lg = sb("ro_lg", GE)
        xn = sb("ro_xn", [P, G, D])
        xnh = sb("ro_xnh", [P, G, D], F32R)
        xnl = sb("ro_xnl", [P, G, D], F32R)
        tri = sb("ro_tri", [P, 2, P])
        rowc = sb("ro_rowc", [P, E + CAP])
        ident = sb("ro_ident", [P, P])
        top = sb("ro_top", [P, 2, G])
        ex = sb("ro_ex", GE)
        raw = sb("ro_raw", GE)
        rest = sb("ro_rest", GE)
        eq = sb("ro_eq", GE)
        cand = sb("ro_cand", GE)
        pick = sb("ro_pick", [P, G])
        mask = sb("ro_mask", [P, 2, G, E])
        kept = sb("ro_kept", [P, 2, G, E])
        pos = sb("ro_pos", [P, 2, G])
        slot1 = sb("ro_slot1", [P, 2, G, CAP])
        small = sb("ro_small", [P, 2, G])
        parts = sb("ro_parts", [P, 2, G, SLOTS])
        disp = sb("ro_disp", [P, G, SLOTS], F32R)
        pp = es.enter_context(nc.psum_tensor("ro_pp", [P, 2, 512], F32))
        pt = es.enter_context(nc.psum_tensor("ro_pt", [P, 2, 512], F32))
        pd = es.enter_context(nc.psum_tensor("ro_pd", [P, 2, 2, 512], F32))

        s_in = sem("ro_in")
        s_xn = sem("ro_xn_in")
        s_v = sem("ro_v")
        s_d = sem("ro_d")
        s_ex = sem("ro_ex_ready")
        s_m = sem("ro_m")
        s_p = sem("ro_p")
        s_comb = sem("ro_comb")
        s_disp = sem("ro_disp_ready")
        s_xnh = sem("ro_xnh_ready")
        s_xnl = sem("ro_xnl_ready")
        s_t = sem("ro_t")
        s_tc = sem("ro_tc")
        s_x = sem("ro_x")
        s_xh = sem("ro_xh")
        s_xl = sem("ro_xl")
        block = es.enter_context(nc.Block())

        def over(a, n):
            return a.unsqueeze(2).to_broadcast([P, G, n])

        @block.sync
        def _(sp):
            sp.dma_start(lg[:, :, :], lg_scr.rearrange("g p e -> p g e")).then_inc(s_in, 16)
            sp.dma_start(rowc[:, :], rowc_in).then_inc(s_in, 16)
            sp.dma_start(tri[:, :, :], tri_in).then_inc(s_in, 16)
            sp.dma_start(ident[:, :], ident_in).then_inc(s_in, 16)
            sp.dma_start(xn[:, :, :], xn_scr.rearrange("g p m -> p g m")).then_inc(s_xn, 16)

        @block.scalar
        def _(act):
            act.wait_ge(s_d, 1)
            nc.scalar.activation(ex[:, :, :], ex[:, :, :], ACT.Exp).then_inc(s_ex, 1)
            act.wait_ge(s_xn, 16)
            for g in range(G):
                nc.scalar.activation(xnh[:, g, :], xn[:, g, :], ACT.Copy).then_inc(s_xnh, 1)
            for i in range(4):
                act.wait_ge(s_t, i + 1)
                nc.scalar.activation(combT[:, :, 2 * i:2 * i + 2, :].rearrange("p h g n -> p g h n"),
                                     pt[:, i % 2, :].rearrange("p (g h n) -> p g h n", g=2, h=2), ACT.Copy)\
                  .then_inc(s_tc, 1)
            for n in range(2 * G):
                g, kk = n // 2, n % 2
                act.wait_ge(s_x, n + 1)
                for k in range(2):
                    ins = nc.scalar.activation(xeh[:, 2 * kk + k, :, CAP * g:CAP * (g + 1)],
                                               pd[:, n % 2, 0, 256 * k:256 * (k + 1)].rearrange("p (e c) -> p e c", e=E),
                                               ACT.Copy)
                ins.then_inc(s_xh, 1)

        @block.vector
        def _(dve):
            steps = [0]

            def after():
                dve.wait_ge(s_v, steps[0])

            def do(ins):
                steps[0] += 1
                ins.then_inc(s_v, 1)

            v = nc.vector
            em8 = rowc[:, 0:E].unsqueeze(1).to_broadcast(GE)
            dve.wait_ge(s_in, 64)
            do(v.tensor_reduce(pick[:, :], lg[:, :, :], AX.X, ALU.max))
            after()
            v.tensor_tensor(ex[:, :, :], lg[:, :, :], over(pick[:, :], E), ALU.subtract).then_inc(s_d, 1)
            dve.wait_ge(s_ex, 1)
            do(v.tensor_reduce(small[:, 0, :], ex[:, :, :], AX.X, ALU.add))
            after()
            do(v.reciprocal(small[:, 1, :], small[:, 0, :]))
            after()
            do(v.tensor_tensor(raw[:, :, :], ex[:, :, :], over(small[:, 1, :], E), ALU.mult))
            after()
            for i, src in enumerate((raw, rest)):
                if i:
                    do(v.tensor_tensor(cand[:, :, :], raw[:, :, :], mask[:, 0, :, :], ALU.mult))
                    after()
                    do(v.tensor_tensor(rest[:, :, :], raw[:, :, :], cand[:, :, :], ALU.subtract))
                    after()
                do(v.tensor_reduce(top[:, i, :], src[:, :, :], AX.X, ALU.max))
                after()
                do(v.tensor_tensor(eq[:, :, :], src[:, :, :], over(top[:, i, :], E), ALU.is_equal))
                after()
                do(v.tensor_tensor(cand[:, :, :], eq[:, :, :], em8, ALU.mult))
                after()
                do(v.tensor_reduce(pick[:, :], cand[:, :, :], AX.X, ALU.min))
                after()
                v.tensor_tensor(mask[:, i, :, :], over(pick[:, :], E), em8, ALU.is_equal).then_inc(s_m, 1)
                dve.wait_ge(s_m, i + 1)
            for i in range(2):
                dve.wait_ge(s_p, i + 1)
                p = pp[:, i, 0:G * E].rearrange("p (g e) -> p g e", g=G)
                v.scalar_tensor_tensor(kept[:, i, :, :].rearrange("p g e -> p (g e)"), pp[:, i, 0:G * E], float(CAP),
                                       mask[:, i, :, :].rearrange("p g e -> p (g e)"), ALU.is_lt, ALU.mult)\
                 .then_inc(s_m, 1)
                dve.wait_ge(s_m, i + 3)
                do(v.tensor_tensor(cand[:, :, :], p, kept[:, i, :, :], ALU.mult))
                after()
                do(v.tensor_reduce(pos[:, i, :], cand[:, :, :], AX.X, ALU.add))
                after()
                do(v.tensor_tensor(slot1[:, i, :, :], rowc[:, E:E + CAP].unsqueeze(1).to_broadcast([P, G, CAP]),
                                   over(pos[:, i, :], CAP), ALU.is_equal))
                do(v.tensor_tensor(eq[:, :, :], kept[:, i, :, :], over(top[:, i, :], E), ALU.mult))
                after()
                for g in range(G):
                    ins = v.tensor_tensor(parts[:, i, g, :].rearrange("p (e c) -> p e c", e=E),
                                          eq[:, g, :].unsqueeze(2).to_broadcast([P, E, CAP]),
                                          slot1[:, i, g, :].unsqueeze(1).to_broadcast([P, E, CAP]), ALU.mult)
                do(ins)
                after()
            do(v.tensor_tensor(parts[:, 0, :, :], parts[:, 0, :, :], parts[:, 1, :, :], ALU.add))
            after()
            v.tensor_scalar(disp[:, :, :], parts[:, 0, :, :], 0.0, None, ALU.not_equal).then_inc(s_disp, 1)
            for g in range(G):
                dve.wait_ge(s_xnh, g + 1)
                v.tensor_tensor(xnl[:, g, :], xn[:, g, :], xnh[:, g, :], ALU.subtract).then_inc(s_xnl, 1)
            for n in range(2 * G):
                g, kk = n // 2, n % 2
                dve.wait_ge(s_x, n + 1)
                for k in range(2):
                    ins = v.tensor_copy(xel[:, 2 * kk + k, :, CAP * g:CAP * (g + 1)],
                                        pd[:, n % 2, 1, 256 * k:256 * (k + 1)].rearrange("p (e c) -> p e c", e=E))
                ins.then_inc(s_xl, 1)

        @block.tensor
        def _(pe):
            pe.wait_ge(s_in, 64)
            pe.wait_ge(s_m, 1)
            nc.tensor.matmul(pp[:, 0, 0:G * E], tri[:, 0, :], mask[:, 0, :, :].rearrange("p g e -> p (g e)"),
                             start=True, stop=True).then_inc(s_p, 1)
            pe.wait_ge(s_m, 3)
            nc.tensor.matmul(pp[:, 1, 0:G * E], tri[:, 0, :], mask[:, 1, :, :].rearrange("p g e -> p (g e)"),
                             start=True, stop=False)
            nc.tensor.matmul(pp[:, 1, 0:G * E], tri[:, 1, :], kept[:, 0, :, :].rearrange("p g e -> p (g e)"),
                             start=False, stop=True).then_inc(s_p, 1)
            pe.wait_ge(s_disp, 1)
            for i in range(4):
                if i >= 2:
                    pe.wait_ge(s_tc, i - 1)
                for j in range(4):
                    g, h = 2 * i + j // 2, j % 2
                    ins = nc.tensor.transpose(pt[:, i % 2, P * j:P * (j + 1)], parts[:, 0, g, P * h:P * (h + 1)],
                                              ident[:, :])
                ins.then_inc(s_t, 1)
            for n in range(2 * G):
                g, kk = n // 2, n % 2
                pe.wait_ge(s_xnl, g + 1)
                if n >= 2:
                    pe.wait_ge(s_xh, n - 1)
                    pe.wait_ge(s_xl, n - 1)
                for part, src in enumerate((xnh, xnl)):
                    for k in range(2):
                        m = P * (2 * kk + k)
                        ins = nc.tensor.matmul(pd[:, n % 2, part, 256 * k:256 * (k + 1)], src[:, g, m:m + P],
                                               disp[:, g, :], start=True, stop=True)
                ins.then_inc(s_x, 1)


def run_experts(nc, x2_scr, w01, wout, eo_scr, xeh, xel, combT, out):
    with ExitStack() as es:
        def sb(name, shape, dt=F32):
            return es.enter_context(nc.sbuf_tensor(name, shape, dt))

        def sem(name):
            return es.enter_context(nc.semaphore(name))

        raw01 = sb("ex_raw01", [P, 2, 2 * KC * P])
        rawo = sb("ex_rawo", [P, 2, D])
        w01h = sb("ex_w01h", [P, 2, 2, KC, P], F32R)
        w01l = sb("ex_w01l", [P, 2, 2, KC, P], F32R)
        woh = sb("ex_woh", [P, 2, D], F32R)
        wol = sb("ex_wol", [P, 2, D], F32R)
        gelu = sb("ex_gelu", [P, 2, ROWS])
        hid = sb("ex_hid", [P, 2, ROWS])
        hh = sb("ex_hh", [P, 2, ROWS], F32R)
        hl = sb("ex_hl", [P, 2, ROWS], F32R)
        eo = sb("ex_eo", [P, 2, D])
        eog = sb("ex_eog", [P, 2, G, D])
        x2 = sb("ex_x2", [P, G, D])
        up = es.enter_context(nc.psum_tensor("ex_up", [P, 2, 512], F32))
        acc = es.enter_context(nc.psum_tensor("ex_acc", [P, 2, 512], F32))
        comb = es.enter_context(nc.psum_tensor("ex_comb", [P, 4, 512], F32))

        s_r01 = [sem("ex_r01a"), sem("ex_r01b")]
        s_ro = [sem("ex_roa"), sem("ex_rob")]
        s_h01 = sem("ex_h01")
        s_l01 = sem("ex_l01")
        s_ho = sem("ex_ho")
        s_lo = sem("ex_lo")
        s_up = sem("ex_up_full")
        s_gelu = sem("ex_gelu_ready")
        s_hh = sem("ex_hh_ready")
        s_hl = sem("ex_hl_ready")
        s_down = sem("ex_down")
        s_eo = sem("ex_eo_ready")
        s_eoo = sem("ex_eo_out")
        s_eog = [sem("ex_eog0"), sem("ex_eog1"), sem("ex_eog2")]
        s_x2 = sem("ex_x2_in")
        s_c = sem("ex_c")
        s_sum = sem("ex_sum")
        s_out = sem("ex_out")

        def pieces(eng, e, last, step):
            half = e * (FC // 2)
            step(half, 0, e, True, False, False, False)
            step(half, 1, e, False, False, False, False)
            with eng.Fori(1, FC // 2 - 1) as j:
                step(half + j, 0, e, False, False, False, False)
                step(half + j, 1, e, False, False, False, False)
            step(half + (FC // 2 - 1), 0, e, False, False, last, False)
            step(half + (FC // 2 - 1), 1, e, False, True, last, last)

        block = es.enter_context(nc.Block())

        @block.sync
        def _(sp):
            def load01(n, par):
                sp.dma_start(raw01[:, par, :], w01[n, :, :]).then_inc(s_r01[par], 16)

            def loado(n, par):
                sp.dma_start(rawo[:, par, :], wout[n, :, :]).then_inc(s_ro[par], 16)

            load01(0, 0)
            loado(0, 0)
            load01(1, 1)
            loado(1, 1)
            sp.sem_inc(s_eoo, 32)

            def step(half, par, e, head, tail, no_next2, no_next):
                n = half * 2 + par
                if not no_next2:
                    sp.wait_ge(s_l01, n + 1)
                    load01(n + 2, par)
                    sp.wait_ge(s_lo, n + 1)
                    loado(n + 2, par)

            def expert(e, last):
                pieces(sp, e, last, step)
                sp.wait_ge(s_eo, 2 * e + 4)
                for r in range(2):
                    sp.dma_start(eo_scr[e, P * r:P * (r + 1), :], eo[:, r, :]).then_inc(s_eoo, 16)

            def gather(e, which):
                sp.wait_ge(s_eoo, 32 * e + 64)
                q = CAP * (e % 4)
                sp.dma_start(eog[q:q + CAP, e // 4, :, :], eo_scr[e, :, :].rearrange("(g c) m -> c g m", c=CAP))\
                  .then_inc(s_eog[which], 16)

            with sp.Fori(0, 4) as e:
                expert(e, False)
            sp.dma_start(x2[:, :, :], x2_scr.rearrange("g p m -> p g m")).then_inc(s_x2, 16)
            with sp.Fori(4, E - 1) as e:
                expert(e, False)
            for e in range(E - 1):
                gather(e, e // 4)
            expert(E - 1, True)
            gather(E - 1, 2)
            for g in range(G):
                sp.wait_ge(s_sum, g + 1)
                sp.dma_start(out[g, :, :], x2[:, g, :]).then_inc(s_out, 16)
            sp.wait_ge(s_out, 16 * G)

        def flat01(t, par):
            return t[:, par, :, :, :].rearrange("p a k n -> p (a k n)")

        @block.scalar
        def _(act):
            def hi01(par, count):
                act.wait_ge(s_r01[par], count)
                nc.scalar.activation(flat01(w01h, par), raw01[:, par, :], ACT.Copy).then_inc(s_h01, 1)

            def hio(par, count):
                act.wait_ge(s_ro[par], count)
                nc.scalar.activation(woh[:, par, :], rawo[:, par, :], ACT.Copy).then_inc(s_ho, 1)

            def step(half, par, e, head, tail, no_next2, no_next):
                n = half * 2 + par
                act.wait_ge(s_up, n + 1)
                nc.scalar.activation(gelu[:, par, :], up[:, par, 0:ROWS], ACT.Gelu_apprx_tanh).then_inc(s_gelu, 1)
                if not no_next2:
                    hi01(par, half * 16 + 32)
                if not no_next:
                    act.wait_ge(s_down, n + 1)
                    hio(1 - par, half * 16 + 16 * (1 + par))
                if tail:
                    act.wait_ge(s_down, n + 2)
                    act.wait_ge(s_eoo, 32 * e + 32)
                    nc.scalar.activation(eo[:, 0, :], acc[:, 0, :], ACT.Copy).then_inc(s_eo, 1)

            act.sem_inc(s_eo, 2)
            hi01(0, 16)
            hio(0, 16)
            hi01(1, 16)
            with act.Fori(0, E - 1) as e:
                pieces(act, e, False, step)
            pieces(act, E - 1, True, step)

        @block.vector
        def _(dve):
            def lo01(par, count):
                dve.wait_ge(s_h01, count)
                nc.vector.tensor_tensor(flat01(w01l, par), raw01[:, par, :], flat01(w01h, par), ALU.subtract)\
                  .then_inc(s_l01, 1)

            def loo(par, count):
                dve.wait_ge(s_ho, count)
                nc.vector.tensor_tensor(wol[:, par, :], rawo[:, par, :], woh[:, par, :], ALU.subtract).then_inc(s_lo, 1)

            def step(half, par, e, head, tail, no_next2, no_next):
                n = half * 2 + par
                dve.wait_ge(s_gelu, n + 1)
                nc.vector.tensor_tensor(hid[:, par, :], gelu[:, par, :], up[:, par, ROWS:2 * ROWS], ALU.mult)
                nc.vector.tensor_tensor(hh[:, par, :], gelu[:, par, :], up[:, par, ROWS:2 * ROWS], ALU.mult)\
                  .then_inc(s_hh, 1)
                dve.wait_ge(s_hh, n + 2)
                nc.vector.tensor_tensor(hl[:, par, :], hid[:, par, :], hh[:, par, :], ALU.subtract).then_inc(s_hl, 1)
                if not no_next2:
                    lo01(par, n + 3)
                if not no_next:
                    loo(1 - par, n + 2)
                if tail:
                    dve.wait_ge(s_down, n + 2)
                    dve.wait_ge(s_eoo, 32 * e + 32)
                    nc.vector.tensor_copy(eo[:, 1, :], acc[:, 1, :]).then_inc(s_eo, 1)

            dve.sem_inc(s_hh, 1)
            lo01(0, 1)
            loo(0, 1)
            lo01(1, 2)
            with dve.Fori(0, E - 1) as e:
                pieces(dve, e, False, step)
            pieces(dve, E - 1, True, step)
            dve.wait_ge(s_x2, 16)
            for g in range(G):
                dve.wait_ge(s_c, g + 1)
                nc.vector.tensor_tensor(x2[:, g, :], x2[:, g, :], comb[:, g % 4, :], ALU.add).then_inc(s_sum, 1)

        @block.tensor
        def _(pe):
            def product3(out, lh, ll, rh, rl, start, stop):
                nc.tensor.matmul(out, lh, rh, start=start, stop=False)
                nc.tensor.matmul(out, lh, rl, start=False, stop=False)
                return nc.tensor.matmul(out, ll, rh, start=False, stop=stop)

            def first_products(n, par, e):
                pe.wait_ge(s_l01, n + 1)
                for a in range(2):
                    for k in range(KC):
                        ins = product3(up[:, par, ROWS * a:ROWS * (a + 1)], w01h[:, par, a, k, :], w01l[:, par, a, k, :],
                                       xeh[:, k, e, :], xel[:, k, e, :], k == 0, k == KC - 1)
                ins.then_inc(s_up, 1)

            def step(half, par, e, head, tail, no_next2, no_next):
                n = half * 2 + par
                if not no_next:
                    pe.wait_ge(s_hh, n + 1)
                    first_products(n + 1, 1 - par, e + 1 if tail else e)
                if head:
                    pe.wait_ge(s_eo, 2 * e + 2)
                pe.wait_ge(s_lo, n + 1)
                pe.wait_ge(s_hl, n + 1)
                for r in range(2):
                    at = (slice(None), par, slice(P * r, P * (r + 1)))
                    ins = product3(acc[:, r, :], hh[at], hl[at], woh[:, par, :], wol[:, par, :], head, tail)
                ins.then_inc(s_down, 1)

            pe.sem_inc(s_down, 1)
            first_products(0, 0, 0)
            with pe.Fori(0, E - 1) as e:
                pieces(pe, e, False, step)
            pieces(pe, E - 1, True, step)
            for g0 in (0, 4):
                pe.wait_ge(s_eog[0], 64)
                for g in range(g0, g0 + 4):
                    if g >= 4:
                        pe.wait_ge(s_sum, g - 3)
                    nc.tensor.matmul(comb[:, g % 4, :], combT[:, 0, g, :], eog[:, 0, g, :], start=True, stop=False)
                pe.wait_ge(s_eog[1], 48)
                pe.wait_ge(s_eog[2], 16)
                for g in range(g0, g0 + 4):
                    nc.tensor.matmul(comb[:, g % 4, :], combT[:, 1, g, :], eog[:, 1, g, :], start=False, stop=True)\
                      .then_inc(s_c, 1)


def perceiver_layer(nc, x, ctx, xwq, xbq, xwk, xbk, xwv, xbv, xwo, xbo, wqkv, wo, bo, router, w01, wout,
                    ident, heads, tri, rowc, out):
    batches = ctx.shape[0]
    tiles = batches * NQ // P

    def scratch(name, shape):
        return nc.dram_tensor(name, shape, F32, kind="Internal").ap()

    q_scr = scratch("q_scratch", (batches, P, 4, NQ))
    o_scr = scratch("o_scratch", (batches, P, 4, NQ))
    x2_scr = scratch("x2_scratch", (tiles, P, D))
    xn_scr = scratch("xn_scratch", (tiles, P, D))
    lg_scr = scratch("lg_scratch", (tiles, P, E))
    eo_scr = scratch("eo_scratch", (E, ROWS, D))
    cross_attention(nc, x, ctx, xwq, xbq, xwk, xbk, xwv, xbv, ident, heads, q_scr, o_scr, batches)
    self_attention(nc, x, o_scr, xwo, xbo, wqkv, wo, bo, router, ident, x2_scr, xn_scr, lg_scr, tiles)
    experts(nc, x2_scr, xn_scr, lg_scr, w01, wout, tri, rowc, ident, eo_scr, out)


def by_rows(w):
    return np.ascontiguousarray(w.reshape(-1, P, w.shape[1]).transpose(1, 0, 2))


def by_column(b):
    return np.ascontiguousarray(b.reshape(-1, P).T)


def constants():
    ident = np.eye(P, dtype=np.float32)
    heads = np.zeros((P, 2, P), np.float32)
    for pair in range(2):
        for h in range(2):
            at = DH * (2 * pair + h)
            heads[NQ * h:NQ * (h + 1), pair, at:at + DH] = 1
    eye2 = np.concatenate([np.eye(NQ), np.eye(NQ)]).astype(np.float32)
    heads = np.concatenate([heads.reshape(P, 2 * P), eye2], axis=1)
    tri = np.stack([np.triu(np.ones((P, P)), 1), np.ones((P, P))], axis=1).astype(np.float32)
    rowc = np.tile(np.concatenate([np.arange(E) - E, np.arange(CAP)]).astype(np.float32), (P, 1))
    return ident, heads, tri, rowc


def lay_out(x, ctx_1024, L0_xattn_wq, L0_xattn_bq, L0_xattn_wk, L0_xattn_bk, L0_xattn_wv, L0_xattn_bv, L0_xattn_wo,
            L0_xattn_bo, L0_attn_Wq, L0_attn_Wkv, L0_attn_Wo, L0_attn_bo, L0_ffn_router_w, L0_ffn_w0_kernel,
            L0_ffn_w1_kernel, L0_ffn_wo_kernel):
    b = ctx_1024.shape[0]
    ctx = np.zeros((b, NC * CH, D), np.float32)
    ctx[:, :NK] = ctx_1024
    ctx = np.ascontiguousarray(ctx.reshape(b, NC, CH, KC, P).transpose(0, 1, 4, 3, 2))
    hidden = L0_ffn_w0_kernel.shape[2]
    w01 = np.zeros((E, FC * P, 2, D), np.float32)
    w01[:, :hidden, 0] = L0_ffn_w0_kernel.transpose(0, 2, 1)
    w01[:, :hidden, 1] = L0_ffn_w1_kernel.transpose(0, 2, 1)
    w01 = np.ascontiguousarray(w01.reshape(E, FC, P, 2, KC, P).transpose(0, 1, 5, 3, 4, 2)).reshape(E * FC, P, 2 * KC * P)
    wout = np.zeros((E, FC * P, D), np.float32)
    wout[:, :hidden] = L0_ffn_wo_kernel
    ident, heads, tri, rowc = constants()
    return {
        "x": x.reshape(-1, P, D), "ctx": ctx,
        "xwq": by_rows(L0_xattn_wq.T), "xbq": by_column(L0_xattn_bq),
        "xwk": by_rows(L0_xattn_wk.T), "xbk": by_column(L0_xattn_bk),
        "xwv": by_rows(L0_xattn_wv.T), "xbv": by_column(L0_xattn_bv),
        "xwo": by_rows(L0_xattn_wo.T), "xbo": L0_xattn_bo.reshape(1, D),
        "wqkv": by_rows(np.concatenate([L0_attn_Wq, L0_attn_Wkv], axis=1)),
        "wo": by_rows(L0_attn_Wo), "bo": L0_attn_bo.reshape(1, D), "router": by_rows(L0_ffn_router_w),
        "w01": w01, "wout": wout.reshape(E * FC, P, D),
        "ident": ident, "heads": heads, "tri": tri, "rowc": rowc,
    }


def kernel(**inputs):
    from concourse import bacc
    from concourse.bass_utils import run_bass_kernel_spmd

    inputs = {name: np.asarray(a) for name, a in inputs.items()}
    arrays = lay_out(**inputs)
    nc = bacc.Bacc("TRN2", target_bir_lowering=False, num_devices=1)
    arrays = {f"in_{name}": np.ascontiguousarray(a) for name, a in arrays.items()}
    args = [nc.dram_tensor(name, a.shape, mybir.dt.from_np(a.dtype), kind="ExternalInput").ap()
            for name, a in arrays.items()]
    shape = inputs["x"].shape
    out = nc.dram_tensor("out_x", (shape[0] * shape[1] // P, P, D), F32, kind="ExternalOutput").ap()
    perceiver_layer(nc, *args, out)
    got = run_bass_kernel_spmd(nc, [arrays], core_ids=[0])
    return got.results[0]["out_x"].reshape(shape)
```

```python
from contextlib import ExitStack

import concourse.bass as bass
from concourse import mybir
import numpy as np

P = 128
D = 512
KC = D // P
NQ = 64
H = 16
DH = D // H
NK = 1601
CH = 402
NC = 4
LAST = NK - (NC - 1) * CH
KT = -(-NK // P)
HW = 256
EPS = 1e-5
SCALE = DH ** -0.5

SH = 64
SI = H * SH
SSCALE = SH ** -0.5

E = 8
CAP = 32
ROWS = 256
FC = 22

F32 = mybir.dt.float32
F32R = mybir.dt.float32r
ALU = mybir.AluOpType
ACT = mybir.ActivationFunctionType
AX = mybir.AxisListType


def tile_rows(t):
    return min(P, NK - P * t)


def tile_chunk(t):
    return (min(P * t + P, NK) - 1) // CH


def freed_by(t):
    return [c for c in range(NC) if min(CH * (c + 1) - 1, NK - 1) // P == t]


TU = (KT + 1) // 2


def cross_order():
    def softmax(n, ahead=0):
        return ("S", n, 0, ahead), ("E", n, 0, ahead)

    order = []
    for g in range(4):
        ahead = int(g >= 2)
        s1, e1 = softmax((2 * g + 2) % 8, int(g == 3))
        s2, e2 = softmax((2 * g + 3) % 8, int(g == 3))
        j, j_ahead = (g + 2) % 4, ahead
        ks = [("K", j, c, j_ahead) for c in range(NC)]
        t = [("t", g, d, 0) for d in range(TU)]
        m = [("m", g, d, 0) for d in range(TU)]
        if g == 3:
            order.append(("D", 0, 0, 0))
        order += [s1, t[0]]
        if g:
            order.append(("O", g - 1, 0, 0))
        order += [ks[0], e1, t[1], m[0], ks[1], t[2], m[1]]
        if g % 2 == 0:
            order += [s2, ks[2], e2, t[3], m[2], ks[3]]
            if g == 2:
                order.append(("Q", 0, 0, 1))
            order += [t[4], m[3], t[5], m[4], t[6], m[5], m[6]]
        else:
            v = [("V", 1 - g // 2, n, int(g == 3)) for n in range(KT)]
            order += [ks[2], t[3], m[2], ks[3], s2, t[4], m[3], v[0], e2, v[1], t[5], m[4], v[2], v[3]]
            order += [("X", 0, c, 1) for c in freed_by(3) if g == 1]
            order += [t[6], m[5], v[4], m[6], v[5]]
            if g == 3:
                order.append(("O", 3, 0, 0))
            for n in range(6, KT):
                order.append(v[n])
                if g == 3 and n in (7, 9):
                    order.append(("N", (n - 7) // 2, 0, 0))
                if g == 1:
                    order += [("X", 0, c, 1) for c in freed_by(n)]
    return order


def cross_prologue(tiles, q_units):
    order = [("W", 0), ("X", 0), ("K", 0, 0), ("K", 1, 0), ("W", 1)]
    c = 1
    for t in range(tiles):
        if t % 2 == 0 and c < NC:
            order.append(("X", c))
        order.append(("T", t))
        if c < NC:
            order.append(("K", t % 2, c))
            c += t % 2
    for c in range(c, NC):
        order += [("X", c), ("K", 0, c), ("K", 1, c)]
    for n in range(max(KT, q_units)):
        if n < q_units:
            order.append(("U", n))
        if n < KT:
            order.append(("V", 0, n))
    order += [("Q", 0), ("S", 0), ("E", 0), ("S", 1), ("E", 1)]
    full = []
    for kind, n, *i in order:
        full.append((kind, 0, n, 0) if kind == "X" else (kind, n, i[0] if i else 0, 0))
    return full


ROOM = 3 * SI * KC + D * SI // P + D * KC

BANKS = 3
CROSS_PRO = 2 * NC + KT


def cross_numbered(order, start, last=False):
    unit = hi = start
    for kind, n, i, ahead in order:
        if last and ahead:
            continue
        yield kind, n, i, ahead, unit, hi
        unit += kind in "KVtN"
        hi += kind in "KVt"


CROSS_UNITS = sum(item[0] in "KVtN" for item in cross_order())
CROSS_HIS = sum(item[0] in "KVt" for item in cross_order())
assert CROSS_UNITS % BANKS == 0


def cross_attention(nc, x, ctx, wq, bq, wk, bk, wv, bv, ident_in, sel_in, q_scr, o_scr, batches,
                    room, prefetch):
    rows = batches * NQ
    tiles = rows // P
    QN = min(512, rows)
    with ExitStack() as es:
        def sb(name, shape, dt=F32):
            return es.enter_context(nc.sbuf_tensor(name, shape, dt))

        def sem(name):
            return es.enter_context(nc.semaphore(name))

        cxh = room("xa_cxh", 0, [KC, NC * CH], F32R)
        cxl = room("xa_cxl", KC * NC * CH, [KC, NC * CH], F32R)
        wkh = room("xa_wkh", 2 * KC * NC * CH, [KC, D], F32R)
        raw = room("xa_raw", KC * (2 * NC * CH + D), [2, KC, CH], F32)
        wkl = sb("xa_wkl", [P, KC, D], F32R)
        wvh = sb("xa_wvh", [P, KC, D], F32R)
        wvl = sb("xa_wvl", [P, KC, D], F32R)
        kth = sb("xa_kth", [P, 2, NC * CH], F32R)
        ktl = sb("xa_ktl", [P, 2, NC * CH], F32R)
        vh = sb("xa_vh", [P, KT, HW], F32R)
        vl = sb("xa_vl", [P, KT, HW], F32R)
        probs = sb("xa_probs", [P, 4, NC * CH])
        pth = sb("xa_pth", [P, 2, 512], F32R)
        ptl = sb("xa_ptl", [P, 2, 512], F32R)
        qraw = sb("xa_qraw", [P, 4, NQ])
        qbh = sb("xa_qbh", [P, 4, 2, P], F32R)
        qbl = sb("xa_qbl", [P, 4, 2, P], F32R)
        lnbuf = sb("xa_lnbuf", [P, 2048])
        ident = sb("xa_ident", [P, P])
        sel = sb("xa_sel", [P, 2, P])
        eye2 = sb("xa_eye2", [P, NQ])
        bqs = sb("xa_bqs", [P, 4])
        bias = sb("xa_bias", [P, 3, 4])
        mx = sb("xa_mx", [P, 2, 2])
        negmax = sb("xa_negmax", [P, 2])
        rowsum = sb("xa_rowsum", [P, 2, 8])
        total = sb("xa_total", [P, 8])
        inv = sb("xa_inv", [P, 8])
        diag = sb("xa_diag", [P, 8, NQ])
        outT = sb("xa_outT", [P, 4, NQ])
        outn = sb("xa_outn", [P, 4, NQ])
        stat = sb("xa_stat", [P, 2, 6])
        mv = sb("xa_mv", [P, 2, 2])
        rstd = sb("xa_rstd", [P, 2, 1])
        pf = probs[:, :, :].rearrange("p a n -> p (a n)")
        wkv_raw = pf[:, 0:4096].rearrange("p (a k n) -> p a k n", a=2, k=KC)
        xnT = pf[:, 0:4096].rearrange("p (k n) -> p k n", k=KC)
        wq_sb = pf[:, 4096:6144].rearrange("p (k n) -> p k n", k=KC)
        xt = lnbuf[:, 0:1024].rearrange("p (a n) -> p a n", a=2)
        xn = lnbuf[:, 1024:2048].rearrange("p (a n) -> p a n", a=2)
        qst = lnbuf[:, :].rearrange("p (a n) -> p a n", a=4)

        sps = es.enter_context(nc.psum_tensor("xa_sps", [P, 4, 512], F32))
        work = es.enter_context(nc.psum_tensor("xa_work", [P, 3, 512], F32))
        ops = es.enter_context(nc.psum_tensor("xa_ops", [P, 512], F32))

        s_const = sem("xa_const")
        s_sel = sem("xa_sel_ready")
        s_wq = sem("xa_wq")
        s_wkv = [sem("xa_wk"), sem("xa_wv")]
        s_x = [sem("xa_x0"), sem("xa_x1")]
        s_raw = [sem("xa_raw0"), sem("xa_raw1")]
        s_qin = sem("xa_qin")
        s_qout = [sem(f"xa_qout{i}") for i in range(4)]
        s_oout = sem("xa_oout")
        s_zero = sem("xa_zero")
        s_whi = sem("xa_whi")
        s_wlo = sem("xa_wlo")
        s_ln = sem("xa_ln")
        s_var = sem("xa_var")
        s_std = sem("xa_std")
        s_xn = sem("xa_xn")
        s_xT = sem("xa_xT")
        s_xTc = sem("xa_xTc")
        s_bqs = sem("xa_bqs_ready")
        s_q = sem("xa_q")
        s_qs = sem("xa_qs")
        s_cxh = sem("xa_cxh_ready")
        s_cx = sem("xa_cx_ready")
        s_full = sem("xa_full")
        s_hi = sem("xa_hi")
        s_evac = sem("xa_evac")
        s_scores = sem("xa_scores")
        s_mx = sem("xa_mx_part")
        s_negmax = sem("xa_negmax_ready")
        s_exp = sem("xa_exp")
        s_pv = sem("xa_pv")
        s_out = sem("xa_out")
        s_tot = sem("xa_tot")
        s_diag = sem("xa_diag_ready")
        s_outr = sem("xa_outn_ready")
        s_qh = sem("xa_qh")
        s_qb = sem("xa_qb")

        QU = 4 * (rows // QN)
        CONSTS = 4 * 16
        prologue = list(cross_numbered(cross_prologue(tiles, QU), 0))

        def unit(b, u):
            return b * CROSS_UNITS + u

        def hi_part(b, h):
            return b * CROSS_HIS + h

        def at_keys(c):
            return slice(CH * c, CH * (c + 1))

        block = es.enter_context(nc.Block())

        @block.sync
        def _(sp):
            def chunk(b, c):
                sp.dma_start(raw[:, c % 2, :, :], ctx[b, c, :, :, :]).then_inc(s_raw[c % 2], 16)

            sp.dma_start(wkv_raw[:, 0, :, :], wk).then_inc(s_wkv[0], 16)
            chunk(0, 0)
            sp.dma_start(wkv_raw[:, 1, :, :], wv).then_inc(s_wkv[1], 16)
            chunk(0, 1)
            for c in range(2, NC):
                sp.wait_ge(s_cx, c - 1)
                chunk(0, c)
            sp.sem_inc(s_oout, 16)
            for slot in s_qout:
                sp.wait_ge(slot, 16 * (QU // 4))
            sp.dma_start(qraw[:, :, :], q_scr[0, :, :, :]).then_inc(s_qin, 16)

            def batch(b, last):
                if not last:
                    for c in range(NC):
                        sp.wait_ge(s_cx, b * NC + c + 3)
                        chunk(b + 1, c)
                        if c == 1:
                            sp.wait_ge(s_qb, b + 1)
                            sp.dma_start(qraw[:, :, :], q_scr[b + 1, :, :, :]).then_inc(s_qin, 16)
                sp.wait_ge(s_outr, 2 * b + 2)
                sp.dma_start(o_scr[b, :, :, :], outn[:, :, :]).then_inc(s_oout, 16)

            if batches > 1:
                with sp.Fori(0, batches - 1) as b:
                    batch(b, False)
            v_end = max(u for kind, _, _, _, u, _ in cross_numbered(cross_order(), CROSS_PRO, last=True) if kind == "V")
            sp.wait_ge(s_full, unit(batches - 1, v_end) + 1)
            for dst, src, arrived in prefetch:
                sp.dma_start(dst, src).then_inc(arrived, 16)
            batch(batches - 1, True)
            sp.wait_ge(s_oout, 16 * batches + 16)

        @block.gpsimd
        def _(pool):
            def load_x(t):
                pool.dma_start(xt[:, t % 2, :], x[t, :, :]).then_inc(s_x[t % 2], 16)

            load_x(0)
            pool.dma_start(ident[:, :], ident_in).then_inc(s_const, 16)
            for n, v in enumerate((bq, bk, bv)):
                pool.dma_start(bias[:, n, :], v).then_inc(s_const, 16)
            load_x(1)
            pool.dma_start(sel[:, :, :], sel_in[:, 0:2 * P].rearrange("p (a n) -> p a n", a=2)).then_inc(s_sel, 16)
            pool.dma_start(eye2[:, :], sel_in[:, 2 * P:2 * P + NQ]).then_inc(s_sel, 16)
            nc.gpsimd.memset(qbh[:, :, :, :].bitcast(F32), 0.0).then_inc(s_zero, 1)
            nc.gpsimd.memset(qbl[:, :, :, :].bitcast(F32), 0.0).then_inc(s_zero, 1)
            for t in range(2, tiles):
                pool.wait_ge(s_xn, t - 1)
                load_x(t)
                if t == min(3, tiles - 1):
                    pool.dma_start(wq_sb, wq).then_inc(s_wq, 16)
            if tiles <= 2:
                pool.dma_start(wq_sb, wq).then_inc(s_wq, 16)
            for u in range(QU):
                pool.wait_ge(s_qs, u + 1)
                b0 = (u // 4) * (QN // NQ)
                pool.dma_start(q_scr[b0:b0 + QN // NQ, :, u % 4, :].rearrange("b p n -> p b n"),
                               qst[:, u % 4, 0:QN].rearrange("p (b n) -> p b n", n=NQ)).then_inc(s_qout[u % 4], 16)

        @block.scalar
        def _(act):
            def item(b, kind, n, i, ahead, u, h):
                at_bank = u % BANKS
                if kind == "X":
                    act.wait_ge(s_raw[i % 2], 16 * (2 * (b + ahead) + i // 2 + 1))
                    nc.scalar.activation(cxh[:, :, at_keys(i)], raw[:, i % 2, :, :], ACT.Copy).then_inc(s_cxh, 1)
                elif kind == "Q":
                    act.wait_ge(s_qin, 16 * (b + ahead) + 16)
                    for r in range(4):
                        ins = nc.scalar.activation(qbh[32 * r:32 * r + 32, :, r // 2, NQ * (r % 2):NQ * (r % 2 + 1)],
                                                   qraw[32 * r:32 * r + 32, :, :], ACT.Copy)
                    ins.then_inc(s_qh, 1)
                elif kind == "E":
                    act.wait_ge(s_negmax, 8 * (b + ahead) + n + 1)
                    nc.scalar.activation(probs[:, n % 4, 0:3 * CH].rearrange("p (c n) -> p c n", c=3),
                                         sps[:, 0:3, 0:CH], ACT.Exp, bias=negmax[:, n % 2:n % 2 + 1],
                                         accum_out=rowsum[:, 0, n:n + 1])
                    nc.scalar.activation(probs[:, n % 4, 3 * CH:NK], sps[:, 3, 0:LAST], ACT.Exp,
                                         bias=negmax[:, n % 2:n % 2 + 1],
                                         accum_out=rowsum[:, 1, n:n + 1]).then_inc(s_exp, 1)
                elif kind == "K":
                    act.wait_ge(s_full, unit(b, u) + 1)
                    nc.scalar.activation(kth[:, n % 2, at_keys(i)], work[:, at_bank, 0:CH],
                                         ACT.Identity, bias=bias[:, 1, n:n + 1]).then_inc(s_hi, 1)
                elif kind == "V":
                    m = tile_rows(i)
                    act.wait_ge(s_full, unit(b, u) + 1)
                    nc.scalar.activation(vh[0:m, i, :], work[0:m, at_bank, 0:HW], ACT.Copy).then_inc(s_hi, 1)
                elif kind == "t":
                    m, w = tile_rows(2 * i), 256 * min(2, KT - 2 * i)
                    tn = TU * n + i
                    act.wait_ge(s_pv, 4 * TU * b + tn + 1)
                    act.wait_ge(s_full, unit(b, u) + 1)
                    nc.scalar.activation(pth[0:m, tn % 2, 0:w], work[0:m, at_bank, 0:w], ACT.Copy).then_inc(s_hi, 1)
                elif kind == "O":
                    act.wait_ge(s_pv, 4 * TU * b + TU * (n + 1) + 2)
                    for r in range(4):
                        ins = nc.scalar.activation(outT[32 * r:32 * r + 32, n, :],
                                                   ops[32 * r:32 * r + 32, NQ * r:NQ * (r + 1)], ACT.Copy)
                    ins.then_inc(s_out, 1)
                elif kind == "W":
                    act.wait_ge(s_wkv[n], 16)
                    nc.scalar.activation((wkh, wvh)[n][:, :, :], wkv_raw[:, n, :, :], ACT.Copy).then_inc(s_whi, 1)
                elif kind == "T":
                    act.wait_ge(s_var, n + 1)
                    nc.scalar.activation(rstd[:, n % 2, :], rstd[:, n % 2, :], ACT.Sqrt).then_inc(s_std, 1)
                    act.wait_ge(s_wlo, 2)
                    act.wait_ge(s_xT, n + 1)
                    nc.scalar.activation(xnT[:, :, P * n:P * (n + 1)],
                                         sps[:, n % 4, :].rearrange("p (k n) -> p k n", k=KC),
                                         ACT.Copy).then_inc(s_xTc, 1)
                elif kind == "U":
                    act.wait_ge(s_q, n + 1)
                    if n >= 4:
                        act.wait_ge(s_qout[n % 4], 16 * (n // 4))
                    nc.scalar.activation(qst[:, n % 4, 0:QN], sps[:, n % 4, 0:QN], ACT.Identity,
                                         bias=bqs[:, n % 4:n % 4 + 1], scale=SCALE).then_inc(s_qs, 1)

            act.sem_inc(s_exp, 1)
            act.sem_inc(s_out, 1)
            act.wait_ge(s_const, CONSTS)
            nc.scalar.mul(bqs[:, :], bias[:, 0, :], SCALE).then_inc(s_bqs, 1)
            act.wait_ge(s_bqs, 1)
            for step in prologue:
                if step[0] == "Q":
                    act.wait_ge(s_zero, 2)
                item(0, *step)
            if batches > 1:
                with act.Fori(0, batches - 1) as b:
                    for step in cross_numbered(cross_order(), CROSS_PRO):
                        item(b, *step)
            for step in cross_numbered(cross_order(), CROSS_PRO, last=True):
                item(batches - 1, *step)

        @block.vector
        def _(dve):
            def item(b, kind, n, i, ahead, u, h):
                at_bank = u % BANKS
                if kind == "X":
                    dve.wait_ge(s_cxh, NC * (b + ahead) + i + 1)
                    nc.vector.tensor_tensor(cxl[:, :, at_keys(i)], raw[:, i % 2, :, :], cxh[:, :, at_keys(i)],
                                            ALU.subtract).then_inc(s_cx, 1)
                elif kind == "Q":
                    dve.wait_ge(s_qh, b + ahead + 1)
                    for r in range(4):
                        at = (slice(32 * r, 32 * r + 32), slice(None), r // 2, slice(NQ * (r % 2), NQ * (r % 2 + 1)))
                        ins = nc.vector.tensor_tensor(qbl[at], qraw[32 * r:32 * r + 32, :, :], qbh[at], ALU.subtract)
                    ins.then_inc(s_qb, 1)
                elif kind == "S":
                    a = n % 2
                    dve.wait_ge(s_scores, 8 * (b + ahead) + n + 1)
                    nc.vector.tensor_reduce(mx[:, a, 0:1], sps[:, 0:3, 0:CH], AX.XY, ALU.max).then_inc(s_mx, 1)
                    nc.vector.tensor_reduce(mx[:, a, 1:2], sps[:, 3, 0:LAST], AX.X, ALU.max).then_inc(s_mx, 1)
                    dve.wait_ge(s_mx, 16 * (b + ahead) + 2 * n + 2)
                    nc.vector.tensor_scalar(negmax[:, a:a + 1], mx[:, a, 0:1], mx[:, a, 1:2], -1.0,
                                            ALU.max, ALU.mult).then_inc(s_negmax, 1)
                elif kind == "K":
                    dve.wait_ge(s_hi, hi_part(b, h) + 1)
                    nc.vector.scalar_tensor_tensor(ktl[:, n % 2, at_keys(i)], work[:, at_bank, 0:CH],
                                                   bias[:, 1, n:n + 1], kth[:, n % 2, at_keys(i)],
                                                   ALU.add, ALU.subtract).then_inc(s_evac, 1)
                elif kind == "V":
                    m = tile_rows(i)
                    dve.wait_ge(s_hi, hi_part(b, h) + 1)
                    nc.vector.tensor_tensor(vl[0:m, i, :], work[0:m, at_bank, 0:HW], vh[0:m, i, :],
                                            ALU.subtract).then_inc(s_evac, 1)
                elif kind == "t":
                    m, w = tile_rows(2 * i), 256 * min(2, KT - 2 * i)
                    a = (TU * n + i) % 2
                    dve.wait_ge(s_hi, hi_part(b, h) + 1)
                    nc.vector.tensor_tensor(ptl[0:m, a, 0:w], work[0:m, at_bank, 0:w], pth[0:m, a, 0:w],
                                            ALU.subtract).then_inc(s_evac, 1)
                elif kind == "D":
                    dve.wait_ge(s_exp, 8 * b + 9)
                    nc.vector.tensor_tensor(total[:, :], rowsum[:, 0, :], rowsum[:, 1, :], ALU.add).then_inc(s_tot, 1)
                    dve.wait_ge(s_tot, 2 * b + 1)
                    nc.vector.reciprocal(inv[:, :], total[:, :]).then_inc(s_tot, 1)
                    dve.wait_ge(s_tot, 2 * b + 2)
                    nc.vector.tensor_tensor(diag[:, :, :], eye2[:, :].unsqueeze(1).to_broadcast([P, 8, NQ]),
                                            inv[:, :].unsqueeze(2).to_broadcast([P, 8, NQ]), ALU.mult)\
                      .then_inc(s_diag, 1)
                elif kind == "N":
                    at = (slice(None), slice(2 * n, 2 * n + 2), slice(None))
                    dve.wait_ge(s_oout, 16 * b + 16)
                    dve.wait_ge(s_out, 4 * b + 2 * n + 3)
                    dve.wait_ge(s_full, unit(b, u) + 1)
                    nc.vector.tensor_tensor(outn[at], outT[at],
                                            work[:, at_bank, 0:P].rearrange("p (g n) -> p g n", g=2),
                                            ALU.mult).then_inc(s_evac, 1)
                    dve.wait_ge(s_evac, unit(b, u) + 1)
                    nc.vector.tensor_tensor(outn[at], outn[at],
                                            bias[:, 2, 2 * n:2 * n + 2].unsqueeze(2).to_broadcast([P, 2, NQ]),
                                            ALU.add).then_inc(s_outr, 1)
                elif kind == "W":
                    dve.wait_ge(s_whi, n + 1)
                    nc.vector.tensor_tensor((wkl, wvl)[n][:, :, :], wkv_raw[:, n, :, :], (wkh, wvh)[n][:, :, :],
                                            ALU.subtract).then_inc(s_wlo, 1)
                elif kind == "T":
                    a = n % 2
                    dve.wait_ge(s_x[a], 16 * (n // 2 + 1))
                    nc.vector.bn_stats(stat[:, a, :], xt[:, a, :]).then_inc(s_ln, 1)
                    dve.wait_ge(s_ln, 3 * n + 1)
                    nc.vector.bn_aggr(mv[:, a, :], stat[:, a, :]).then_inc(s_ln, 1)
                    dve.wait_ge(s_ln, 3 * n + 2)
                    nc.vector.tensor_scalar(rstd[:, a, :], mv[:, a, 1:2], EPS, None, ALU.add).then_inc(s_var, 1)
                    dve.wait_ge(s_std, n + 1)
                    nc.vector.reciprocal(rstd[:, a, :], rstd[:, a, :]).then_inc(s_ln, 1)
                    dve.wait_ge(s_ln, 3 * n + 3)
                    if n >= 2:
                        dve.wait_ge(s_xT, n - 1)
                    nc.vector.tensor_scalar(xn[:, a, :], xt[:, a, :], mv[:, a, 0:1], rstd[:, a, :],
                                            ALU.subtract, ALU.mult).then_inc(s_xn, 1)

            dve.wait_ge(s_const, CONSTS)
            for step in prologue:
                item(0, *step)
            dve.wait_ge(s_sel, 32)
            if batches > 1:
                with dve.Fori(0, batches - 1) as b:
                    for step in cross_numbered(cross_order(), CROSS_PRO):
                        item(b, *step)
            for step in cross_numbered(cross_order(), CROSS_PRO, last=True):
                item(batches - 1, *step)

        @block.tensor
        def _(pe):
            def product3(out, lh, ll, rh, rl, start, stop):
                nc.tensor.matmul(out, lh, rh, start=start, stop=False)
                nc.tensor.matmul(out, lh, rl, start=False, stop=False)
                return nc.tensor.matmul(out, ll, rh, start=False, stop=stop)

            def free_bank(b, u):
                if u >= BANKS:
                    pe.wait_ge(s_evac, unit(b, u) - BANKS + 1)

            def item(b, kind, n, i, ahead, u, h):
                at_bank = u % BANKS
                if kind == "S":
                    j = n // 2
                    if n % 2 == 0:
                        pe.wait_ge(s_qb, b + ahead + 1)
                        pe.wait_ge(s_evac, unit(b, u) - BANKS)
                    pe.wait_ge(s_exp, 8 * (b + ahead) + n + 1)
                    for c in range(NC):
                        at = (slice(None), j % 2, at_keys(c))
                        ins = product3(sps[:, c, 0:CH], qbh[:, j, n % 2, :], qbl[:, j, n % 2, :],
                                       kth[at], ktl[at], True, True)
                    ins.then_inc(s_scores, 1)
                elif kind == "K":
                    free_bank(b, u)
                    pe.wait_ge(s_cx, NC * (b + ahead) + i + 1)
                    for k in range(KC):
                        w = (slice(None), k, slice(P * n, P * (n + 1)))
                        at = (slice(None), k, at_keys(i))
                        ins = product3(work[:, at_bank, 0:CH], wkh[w], wkl[w], cxh[at], cxl[at],
                                       k == 0, k == KC - 1)
                    ins.then_inc(s_full, 1)
                elif kind == "V":
                    m = tile_rows(i)
                    free_bank(b, u)
                    pe.wait_ge(s_cx, NC * (b + ahead) + tile_chunk(i) + 1)
                    for k in range(KC):
                        at = (slice(None), k, slice(P * i, P * i + m))
                        w = (slice(None), k, slice(HW * n, HW * (n + 1)))
                        ins = product3(work[0:m, at_bank, 0:HW], cxh[at], cxl[at], wvh[w], wvl[w],
                                       k == 0, k == KC - 1)
                    ins.then_inc(s_full, 1)
                elif kind == "t":
                    if i == 0:
                        pe.wait_ge(s_exp, 8 * b + 2 * n + 3)
                    free_bank(b, u)
                    for tt in range(min(2, KT - 2 * i)):
                        t = 2 * i + tt
                        m = tile_rows(t)
                        for pp in range(2):
                            at = 256 * tt + P * pp
                            ins = nc.tensor.transpose(work[0:m, at_bank, at:at + P],
                                                      probs[:, (2 * n + pp) % 4, P * t:P * t + m], ident[:, :])
                    ins.then_inc(s_full, 1)
                elif kind == "m":
                    pe.wait_ge(s_evac, unit(b, transposed[n, i]) + 1)
                    if i == 0:
                        pe.wait_ge(s_out, 4 * b + n + 1)
                    for tt in range(min(2, KT - 2 * i)):
                        t = 2 * i + tt
                        m = tile_rows(t)
                        v = (slice(0, m), t, slice(P * (n % 2), P * (n % 2 + 1)))
                        at = (slice(0, m), (TU * n + i) % 2, slice(256 * tt, 256 * (tt + 1)))
                        ins = product3(ops[:, 0:256], vh[v], vl[v], pth[at], ptl[at], t == 0, t == KT - 1)
                    ins.then_inc(s_pv, 1)
                elif kind == "N":
                    pe.wait_ge(s_diag, b + 1)
                    free_bank(b, u)
                    for pp in range(2):
                        ins = nc.tensor.matmul(work[:, at_bank, 0:P], sel[:, pp, :],
                                               diag[:, 4 * n + pp:4 * n + pp + 3:2, :],
                                               start=(pp == 0), stop=(pp == 1))
                    ins.then_inc(s_full, 1)
                elif kind == "W":
                    pe.wait_ge(s_wlo, n + 1)
                elif kind == "T":
                    pe.wait_ge(s_xn, n + 1)
                    if n >= 4:
                        pe.wait_ge(s_xTc, n - 3)
                    for k in range(KC):
                        ins = nc.tensor.transpose(sps[:, n % 4, P * k:P * (k + 1)], xn[:, n % 2, P * k:P * (k + 1)],
                                                  ident[:, :])
                    ins.then_inc(s_xT, 1)
                elif kind == "U":
                    if n == 0:
                        pe.wait_ge(s_wq, 16)
                        pe.wait_ge(s_xTc, tiles)
                    if n >= 4:
                        pe.wait_ge(s_qs, n - 3)
                    for k in range(KC):
                        ins = nc.tensor.matmul(sps[:, n % 4, 0:QN], wq_sb[:, k, P * (n % 4):P * (n % 4 + 1)],
                                               xnT[:, k, QN * (n // 4):QN * (n // 4 + 1)],
                                               start=(k == 0), stop=(k == KC - 1))
                    ins.then_inc(s_q, 1)

            pe.sem_inc(s_pv, 2)
            pe.wait_ge(s_const, CONSTS)
            pe.wait_ge(s_sel, 32)
            for step in prologue:
                if step[0] == "S":
                    pe.wait_ge(s_qs, QU)
                item(0, *step)

            if batches > 1:
                transposed = {(n, i): u for kind, n, i, _, u, _ in cross_numbered(cross_order(), CROSS_PRO) if kind == "t"}
                with pe.Fori(0, batches - 1) as b:
                    for step in cross_numbered(cross_order(), CROSS_PRO):
                        item(b, *step)
            transposed = {(n, i): u for kind, n, i, _, u, _ in cross_numbered(cross_order(), CROSS_PRO, last=True) if kind == "t"}
            for step in cross_numbered(cross_order(), CROSS_PRO, last=True):
                item(batches - 1, *step)


SELF_STEPS = [("TQ", 0), ("O1", 1), ("TL", -1), ("S", 0), ("TX", 1), ("LG", -1), ("SM", 0), ("QK", 1), ("TP", 0),
              ("V0", 1), ("O2", 0), ("V1", 1)]
SELF_UNITS = {"TQ": 0, "TL": 1, "O1": 1, "LG": 1, "S": 0, "SM": 0, "TX": 1, "QK": 4, "TP": 4, "V0": 1, "V1": 1, "O2": 1}
RING = 3
SELF_PER = sum(SELF_UNITS.values())
assert SELF_PER % RING == 0


def numbered(kinds, at):
    first = {}
    for kind in kinds:
        first[kind] = at
        at += SELF_UNITS[kind]
    return first, at


SELF_PROLOGUE, _n = numbered(["O1", "TX", "QK", "V0", "V1"], 0)
SELF_START = _n - SELF_UNITS["TL"] - SELF_UNITS["LG"]
SELF_BODY, _n = numbered([kind for kind, _ in SELF_STEPS], SELF_START)
SELF_LAST, _n = numbered([kind for kind, shift in SELF_STEPS if shift < 1], SELF_START)
SELF_TAIL, _n = numbered(["TL", "LG"], _n)
SELF_PIECES = 8


def self_weights(nc, es, wqkv, wo1, wo2):
    KI = SI // P
    base = -(-nc.sbuf_base // 32) * 32
    es.enter_context(nc.sbuf_tensor("room", [P, ROOM], F32))

    def place(name, word, shape, dt):
        assert word + int(np.prod(shape)) <= ROOM
        return nc.alloc_sbuf_tensor_at(name, [P] + shape, dt, offset=base + 4 * word)

    piece = KC * D
    sources = [wqkv[:, :, D * n:D * (n + 1)] for n in range(6)] + [wo2[:, KC * n:KC * (n + 1), :] for n in range(KI // KC)]
    loads, lo = [], []
    for n, src in enumerate([wo1] + sources):
        raw = place(f"sa_raw{n}", piece * n, [KC, D], F32)
        loads.append((raw[:, :, :], src, es.enter_context(nc.semaphore(f"sa_weights{n}"))))
        if n:
            lo.append(place(f"sa_lo{n}", piece * n, [KC, D], F32R))
    return place, loads, lo


def self_attention(nc, x, o_scr, prefetch, lo, bo1, bo2, router, ident_in, x2_scr, xn_scr, lg_scr, tiles):
    with ExitStack() as es:
        def sb(name, shape, dt=F32):
            return es.enter_context(nc.sbuf_tensor(name, shape, dt))

        def sem(name):
            return es.enter_context(nc.semaphore(name))

        KI = SI // P
        wqh = sb("sa_wqh", [P, KC, 3 * SI], F32R)
        woh = sb("sa_woh", [P, KI, D], F32R)
        wo1_sb = prefetch[0][0]
        raw = [dst for dst, _, _ in prefetch[1:]]
        s_weights = [sem for _, _, sem in prefetch]
        router_sb = sb("sa_router", [P, KC, E])
        kbd = sb("sa_kbd", [P, KI, 2 * P])
        qT = sb("sa_qT", [P, KI, P])
        pT = sb("sa_pT", [P, 2, 4, P])
        pc = pT[:, :, :, :].rearrange("p a h n -> p (a h n)").rearrange("p (h n) -> p h n", h=H)
        ident = sb("sa_ident", [P, P])
        bos = sb("sa_bos", [P, 2, D])
        oin = sb("sa_oin", [P, KC, P])
        xin = sb("sa_xin", [P, D])
        xb = sb("sa_xb", [P, D])
        x1 = sb("sa_x1", [P, D])
        x1b = sb("sa_x1b", [P, D])
        xn = sb("sa_xn", [P, D])
        xTh = sb("sa_xTh", [P, KC, P], F32R)
        xTl = sb("sa_xTl", [P, KC, P], F32R)
        rows = sb("sa_rows", [P, 3, SI])
        prob = sb("sa_prob", [P, H, P])
        aTh = sb("sa_aTh", [P, KI, P], F32R)
        aTl = sb("sa_aTl", [P, KI, P], F32R)
        x2 = sb("sa_x2", [P, D])
        xn3 = sb("sa_xn3", [P, D])
        xn3T = sb("sa_xn3T", [P, KC, P])
        lg = sb("sa_lg", [P, E])
        stat = sb("sa_stat", [P, 2, 6])
        mv = sb("sa_mv", [P, 2, 2])
        rstd = sb("sa_rstd", [P, 2, 1])
        idle = sb("sa_idle", [P, 2])
        mx = sb("sa_mx", [P, H])
        tot = sb("sa_tot", [P, 2, H])

        big = es.enter_context(nc.psum_tensor("sa_big", [P, 4, 512], F32))
        ring = es.enter_context(nc.psum_tensor("sa_ring", [P, RING, 512], F32))

        s_const = sem("sa_const")
        s_whi = sem("sa_whi")
        s_wlo = sem("sa_wlo")
        s_zero = sem("sa_zero")
        s_oin = sem("sa_oin_ready")
        s_xin = sem("sa_xin_ready")
        s_xb = sem("sa_xb_ready")
        s_x1b = sem("sa_x1b_ready")
        s_ln = [sem("sa_ln1"), sem("sa_ln3")]
        s_var = [sem("sa_var1"), sem("sa_var3")]
        s_std = [sem("sa_std1"), sem("sa_std3")]
        s_xn = sem("sa_xn_ready")
        s_xn3 = sem("sa_xn3_ready")
        s_xTh = sem("sa_xTh_ready")
        s_full = sem("sa_full")
        s_free = [sem(f"sa_free{i}") for i in range(RING)]
        s_tq = sem("sa_tq")
        s_qT = sem("sa_qT_ready")
        s_kbd = sem("sa_kbd_ready")
        s_s = sem("sa_scores")
        s_sm = sem("sa_softmax")
        s_sub = sem("sa_sub")
        s_exp = sem("sa_exp")
        s_prob = sem("sa_prob_ready")
        s_pv = sem("sa_pv")
        s_aTh = sem("sa_aTh_ready")
        s_aTl = sem("sa_aTl_ready")
        s_x2o = sem("sa_x2_out")
        s_xno = sem("sa_xn_out")
        s_lgo = sem("sa_lg_out")

        CONSTS = 4 * 16
        PROLOGUE, TAIL = -1, tiles

        def steps(t, last):
            for kind, shift in SELF_STEPS:
                if not ((shift < 0 and isinstance(t, int) and t == 0) or (shift > 0 and last)):
                    yield kind, shift

        def first(kind, tb):
            if isinstance(tb, int) and tb == PROLOGUE:
                return SELF_PROLOGUE[kind], 0
            if isinstance(tb, int) and tb >= tiles - 1:
                return (SELF_TAIL if tb == TAIL else SELF_LAST)[kind], tiles - 1
            if isinstance(tb, int) and tb == 0 and kind in ("O1", "TX"):
                return SELF_BODY[kind] + SELF_UNITS["LG"] + (SELF_UNITS["TL"] if kind == "O1" else 0), 0
            return SELF_BODY[kind], tb

        def number(kind, tb, i=0):
            c, n = first(kind, tb)
            return n * SELF_PER + c + i

        def bank(kind, tb, i=0):
            return (first(kind, tb)[0] + i) % RING

        def uses(kind, tb, i=0):
            c, n = first(kind, tb)
            return n * (SELF_PER // RING) + (c + i) // RING

        def filled(eng, kind, tb, i=0):
            eng.wait_ge(s_full, number(kind, tb, i) + 1)

        def emptied(eng, kind, tb, i=0):
            eng.wait_ge(s_free[bank(kind, tb, i)], uses(kind, tb, i) + 1)

        def run(eng, body):
            body(0, tiles == 1)
            if tiles > 2:
                with eng.Fori(1, tiles - 1) as t:
                    body(t, False)
            if tiles > 1:
                body(tiles - 1, True)

        def piece(wq, wo, n):
            return wq[:, :, D * n:D * (n + 1)] if n < 6 else wo[:, KC * (n - 6):KC * (n - 5), :]

        def half(b):
            return slice(NQ * b, NQ * b + NQ)

        block = es.enter_context(nc.Block())

        @block.sync
        def _(sp):
            def inputs(t):
                sp.dma_start(oin[:, :, 0:NQ], o_scr[2 * t, :, :, :]).then_inc(s_oin, 16)
                sp.dma_start(oin[:, :, NQ:P], o_scr[2 * t + 1, :, :, :]).then_inc(s_oin, 16)
                sp.dma_start(xin[:, :], x[t, :, :]).then_inc(s_xin, 16)

            sp.sem_inc(s_lgo, 16)
            inputs(0)
            sp.dma_start(ident[:, :], ident_in).then_inc(s_const, 16)
            sp.dma_start(bos[:, 0, :], bo1.to_broadcast([P, D])).then_inc(s_const, 16)
            sp.dma_start(bos[:, 1, :], bo2.to_broadcast([P, D])).then_inc(s_const, 16)
            sp.dma_start(router_sb[:, :, :], router).then_inc(s_const, 16)

            def logits_out(t, tb):
                emptied(sp, "LG", tb)
                sp.dma_start(lg_scr[t, :, :], lg[:, :]).then_inc(s_lgo, 16)

            def body(t, last):
                if not last:
                    sp.wait_ge(s_var[0], t + 1)
                    inputs(t + 1)
                if not (isinstance(t, int) and t == 0):
                    logits_out(t - 1, t)

            run(sp, body)
            logits_out(tiles - 1, TAIL)
            sp.wait_ge(s_lgo, 16 * tiles + 16)

        @block.scalar
        def _(act):
            def root(a, t):
                act.wait_ge(s_var[a], t + 1)
                nc.scalar.activation(rstd[:, a, :], rstd[:, a, :], ACT.Sqrt).then_inc(s_std[a], 1)

            def step(kind, t, tb):
                if kind == "O1":
                    root(0, t)
                elif kind == "TX":
                    filled(act, kind, tb)
                    nc.scalar.activation(xTh[:, :, :], ring[:, bank(kind, tb), :].rearrange("p (k n) -> p k n", k=KC),
                                         ACT.Copy).then_inc(s_xTh, 1)
                elif kind in ("QK", "V0", "V1"):
                    n0 = {"QK": 0, "V0": 4, "V1": 5}[kind]
                    for i in range(SELF_UNITS[kind]):
                        n = n0 + i
                        filled(act, kind, tb, i)
                        nc.scalar.activation(rows[:, n // 2, D * (n % 2):D * (n % 2 + 1)],
                                             ring[:, bank(kind, tb, i), :], ACT.Copy).then_inc(s_free[bank(kind, tb, i)], 1)
                elif kind == "TQ":
                    for i in range(2):
                        act.wait_ge(s_tq, 4 * t + i + 1)
                        nc.scalar.activation(qT[:, 4 * i:4 * i + 4, :],
                                             big[:, i, :].rearrange("p (r n) -> p r n", r=4), ACT.Copy).then_inc(s_qT, 1)
                elif kind == "SM":
                    for b in range(2):
                        act.wait_ge(s_sub, 2 * t + b + 1)
                        nc.scalar.activation(pc[half(b), :, :], pc[half(b), :, :], ACT.Exp, scale=SSCALE)\
                          .then_inc(s_exp, 1)
                elif kind == "LG":
                    filled(act, kind, tb)
                    act.wait_ge(s_lgo, 16 * t + 16)
                    nc.scalar.activation(lg[:, :], ring[:, bank(kind, tb), 0:E], ACT.Copy).then_inc(s_free[bank(kind, tb)], 1)
                elif kind == "TP":
                    for i in range(4):
                        filled(act, kind, tb, i)
                        if i >= 2:
                            act.wait_ge(s_pv, 4 * t + i - 1)
                        nc.scalar.activation(pT[:, i % 2, :, :], ring[:, bank(kind, tb, i), :]
                                             .rearrange("p (h n) -> p h n", h=4), ACT.Copy).then_inc(s_free[bank(kind, tb, i)], 1)
                        if i >= 1:
                            heads_hi(t, i - 1)
                    heads_hi(t, 3)
                elif kind == "O2":
                    root(1, t)
                    emptied(act, kind, tb)
                    act.dma_start(x2_scr[t, :, :], x2[:, :]).then_inc(s_x2o, 16)
                elif kind == "TL":
                    filled(act, kind, tb)
                    act.wait_ge(s_xn3, t + 1)
                    act.dma_start(xn_scr[t, :, :], xn3[:, :]).then_inc(s_xno, 16)
                    nc.scalar.activation(xn3T[:, :, :], ring[:, bank(kind, tb), :].rearrange("p (k n) -> p k n", k=KC),
                                         ACT.Copy).then_inc(s_free[bank(kind, tb)], 1)

            def heads_hi(t, i):
                act.wait_ge(s_pv, 4 * t + i + 1)
                for hh in range(2):
                    src = big[half(hh), i, :].rearrange("p (r n) -> p r n", r=2)
                    ins = nc.scalar.activation(aTh[half(hh), 2 * i:2 * i + 2, :], src[:, :, P * hh:P * (hh + 1)], ACT.Copy)
                ins.then_inc(s_aTh, 1)

            for n in range(SELF_PIECES):
                act.wait_ge(s_weights[n + 1], 16)
                nc.scalar.activation(piece(wqh, woh, n), raw[n], ACT.Copy).then_inc(s_whi, 1)
                if n == 0:
                    step("O1", 0, PROLOGUE)
                if n == 1:
                    step("TX", 0, PROLOGUE)
                if n == 3:
                    step("QK", 0, PROLOGUE)
            step("V0", 0, PROLOGUE)
            step("V1", 0, PROLOGUE)

            def body(t, last):
                for kind, shift in steps(t, last):
                    step(kind, t + shift, t)

            run(act, body)
            step("TL", tiles - 1, TAIL)
            step("LG", tiles - 1, TAIL)
            for s in (s_x2o, s_xno):
                act.wait_ge(s, 16 * tiles)

        @block.vector
        def _(dve):
            def layer_norm(a, t, src, dst, s_dst, out_wait=None):
                nc.vector.bn_stats(stat[:, a, :], src).then_inc(s_ln[a], 1)
                dve.wait_ge(s_ln[a], 3 * t + 1)
                nc.vector.memset(idle[:, a:a + 1], 0.0)
                nc.vector.bn_aggr(mv[:, a, :], stat[:, a, :]).then_inc(s_ln[a], 1)
                dve.wait_ge(s_ln[a], 3 * t + 2)
                nc.vector.tensor_scalar(rstd[:, a, :], mv[:, a, 1:2], EPS, None, ALU.add).then_inc(s_var[a], 1)
                dve.wait_ge(s_std[a], t + 1)
                nc.vector.reciprocal(rstd[:, a, :], rstd[:, a, :]).then_inc(s_ln[a], 1)
                dve.wait_ge(s_ln[a], 3 * t + 3)
                if out_wait is not None:
                    dve.wait_ge(*out_wait)
                nc.vector.tensor_scalar(dst, src, mv[:, a, 0:1], rstd[:, a, :], ALU.subtract, ALU.mult).then_inc(s_dst, 1)

            def step(kind, t, tb):
                if kind == "O1":
                    dve.wait_ge(s_xin, 16 * t + 16)
                    nc.vector.tensor_tensor(xb[:, :], xin[:, :], bos[:, 0, :], ALU.add).then_inc(s_xb, 1)
                    dve.wait_ge(s_xb, t + 1)
                    if not (isinstance(t, int) and t == 0):
                        dve.wait_ge(s_x1b, t)
                    filled(dve, kind, tb)
                    nc.vector.tensor_tensor(x1[:, :], ring[:, bank(kind, tb), :], xb[:, :], ALU.add).then_inc(s_free[bank(kind, tb)], 1)
                    emptied(dve, kind, tb)
                    layer_norm(0, t, x1[:, :], xn[:, :], s_xn)
                elif kind == "TX":
                    dve.wait_ge(s_xTh, t + 1)
                    nc.vector.tensor_tensor(xTl[:, :, :], ring[:, bank(kind, tb), :].rearrange("p (k n) -> p k n", k=KC),
                                            xTh[:, :, :], ALU.subtract).then_inc(s_free[bank(kind, tb)], 1)
                elif kind == "TQ":
                    for i in range(2):
                        dve.wait_ge(s_tq, 4 * t + i + 3)
                        for hh in range(2):
                            ins = nc.vector.tensor_copy(kbd[half(hh), 4 * i:4 * i + 4, P * hh:P * (hh + 1)],
                                                        big[half(hh), 2 + i, :].rearrange("p (r n) -> p r n", r=4))
                        ins.then_inc(s_kbd, 1)
                    nc.vector.tensor_tensor(x1b[:, :], x1[:, :], bos[:, 1, :], ALU.add).then_inc(s_x1b, 1)
                elif kind == "S":
                    dve.wait_ge(s_s, t + 1)
                    nc.vector.tensor_reduce(mx[half(0), :], scores(0), AX.X, ALU.max).then_inc(s_sm, 1)
                elif kind == "SM":
                    for b in range(2):
                        if b:
                            nc.vector.tensor_reduce(mx[half(1), :], scores(1), AX.X, ALU.max).then_inc(s_sm, 1)
                        dve.wait_ge(s_sm, 4 * t + b + 1)
                        nc.vector.tensor_tensor(pc[half(b), :, :], scores(b),
                                                mx[half(b), :].unsqueeze(2).to_broadcast([NQ, H, NQ]),
                                                ALU.subtract).then_inc(s_sub, 1)
                    dve.wait_ge(s_exp, 2 * t + 2)
                    nc.vector.tensor_reduce(tot[:, 0, :], pc[:, :, :], AX.X, ALU.add).then_inc(s_sm, 1)
                    dve.wait_ge(s_sm, 4 * t + 3)
                    nc.vector.reciprocal(tot[:, 1, :], tot[:, 0, :]).then_inc(s_sm, 1)
                    dve.wait_ge(s_sm, 4 * t + 4)
                    for b in range(2):
                        nc.vector.tensor_tensor(prob[half(b), :, half(b)], pc[half(b), :, :],
                                                tot[half(b), 1, :].unsqueeze(2).to_broadcast([NQ, H, NQ]),
                                                ALU.mult).then_inc(s_prob, 1)
                elif kind == "TP":
                    for i in range(4):
                        dve.wait_ge(s_aTh, 4 * t + i + 1)
                        for hh in range(2):
                            src = big[half(hh), i, :].rearrange("p (r n) -> p r n", r=2)
                            at = (half(hh), slice(2 * i, 2 * i + 2), slice(None))
                            ins = nc.vector.tensor_tensor(aTl[at], src[:, :, P * hh:P * (hh + 1)], aTh[at], ALU.subtract)
                        ins.then_inc(s_aTl, 1)
                elif kind == "O2":
                    filled(dve, kind, tb)
                    if not (isinstance(t, int) and t == 0):
                        dve.wait_ge(s_x2o, 16 * t)
                    dve.wait_ge(s_x1b, t + 1)
                    nc.vector.tensor_tensor(x2[:, :], ring[:, bank(kind, tb), :], x1b[:, :], ALU.add).then_inc(s_free[bank(kind, tb)], 1)
                    emptied(dve, kind, tb)
                    layer_norm(1, t, x2[:, :], xn3[:, :], s_xn3,
                               None if isinstance(t, int) and t == 0 else (s_xno, 16 * t))

            def scores(b):
                return big[half(b), :, :].rearrange("p a (h n) -> p (a h) n", h=4)[:, :, half(b)]

            nc.vector.memset(prob[:, :, :], 0.0).then_inc(s_zero, 1)
            dve.wait_ge(s_const, CONSTS)
            for n in range(SELF_PIECES):
                dve.wait_ge(s_whi, n + 1)
                nc.vector.tensor_tensor(lo[n][:, :, :], raw[n], piece(wqh, woh, n), ALU.subtract).then_inc(s_wlo, 1)
                if n == 0:
                    step("O1", 0, PROLOGUE)
                if n == 1:
                    step("TX", 0, PROLOGUE)
            nc.vector.memset(kbd[:, :, :], 0.0).then_inc(s_zero, 1)
            dve.wait_ge(s_zero, 2)

            def body(t, last):
                for kind, shift in steps(t, last):
                    step(kind, t + shift, t)

            run(dve, body)

        @block.tensor
        def _(pe):
            def product3(out, lh, ll, rh, rl, start, stop):
                nc.tensor.matmul(out, lh, rh, start=start, stop=False)
                nc.tensor.matmul(out, lh, rl, start=False, stop=False)
                return nc.tensor.matmul(out, ll, rh, start=False, stop=stop)

            def free_bank(kind, tb, i=0):
                n = uses(kind, tb, i)
                if not (isinstance(n, int) and n == 0):
                    pe.wait_ge(s_free[bank(kind, tb, i)], n)

            def turn4(dst, src):
                for k in range(KC):
                    ins = nc.tensor.transpose(dst[:, P * k:P * (k + 1)], src[:, P * k:P * (k + 1)], ident[:, :])
                return ins

            def step(kind, t, tb):
                if SELF_UNITS[kind]:
                    dst = ring[:, bank(kind, tb), :]
                if kind == "O1":
                    free_bank(kind, tb)
                    pe.wait_ge(s_oin, 32 * t + 32)
                    for k in range(KC):
                        ins = nc.tensor.matmul(dst, oin[:, k, :], wo1_sb[:, k, :], start=(k == 0), stop=(k == KC - 1))
                    ins.then_inc(s_full, 1)
                elif kind == "TX":
                    free_bank(kind, tb)
                    pe.wait_ge(s_xn, t + 1)
                    turn4(dst, xn).then_inc(s_full, 1)
                elif kind in ("QK", "V0", "V1"):
                    emptied(pe, "TX", tb)
                    n0 = {"QK": 0, "V0": 4, "V1": 5}[kind]
                    for i in range(SELF_UNITS[kind]):
                        free_bank(kind, tb, i)
                        n = n0 + i
                        if isinstance(t, int) and t == 0:
                            pe.wait_ge(s_wlo, n + 1)
                        for k in range(KC):
                            w = (slice(None), k, slice(D * n, D * (n + 1)))
                            ins = product3(ring[:, bank(kind, tb, i), :], xTh[:, k, :], xTl[:, k, :], wqh[w], lo[n][:, k, :],
                                           k == 0, k == KC - 1)
                        ins.then_inc(s_full, 1)
                elif kind == "TQ":
                    for i in range(4):
                        emptied(pe, "QK", tb - 1, i)
                        turn4(big[:, i, :], rows[:, i // 2, D * (i % 2):D * (i % 2 + 1)]).then_inc(s_tq, 1)
                elif kind == "S":
                    pe.wait_ge(s_qT, 2 * t + 2)
                    pe.wait_ge(s_kbd, 2 * t + 2)
                    for i in range(4):
                        for r in range(2):
                            ins = nc.tensor.matmul(big[:, i, 256 * r:256 * (r + 1)], qT[:, 2 * i + r, :],
                                                   kbd[:, 2 * i + r, :], start=True, stop=True)
                    ins.then_inc(s_s, 1)
                elif kind == "TP":
                    def turn(i):
                        free_bank(kind, tb, i)
                        turn4(ring[:, bank(kind, tb, i), :],
                              prob[:, 4 * i:4 * i + 4, :].rearrange("p h n -> p (h n)")).then_inc(s_full, 1)

                    def meet(i):
                        emptied(pe, kind, tb, i)
                        for r in range(2):
                            pr = 2 * i + r
                            ins = nc.tensor.matmul(big[:, i, 256 * r:256 * (r + 1)], rows[:, 2, P * pr:P * (pr + 1)],
                                                   pT[:, i % 2, 2 * r:2 * r + 2, :], start=True, stop=True)
                        ins.then_inc(s_pv, 1)

                    pe.wait_ge(s_prob, 2 * t + 2)
                    emptied(pe, "V1", tb - 1)
                    turn(0)
                    for i in range(1, 4):
                        turn(i)
                        meet(i - 1)
                    meet(3)
                elif kind == "O2":
                    if isinstance(t, int) and t == 0:
                        pe.wait_ge(s_wlo, 8)
                    free_bank(kind, tb)
                    pe.wait_ge(s_aTl, 4 * t + 4)
                    for k in range(KI):
                        lo2 = lo[6 + k // KC][:, k % KC, :]
                        ins = product3(dst, aTh[:, k, :], aTl[:, k, :], woh[:, k, :], lo2, k == 0, k == KI - 1)
                    ins.then_inc(s_full, 1)
                elif kind == "TL":
                    free_bank(kind, tb)
                    pe.wait_ge(s_xn3, t + 1)
                    turn4(dst, xn3).then_inc(s_full, 1)
                elif kind == "LG":
                    free_bank(kind, tb)
                    emptied(pe, "TL", tb)
                    for k in range(KC):
                        ins = nc.tensor.matmul(dst[:, 0:E], xn3T[:, k, :], router_sb[:, k, :], start=(k == 0),
                                               stop=(k == KC - 1))
                    ins.then_inc(s_full, 1)

            pe.wait_ge(s_const, CONSTS)
            pe.wait_ge(s_weights[0], 16)
            for kind in SELF_PROLOGUE:
                step(kind, 0, PROLOGUE)

            def body(t, last):
                for kind, shift in steps(t, last):
                    step(kind, t + shift, t)

            run(pe, body)
            step("TL", tiles - 1, TAIL)
            step("LG", tiles - 1, TAIL)


G = 8
SLOTS = E * CAP


def experts(nc, x2_scr, xn_scr, lg_scr, w01, wout, tri_in, rowc_in, ident_in, eo_scr, out):
    with ExitStack() as es:
        def sb(name, shape, dt=F32):
            return es.enter_context(nc.sbuf_tensor(name, shape, dt))

        xeh = sb("mo_xeh", [P, KC, E, ROWS], F32R)
        xel = sb("mo_xel", [P, KC, E, ROWS], F32R)
        combT = sb("mo_combT", [P, 2, G, P])
        route(nc, xn_scr, lg_scr, tri_in, rowc_in, ident_in, xeh, xel, combT)
        run_experts(nc, x2_scr, w01, wout, eo_scr, xeh, xel, combT, out)


def route(nc, xn_scr, lg_scr, tri_in, rowc_in, ident_in, xeh, xel, combT):
    with ExitStack() as es:
        def sb(name, shape, dt=F32):
            return es.enter_context(nc.sbuf_tensor(name, shape, dt))

        def sem(name):
            return es.enter_context(nc.semaphore(name))

        GE = [P, G, E]
        lg = sb("ro_lg", GE)
        xn = sb("ro_xn", [P, G, D])
        xnh = sb("ro_xnh", [P, G, D], F32R)
        xnl = sb("ro_xnl", [P, G, D], F32R)
        tri = sb("ro_tri", [P, 2, P])
        rowc = sb("ro_rowc", [P, E + CAP])
        ident = sb("ro_ident", [P, P])
        top = sb("ro_top", [P, 2, G])
        ex = sb("ro_ex", GE)
        raw = sb("ro_raw", GE)
        rest = sb("ro_rest", GE)
        eq = sb("ro_eq", GE)
        cand = sb("ro_cand", GE)
        pick = sb("ro_pick", [P, G])
        mask = sb("ro_mask", [P, 2, G, E])
        kept = sb("ro_kept", [P, 2, G, E])
        pos = sb("ro_pos", [P, 2, G])
        slot1 = sb("ro_slot1", [P, 2, G, CAP])
        small = sb("ro_small", [P, 2, G])
        parts = sb("ro_parts", [P, 2, G, SLOTS])
        disp = sb("ro_disp", [P, G, SLOTS], F32R)
        pp = es.enter_context(nc.psum_tensor("ro_pp", [P, 2, 512], F32))
        pt = es.enter_context(nc.psum_tensor("ro_pt", [P, 2, 512], F32))
        pd = es.enter_context(nc.psum_tensor("ro_pd", [P, 2, 2, 512], F32))

        s_in = sem("ro_in")
        s_xn = sem("ro_xn_in")
        s_v = sem("ro_v")
        s_d = sem("ro_d")
        s_ex = sem("ro_ex_ready")
        s_m = sem("ro_m")
        s_p = sem("ro_p")
        s_comb = sem("ro_comb")
        s_disp = sem("ro_disp_ready")
        s_xnh = sem("ro_xnh_ready")
        s_xnl = sem("ro_xnl_ready")
        s_t = sem("ro_t")
        s_tc = sem("ro_tc")
        s_x = sem("ro_x")
        s_xh = sem("ro_xh")
        s_xl = sem("ro_xl")
        block = es.enter_context(nc.Block())

        def over(a, n):
            return a.unsqueeze(2).to_broadcast([P, G, n])

        @block.sync
        def _(sp):
            sp.dma_start(lg[:, :, :], lg_scr.rearrange("g p e -> p g e")).then_inc(s_in, 16)
            sp.dma_start(rowc[:, :], rowc_in).then_inc(s_in, 16)
            sp.dma_start(tri[:, :, :], tri_in).then_inc(s_in, 16)
            sp.dma_start(ident[:, :], ident_in).then_inc(s_in, 16)
            sp.dma_start(xn[:, :, :], xn_scr.rearrange("g p m -> p g m")).then_inc(s_xn, 16)

        @block.scalar
        def _(act):
            act.wait_ge(s_d, 1)
            nc.scalar.activation(ex[:, :, :], ex[:, :, :], ACT.Exp).then_inc(s_ex, 1)
            act.wait_ge(s_xn, 16)
            for g in range(G):
                nc.scalar.activation(xnh[:, g, :], xn[:, g, :], ACT.Copy).then_inc(s_xnh, 1)
            for i in range(4):
                act.wait_ge(s_t, i + 1)
                nc.scalar.activation(combT[:, :, 2 * i:2 * i + 2, :].rearrange("p h g n -> p g h n"),
                                     pt[:, i % 2, :].rearrange("p (g h n) -> p g h n", g=2, h=2), ACT.Copy)\
                  .then_inc(s_tc, 1)
            for n in range(2 * G):
                g, kk = n // 2, n % 2
                act.wait_ge(s_x, n + 1)
                for k in range(2):
                    ins = nc.scalar.activation(xeh[:, 2 * kk + k, :, CAP * g:CAP * (g + 1)],
                                               pd[:, n % 2, 0, 256 * k:256 * (k + 1)].rearrange("p (e c) -> p e c", e=E),
                                               ACT.Copy)
                ins.then_inc(s_xh, 1)

        @block.vector
        def _(dve):
            steps = [0]

            def after():
                dve.wait_ge(s_v, steps[0])

            def do(ins):
                steps[0] += 1
                ins.then_inc(s_v, 1)

            v = nc.vector
            em8 = rowc[:, 0:E].unsqueeze(1).to_broadcast(GE)
            dve.wait_ge(s_in, 64)
            do(v.tensor_reduce(pick[:, :], lg[:, :, :], AX.X, ALU.max))
            after()
            v.tensor_tensor(ex[:, :, :], lg[:, :, :], over(pick[:, :], E), ALU.subtract).then_inc(s_d, 1)
            dve.wait_ge(s_ex, 1)
            do(v.tensor_reduce(small[:, 0, :], ex[:, :, :], AX.X, ALU.add))
            after()
            do(v.reciprocal(small[:, 1, :], small[:, 0, :]))
            after()
            do(v.tensor_tensor(raw[:, :, :], ex[:, :, :], over(small[:, 1, :], E), ALU.mult))
            after()
            for i, src in enumerate((raw, rest)):
                if i:
                    do(v.tensor_tensor(cand[:, :, :], raw[:, :, :], mask[:, 0, :, :], ALU.mult))
                    after()
                    do(v.tensor_tensor(rest[:, :, :], raw[:, :, :], cand[:, :, :], ALU.subtract))
                    after()
                do(v.tensor_reduce(top[:, i, :], src[:, :, :], AX.X, ALU.max))
                after()
                do(v.tensor_tensor(eq[:, :, :], src[:, :, :], over(top[:, i, :], E), ALU.is_equal))
                after()
                do(v.tensor_tensor(cand[:, :, :], eq[:, :, :], em8, ALU.mult))
                after()
                do(v.tensor_reduce(pick[:, :], cand[:, :, :], AX.X, ALU.min))
                after()
                v.tensor_tensor(mask[:, i, :, :], over(pick[:, :], E), em8, ALU.is_equal).then_inc(s_m, 1)
                dve.wait_ge(s_m, i + 1)
            for i in range(2):
                dve.wait_ge(s_p, i + 1)
                p = pp[:, i, 0:G * E].rearrange("p (g e) -> p g e", g=G)
                v.scalar_tensor_tensor(kept[:, i, :, :].rearrange("p g e -> p (g e)"), pp[:, i, 0:G * E], float(CAP),
                                       mask[:, i, :, :].rearrange("p g e -> p (g e)"), ALU.is_lt, ALU.mult)\
                 .then_inc(s_m, 1)
                dve.wait_ge(s_m, i + 3)
                do(v.tensor_tensor(cand[:, :, :], p, kept[:, i, :, :], ALU.mult))
                after()
                do(v.tensor_reduce(pos[:, i, :], cand[:, :, :], AX.X, ALU.add))
                after()
                do(v.tensor_tensor(slot1[:, i, :, :], rowc[:, E:E + CAP].unsqueeze(1).to_broadcast([P, G, CAP]),
                                   over(pos[:, i, :], CAP), ALU.is_equal))
                do(v.tensor_tensor(eq[:, :, :], kept[:, i, :, :], over(top[:, i, :], E), ALU.mult))
                after()
                for g in range(G):
                    ins = v.tensor_tensor(parts[:, i, g, :].rearrange("p (e c) -> p e c", e=E),
                                          eq[:, g, :].unsqueeze(2).to_broadcast([P, E, CAP]),
                                          slot1[:, i, g, :].unsqueeze(1).to_broadcast([P, E, CAP]), ALU.mult)
                do(ins)
                after()
            do(v.tensor_tensor(parts[:, 0, :, :], parts[:, 0, :, :], parts[:, 1, :, :], ALU.add))
            after()
            v.tensor_scalar(disp[:, :, :], parts[:, 0, :, :], 0.0, None, ALU.not_equal).then_inc(s_disp, 1)
            for g in range(G):
                dve.wait_ge(s_xnh, g + 1)
                v.tensor_tensor(xnl[:, g, :], xn[:, g, :], xnh[:, g, :], ALU.subtract).then_inc(s_xnl, 1)
            for n in range(2 * G):
                g, kk = n // 2, n % 2
                dve.wait_ge(s_x, n + 1)
                for k in range(2):
                    ins = v.tensor_copy(xel[:, 2 * kk + k, :, CAP * g:CAP * (g + 1)],
                                        pd[:, n % 2, 1, 256 * k:256 * (k + 1)].rearrange("p (e c) -> p e c", e=E))
                ins.then_inc(s_xl, 1)

        @block.tensor
        def _(pe):
            pe.wait_ge(s_in, 64)
            pe.wait_ge(s_m, 1)
            nc.tensor.matmul(pp[:, 0, 0:G * E], tri[:, 0, :], mask[:, 0, :, :].rearrange("p g e -> p (g e)"),
                             start=True, stop=True).then_inc(s_p, 1)
            pe.wait_ge(s_m, 3)
            nc.tensor.matmul(pp[:, 1, 0:G * E], tri[:, 0, :], mask[:, 1, :, :].rearrange("p g e -> p (g e)"),
                             start=True, stop=False)
            nc.tensor.matmul(pp[:, 1, 0:G * E], tri[:, 1, :], kept[:, 0, :, :].rearrange("p g e -> p (g e)"),
                             start=False, stop=True).then_inc(s_p, 1)
            pe.wait_ge(s_disp, 1)
            for i in range(4):
                if i >= 2:
                    pe.wait_ge(s_tc, i - 1)
                for j in range(4):
                    g, h = 2 * i + j // 2, j % 2
                    ins = nc.tensor.transpose(pt[:, i % 2, P * j:P * (j + 1)], parts[:, 0, g, P * h:P * (h + 1)],
                                              ident[:, :])
                ins.then_inc(s_t, 1)
            for n in range(2 * G):
                g, kk = n // 2, n % 2
                pe.wait_ge(s_xnl, g + 1)
                if n >= 2:
                    pe.wait_ge(s_xh, n - 1)
                    pe.wait_ge(s_xl, n - 1)
                for part, src in enumerate((xnh, xnl)):
                    for k in range(2):
                        m = P * (2 * kk + k)
                        ins = nc.tensor.matmul(pd[:, n % 2, part, 256 * k:256 * (k + 1)], src[:, g, m:m + P],
                                               disp[:, g, :], start=True, stop=True)
                ins.then_inc(s_x, 1)


def run_experts(nc, x2_scr, w01, wout, eo_scr, xeh, xel, combT, out):
    with ExitStack() as es:
        def sb(name, shape, dt=F32):
            return es.enter_context(nc.sbuf_tensor(name, shape, dt))

        def sem(name):
            return es.enter_context(nc.semaphore(name))

        raw01 = sb("ex_raw01", [P, 2, 2 * KC * P])
        rawo = sb("ex_rawo", [P, 2, D])
        w01h = sb("ex_w01h", [P, 2, 2, KC, P], F32R)
        w01l = sb("ex_w01l", [P, 2, 2, KC, P], F32R)
        woh = sb("ex_woh", [P, 2, D], F32R)
        wol = sb("ex_wol", [P, 2, D], F32R)
        gelu = sb("ex_gelu", [P, 2, ROWS])
        hid = sb("ex_hid", [P, 2, ROWS])
        hh = sb("ex_hh", [P, 2, ROWS], F32R)
        hl = sb("ex_hl", [P, 2, ROWS], F32R)
        eo = sb("ex_eo", [P, 2, D])
        eog = sb("ex_eog", [P, 2, G, D])
        x2 = sb("ex_x2", [P, G, D])
        up = es.enter_context(nc.psum_tensor("ex_up", [P, 2, 512], F32))
        acc = es.enter_context(nc.psum_tensor("ex_acc", [P, 2, 512], F32))
        comb = es.enter_context(nc.psum_tensor("ex_comb", [P, 4, 512], F32))

        s_r01 = [sem("ex_r01a"), sem("ex_r01b")]
        s_ro = [sem("ex_roa"), sem("ex_rob")]
        s_h01 = sem("ex_h01")
        s_l01 = sem("ex_l01")
        s_ho = sem("ex_ho")
        s_lo = sem("ex_lo")
        s_up = sem("ex_up_full")
        s_gelu = sem("ex_gelu_ready")
        s_hh = sem("ex_hh_ready")
        s_hl = sem("ex_hl_ready")
        s_down = sem("ex_down")
        s_eo = sem("ex_eo_ready")
        s_eoo = sem("ex_eo_out")
        s_eog = [sem("ex_eog0"), sem("ex_eog1"), sem("ex_eog2")]
        s_x2 = sem("ex_x2_in")
        s_c = sem("ex_c")
        s_sum = sem("ex_sum")
        s_out = sem("ex_out")

        def pieces(eng, e, last, step):
            half = e * (FC // 2)
            step(half, 0, e, True, False, False, False)
            step(half, 1, e, False, False, False, False)
            with eng.Fori(1, FC // 2 - 1) as j:
                step(half + j, 0, e, False, False, False, False)
                step(half + j, 1, e, False, False, False, False)
            step(half + (FC // 2 - 1), 0, e, False, False, last, False)
            step(half + (FC // 2 - 1), 1, e, False, True, last, last)

        block = es.enter_context(nc.Block())

        @block.sync
        def _(sp):
            def load01(n, par):
                sp.dma_start(raw01[:, par, :], w01[n, :, :]).then_inc(s_r01[par], 16)

            def loado(n, par):
                sp.dma_start(rawo[:, par, :], wout[n, :, :]).then_inc(s_ro[par], 16)

            load01(0, 0)
            loado(0, 0)
            load01(1, 1)
            loado(1, 1)
            sp.sem_inc(s_eoo, 32)

            def step(half, par, e, head, tail, no_next2, no_next):
                n = half * 2 + par
                if not no_next2:
                    sp.wait_ge(s_l01, n + 1)
                    load01(n + 2, par)
                    sp.wait_ge(s_lo, n + 1)
                    loado(n + 2, par)

            def expert(e, last):
                pieces(sp, e, last, step)
                sp.wait_ge(s_eo, 2 * e + 4)
                for r in range(2):
                    sp.dma_start(eo_scr[e, P * r:P * (r + 1), :], eo[:, r, :]).then_inc(s_eoo, 16)

            def gather(e, which):
                sp.wait_ge(s_eoo, 32 * e + 64)
                q = CAP * (e % 4)
                sp.dma_start(eog[q:q + CAP, e // 4, :, :], eo_scr[e, :, :].rearrange("(g c) m -> c g m", c=CAP))\
                  .then_inc(s_eog[which], 16)

            with sp.Fori(0, 4) as e:
                expert(e, False)
            sp.dma_start(x2[:, :, :], x2_scr.rearrange("g p m -> p g m")).then_inc(s_x2, 16)
            with sp.Fori(4, E - 1) as e:
                expert(e, False)
            for e in range(E - 1):
                gather(e, e // 4)
            expert(E - 1, True)
            gather(E - 1, 2)
            for g in range(G):
                sp.wait_ge(s_sum, g + 1)
                sp.dma_start(out[g, :, :], x2[:, g, :]).then_inc(s_out, 16)
            sp.wait_ge(s_out, 16 * G)

        def flat01(t, par):
            return t[:, par, :, :, :].rearrange("p a k n -> p (a k n)")

        @block.scalar
        def _(act):
            def hi01(par, count):
                act.wait_ge(s_r01[par], count)
                nc.scalar.activation(flat01(w01h, par), raw01[:, par, :], ACT.Copy).then_inc(s_h01, 1)

            def hio(par, count):
                act.wait_ge(s_ro[par], count)
                nc.scalar.activation(woh[:, par, :], rawo[:, par, :], ACT.Copy).then_inc(s_ho, 1)

            def step(half, par, e, head, tail, no_next2, no_next):
                n = half * 2 + par
                act.wait_ge(s_up, n + 1)
                nc.scalar.activation(gelu[:, par, :], up[:, par, 0:ROWS], ACT.Gelu_apprx_tanh).then_inc(s_gelu, 1)
                if not no_next2:
                    hi01(par, half * 16 + 32)
                if not no_next:
                    act.wait_ge(s_down, n + 1)
                    hio(1 - par, half * 16 + 16 * (1 + par))
                if tail:
                    act.wait_ge(s_down, n + 2)
                    act.wait_ge(s_eoo, 32 * e + 32)
                    nc.scalar.activation(eo[:, 0, :], acc[:, 0, :], ACT.Copy).then_inc(s_eo, 1)

            act.sem_inc(s_eo, 2)
            hi01(0, 16)
            hio(0, 16)
            hi01(1, 16)
            with act.Fori(0, E - 1) as e:
                pieces(act, e, False, step)
            pieces(act, E - 1, True, step)

        @block.vector
        def _(dve):
            def lo01(par, count):
                dve.wait_ge(s_h01, count)
                nc.vector.tensor_tensor(flat01(w01l, par), raw01[:, par, :], flat01(w01h, par), ALU.subtract)\
                  .then_inc(s_l01, 1)

            def loo(par, count):
                dve.wait_ge(s_ho, count)
                nc.vector.tensor_tensor(wol[:, par, :], rawo[:, par, :], woh[:, par, :], ALU.subtract).then_inc(s_lo, 1)

            def step(half, par, e, head, tail, no_next2, no_next):
                n = half * 2 + par
                dve.wait_ge(s_gelu, n + 1)
                nc.vector.tensor_tensor(hid[:, par, :], gelu[:, par, :], up[:, par, ROWS:2 * ROWS], ALU.mult)
                nc.vector.tensor_tensor(hh[:, par, :], gelu[:, par, :], up[:, par, ROWS:2 * ROWS], ALU.mult)\
                  .then_inc(s_hh, 1)
                dve.wait_ge(s_hh, n + 2)
                nc.vector.tensor_tensor(hl[:, par, :], hid[:, par, :], hh[:, par, :], ALU.subtract).then_inc(s_hl, 1)
                if not no_next2:
                    lo01(par, n + 3)
                if not no_next:
                    loo(1 - par, n + 2)
                if tail:
                    dve.wait_ge(s_down, n + 2)
                    dve.wait_ge(s_eoo, 32 * e + 32)
                    nc.vector.tensor_copy(eo[:, 1, :], acc[:, 1, :]).then_inc(s_eo, 1)

            dve.sem_inc(s_hh, 1)
            lo01(0, 1)
            loo(0, 1)
            lo01(1, 2)
            with dve.Fori(0, E - 1) as e:
                pieces(dve, e, False, step)
            pieces(dve, E - 1, True, step)
            dve.wait_ge(s_x2, 16)
            for g in range(G):
                dve.wait_ge(s_c, g + 1)
                nc.vector.tensor_tensor(x2[:, g, :], x2[:, g, :], comb[:, g % 4, :], ALU.add).then_inc(s_sum, 1)

        @block.tensor
        def _(pe):
            def product3(out, lh, ll, rh, rl, start, stop):
                nc.tensor.matmul(out, lh, rh, start=start, stop=False)
                nc.tensor.matmul(out, lh, rl, start=False, stop=False)
                return nc.tensor.matmul(out, ll, rh, start=False, stop=stop)

            def first_products(n, par, e):
                pe.wait_ge(s_l01, n + 1)
                for a in range(2):
                    for k in range(KC):
                        ins = product3(up[:, par, ROWS * a:ROWS * (a + 1)], w01h[:, par, a, k, :], w01l[:, par, a, k, :],
                                       xeh[:, k, e, :], xel[:, k, e, :], k == 0, k == KC - 1)
                ins.then_inc(s_up, 1)

            def step(half, par, e, head, tail, no_next2, no_next):
                n = half * 2 + par
                if not no_next:
                    pe.wait_ge(s_hh, n + 1)
                    first_products(n + 1, 1 - par, e + 1 if tail else e)
                if head:
                    pe.wait_ge(s_eo, 2 * e + 2)
                pe.wait_ge(s_lo, n + 1)
                pe.wait_ge(s_hl, n + 1)
                for r in range(2):
                    at = (slice(None), par, slice(P * r, P * (r + 1)))
                    ins = product3(acc[:, r, :], hh[at], hl[at], woh[:, par, :], wol[:, par, :], head, tail)
                ins.then_inc(s_down, 1)

            pe.sem_inc(s_down, 1)
            first_products(0, 0, 0)
            with pe.Fori(0, E - 1) as e:
                pieces(pe, e, False, step)
            pieces(pe, E - 1, True, step)
            for g0 in (0, 4):
                pe.wait_ge(s_eog[0], 64)
                for g in range(g0, g0 + 4):
                    if g >= 4:
                        pe.wait_ge(s_sum, g - 3)
                    nc.tensor.matmul(comb[:, g % 4, :], combT[:, 0, g, :], eog[:, 0, g, :], start=True, stop=False)
                pe.wait_ge(s_eog[1], 48)
                pe.wait_ge(s_eog[2], 16)
                for g in range(g0, g0 + 4):
                    nc.tensor.matmul(comb[:, g % 4, :], combT[:, 1, g, :], eog[:, 1, g, :], start=False, stop=True)\
                      .then_inc(s_c, 1)


def perceiver_layer(nc, x, ctx, xwq, xbq, xwk, xbk, xwv, xbv, xwo, xbo, wqkv, wo, bo, router, w01, wout,
                    ident, heads, tri, rowc, out):
    batches = ctx.shape[0]
    tiles = batches * NQ // P

    def scratch(name, shape):
        return nc.dram_tensor(name, shape, F32, kind="Internal").ap()

    q_scr = scratch("q_scratch", (batches, P, 4, NQ))
    o_scr = scratch("o_scratch", (batches, P, 4, NQ))
    x2_scr = scratch("x2_scratch", (tiles, P, D))
    xn_scr = scratch("xn_scratch", (tiles, P, D))
    lg_scr = scratch("lg_scratch", (tiles, P, E))
    eo_scr = scratch("eo_scratch", (E, ROWS, D))
    with ExitStack() as es:
        room, weights, weights_lo = self_weights(nc, es, wqkv, xwo, wo)
        cross_attention(nc, x, ctx, xwq, xbq, xwk, xbk, xwv, xbv, ident, heads, q_scr, o_scr, batches, room, weights)
        self_attention(nc, x, o_scr, weights, weights_lo, xbo, bo, router, ident, x2_scr, xn_scr, lg_scr, tiles)
    experts(nc, x2_scr, xn_scr, lg_scr, w01, wout, tri, rowc, ident, eo_scr, out)


def by_rows(w):
    return np.ascontiguousarray(w.reshape(-1, P, w.shape[1]).transpose(1, 0, 2))


def by_column(b):
    return np.ascontiguousarray(b.reshape(-1, P).T)


def constants():
    ident = np.eye(P, dtype=np.float32)
    heads = np.zeros((P, 2, P), np.float32)
    for pair in range(2):
        for h in range(2):
            at = DH * (2 * pair + h)
            heads[NQ * h:NQ * (h + 1), pair, at:at + DH] = 1
    eye2 = np.concatenate([np.eye(NQ), np.eye(NQ)]).astype(np.float32)
    heads = np.concatenate([heads.reshape(P, 2 * P), eye2], axis=1)
    tri = np.stack([np.triu(np.ones((P, P)), 1), np.ones((P, P))], axis=1).astype(np.float32)
    rowc = np.tile(np.concatenate([np.arange(E) - E, np.arange(CAP)]).astype(np.float32), (P, 1))
    return ident, heads, tri, rowc


def lay_out(x, ctx_1024, L0_xattn_wq, L0_xattn_bq, L0_xattn_wk, L0_xattn_bk, L0_xattn_wv, L0_xattn_bv, L0_xattn_wo,
            L0_xattn_bo, L0_attn_Wq, L0_attn_Wkv, L0_attn_Wo, L0_attn_bo, L0_ffn_router_w, L0_ffn_w0_kernel,
            L0_ffn_w1_kernel, L0_ffn_wo_kernel):
    b = ctx_1024.shape[0]
    ctx = np.zeros((b, NC * CH, D), np.float32)
    ctx[:, :NK] = ctx_1024
    ctx = np.ascontiguousarray(ctx.reshape(b, NC, CH, KC, P).transpose(0, 1, 4, 3, 2))
    hidden = L0_ffn_w0_kernel.shape[2]
    w01 = np.zeros((E, FC * P, 2, D), np.float32)
    w01[:, :hidden, 0] = L0_ffn_w0_kernel.transpose(0, 2, 1)
    w01[:, :hidden, 1] = L0_ffn_w1_kernel.transpose(0, 2, 1)
    w01 = np.ascontiguousarray(w01.reshape(E, FC, P, 2, KC, P).transpose(0, 1, 5, 3, 4, 2)).reshape(E * FC, P, 2 * KC * P)
    wout = np.zeros((E, FC * P, D), np.float32)
    wout[:, :hidden] = L0_ffn_wo_kernel
    ident, heads, tri, rowc = constants()
    return {
        "x": x.reshape(-1, P, D), "ctx": ctx,
        "xwq": by_rows(L0_xattn_wq.T), "xbq": by_column(L0_xattn_bq),
        "xwk": by_rows(L0_xattn_wk.T), "xbk": by_column(L0_xattn_bk),
        "xwv": by_rows(L0_xattn_wv.T), "xbv": by_column(L0_xattn_bv),
        "xwo": by_rows(L0_xattn_wo.T), "xbo": L0_xattn_bo.reshape(1, D),
        "wqkv": by_rows(np.concatenate([L0_attn_Wq, L0_attn_Wkv], axis=1)),
        "wo": by_rows(L0_attn_Wo), "bo": L0_attn_bo.reshape(1, D), "router": by_rows(L0_ffn_router_w),
        "w01": w01, "wout": wout.reshape(E * FC, P, D),
        "ident": ident, "heads": heads, "tri": tri, "rowc": rowc,
    }


def kernel(**inputs):
    from concourse import bacc
    from concourse.bass_utils import run_bass_kernel_spmd

    inputs = {name: np.asarray(a) for name, a in inputs.items()}
    arrays = lay_out(**inputs)
    nc = bacc.Bacc("TRN2", target_bir_lowering=False, num_devices=1)
    arrays = {f"in_{name}": np.ascontiguousarray(a) for name, a in arrays.items()}
    args = [nc.dram_tensor(name, a.shape, mybir.dt.from_np(a.dtype), kind="ExternalInput").ap()
            for name, a in arrays.items()]
    shape = inputs["x"].shape
    out = nc.dram_tensor("out_x", (shape[0] * shape[1] // P, P, D), F32, kind="ExternalOutput").ap()
    perceiver_layer(nc, *args, out)
    got = run_bass_kernel_spmd(nc, [arrays], core_ids=[0])
    return got.results[0]["out_x"].reshape(shape)
```

```python
from contextlib import ExitStack

import concourse.bass as bass
from concourse import mybir
import numpy as np

P = 128
D = 512
KC = D // P
NQ = 64
H = 16
DH = D // H
NK = 1601
CH = 402
NC = 4
LAST = NK - (NC - 1) * CH
KT = -(-NK // P)
HW = 256
EPS = 1e-5
SCALE = DH ** -0.5

SH = 64
SI = H * SH
SSCALE = SH ** -0.5

E = 8
CAP = 32
ROWS = 256
FC = 22

F32 = mybir.dt.float32
F32R = mybir.dt.float32r
ALU = mybir.AluOpType
ACT = mybir.ActivationFunctionType
AX = mybir.AxisListType


def tile_rows(t):
    return min(P, NK - P * t)


def tile_chunk(t):
    return (min(P * t + P, NK) - 1) // CH


TU = (KT + 1) // 2


def cross_order():
    order = []
    for g in range(4):
        ahead = int(g >= 2)
        s1, e1, s2, e2 = ((kind, (2 * g + n) % 8, 0, int(g == 3)) for n in (2, 3) for kind in "SE")
        k = [("K", (g + 2) % 4, c, ahead) for c in range(NC)]
        k_next = [("K", (g + 3) % 4, c, ahead) for c in range(NC)]
        t = [("t", g, d, 0) for d in range(TU)]
        m = [("m", g, d, 0) for d in range(TU)]
        v = [("V", 1 - g // 2, n, ahead) for n in range(KT)]
        x = [("X", 0, c, 1) for c in range(NC)]
        late = [("m", g - 1, TU - 1, 0), ("O", g - 1, 0, 0)]
        if g == 0:
            order += [t[0], s1, k[0], t[1], e1, m[0], k[1], t[2], m[1], s2, t[3], m[2], k[2], t[4], e2, m[3],
                      k[3], t[5], m[4], k_next[0], t[6], m[5], k_next[1]]
        elif g == 2:
            order += [t[0], s1] + late[1:] + [k[0], t[1], e1, m[0], k[1], t[2], m[1], x[2], s2, t[3], m[2],
                                              k_next[0], t[4], e2, m[3], x[3], k_next[1], t[5], m[4],
                                              ("Q", 0, 0, 1), k[2], t[6], m[5], k[3]]
        elif g == 1:
            order += [t[0], s1] + late + [k[2], t[1], e1, m[0], k[3], t[2], m[1], v[0], t[3], m[2], s2, v[1],
                                          t[4], m[3], v[2], e2, v[3], t[5], m[4], v[4], v[5],
                                          t[6], m[5], v[6], m[6], x[0], v[7], v[8], x[1]] + v[9:]
        else:
            order += [("D", 0, 0, 0), t[0]] + late + [k[2], t[1], m[0], k[3], t[2], m[1], s1, v[0], t[3], m[2],
                                                      v[1], e1, v[2], t[4], m[3], v[3], s2, t[5], m[4], v[4], e2, v[5],
                                                      t[6], m[5], v[6], m[6], v[7], ("O", 3, 0, 0), v[8],
                                                      ("N", 0, 0, 0), v[9], v[10], ("N", 1, 0, 0), v[11], v[12]]
    return order


def cross_prologue(tiles, q_units):
    early = tiles * 4 // q_units
    order = [("T", 0)]
    for t in range(1, early):
        order += [("T", t), ("C", t - 1)]
    order.append(("C", early - 1))
    beside = [("K", 0, 0), ("X", 1), ("K", 1, 0), ("W", 1), ("K", 0, 1), ("X", 2), ("K", 1, 1), ("K", 0, 2), ("X", 3),
              ("K", 1, 2), ("K", 0, 3)]
    for n in range(q_units):
        if n == 4:
            order.append(("C", tiles - 1))
        order.append(("U", n))
        t = early + n
        if t < tiles:
            order += [("C", t - 1)] if n else []
            order.append(("T", t))
        if n in (0, 2):
            order.append(("W", 0) if n == 0 else ("X", 0))
        if n >= 4:
            order += beside[:2]
            beside = beside[2:]
    v = [("V", 0, n) for n in range(KT)]
    order += beside + [("Q", 0), ("S", 0), ("K", 1, 3), ("E", 0)] + v[:3] + [("S", 1), v[3], ("E", 1)] + v[4:]
    assert sum(item[0] == "K" for item in order) == 2 * NC
    return [("X", 0, item[1], 0) if item[0] == "X" else (item + (0, 0))[:3] + (0,) for item in order]


ROOM = 3 * SI * KC + D * SI // P + D * KC
BANKS = 3
CROSS_PRO = 2 * NC + KT
CROSS_PRO_HI = 4 * NC + KT


def cross_numbered(order, start, start_hi, last=False):
    unit, hi = start, start_hi
    for kind, n, i, ahead in order:
        if last and ahead:
            continue
        yield kind, n, i, ahead, unit, hi
        unit += kind in "KVtN"
        hi += kind in "KVt" and (2 if kind == "K" else 1)


CROSS_UNITS = sum(item[0] in "KVtN" for item in cross_order())
CROSS_HIS = sum({"K": 2, "V": 1, "t": 1}.get(item[0], 0) for item in cross_order())
assert CROSS_UNITS % BANKS == 0


def cross_attention(nc, x, ctx, wq, bq, wk, bk, wv, bv, ident_in, sel_in, q_scr, o_scr, batches,
                    room, prefetch):
    rows = batches * NQ
    tiles = rows // P
    QN = min(512, rows)
    with ExitStack() as es:
        def sb(name, shape, dt=F32):
            return es.enter_context(nc.sbuf_tensor(name, shape, dt))

        def sem(name):
            return es.enter_context(nc.semaphore(name))

        cxh = room("xa_cxh", 0, [KC, NC * CH], F32R)
        cxl = room("xa_cxl", KC * NC * CH, [KC, NC * CH], F32R)
        wkh = room("xa_wkh", 2 * KC * NC * CH, [KC, D], F32R)
        raw = room("xa_raw", KC * (2 * NC * CH + D), [2, KC, CH], F32)
        wkl = sb("xa_wkl", [P, KC, D], F32R)
        wvh = sb("xa_wvh", [P, KC, D], F32R)
        wvl = sb("xa_wvl", [P, KC, D], F32R)
        kst = sb("xa_kst", [P, 2, 2, NC * CH], F32R)
        v_at = -(-nc.sbuf_base // 32) * 32
        sb("xa_vroom", [P, 2 * KT * HW])
        vh = nc.alloc_sbuf_tensor_at("xa_vh", [P, KT, HW], F32R, offset=v_at)
        vl = nc.alloc_sbuf_tensor_at("xa_vl", [P, KT, HW], F32R, offset=v_at + 4 * KT * HW)
        xnT = nc.alloc_sbuf_tensor_at("xa_xnT", [P, KC, rows], F32, offset=v_at)
        assert KC * rows + 4 * QN <= 2 * KT * HW
        qst = nc.alloc_sbuf_tensor_at("xa_qst", [P, 4, QN], F32, offset=v_at + 4 * KC * rows)
        probs = sb("xa_probs", [P, 4, NC * CH])
        pth = sb("xa_pth", [P, 2, 512], F32R)
        ptl = sb("xa_ptl", [P, 2, 512], F32R)
        qbh = sb("xa_qbh", [P, 2, 4, P], F32R)
        qbl = sb("xa_qbl", [P, 2, 4, P], F32R)
        xt = sb("xa_xt", [P, 4, D])
        xn = sb("xa_xn", [P, 2, D])
        qraw = xt[:, 0, :].rearrange("p (a g n) -> p a g n", a=2, g=4)
        ident = sb("xa_ident", [P, P])
        sel = sb("xa_sel", [P, 2, P])
        eye2 = sb("xa_eye2", [P, NQ])
        zero = sb("xa_zeros", [P, 1])
        bqs = sb("xa_bqs", [P, 4])
        bias = sb("xa_bias", [P, 3, 4])
        mx = sb("xa_mx", [P, 2, 2])
        negmax = sb("xa_negmax", [P, 2])
        rowsum = sb("xa_rowsum", [P, 2, 8])
        total = sb("xa_total", [P, 8])
        inv = sb("xa_inv", [P, 8])
        diag = sb("xa_diag", [P, 8, NQ])
        outT = sb("xa_outT", [P, 4, NQ])
        outn = sb("xa_outn", [P, 4, NQ])
        stat = sb("xa_stat", [P, 2, 6])
        mv = sb("xa_mv", [P, 2, 2])
        rstd = sb("xa_rstd", [P, 2, 1])
        pf = probs[:, :, :].rearrange("p a n -> p (a n)")
        wkv_raw = pf[:, 0:4096].rearrange("p (a k n) -> p a k n", a=2, k=KC)
        wq_sb = pf[:, 4096:6144].rearrange("p (k n) -> p k n", k=KC)

        sps = es.enter_context(nc.psum_tensor("xa_sps", [P, 4, 512], F32))
        work = es.enter_context(nc.psum_tensor("xa_work", [P, 3, 512], F32))
        ops = es.enter_context(nc.psum_tensor("xa_ops", [P, 512], F32))

        s_const = sem("xa_const")
        s_sel = sem("xa_sel_ready")
        s_wq = sem("xa_wq")
        s_wkv = [sem("xa_wk"), sem("xa_wv")]
        s_x = [sem(f"xa_x{i}") for i in range(4)]
        s_raw = [sem("xa_raw0"), sem("xa_raw1")]
        s_qin = sem("xa_qin")
        s_qout = [sem(f"xa_qout{i}") for i in range(4)]
        s_oout = sem("xa_oout")
        s_zero = sem("xa_zero")
        s_whi = sem("xa_whi")
        s_wlo = sem("xa_wlo")
        s_ln = sem("xa_ln")
        s_var = sem("xa_var")
        s_std = sem("xa_std")
        s_xn = sem("xa_xn_ready")
        s_xT = sem("xa_xT")
        s_xTc = sem("xa_xTc")
        s_bqs = sem("xa_bqs_ready")
        s_q = sem("xa_q")
        s_qs = sem("xa_qs")
        s_cxh = sem("xa_cxh_ready")
        s_cx = sem("xa_cx_ready")
        s_full = sem("xa_full")
        s_hi = sem("xa_hi")
        s_evac = sem("xa_evac")
        s_scores = sem("xa_scores")
        s_mx = sem("xa_mx_part")
        s_negmax = sem("xa_negmax_ready")
        s_exp = sem("xa_exp")
        s_pv = sem("xa_pv")
        s_out = sem("xa_out")
        s_tot = sem("xa_tot")
        s_diag = sem("xa_diag_ready")
        s_outr = sem("xa_outn_ready")
        s_qb = sem("xa_qb")

        QU = 4 * (rows // QN)
        CONSTS = 4 * 16
        prologue = list(cross_numbered(cross_prologue(tiles, QU), 0, 0))

        def unit(b, u):
            return b * CROSS_UNITS + u

        def hi_part(b, h):
            return b * CROSS_HIS + h

        def at_keys(c):
            return slice(CH * c, CH * (c + 1))

        def half(pair):
            return slice(2 * DH * pair, 2 * DH * (pair + 1))

        def query_block(r):
            return (slice(DH * r, DH * (r + 1)), slice(None), slice(None), slice(NQ * (r % 2), NQ * (r % 2 + 1)))

        block = es.enter_context(nc.Block())

        @block.sync
        def _(sp):
            def chunk(b, c):
                sp.dma_start(raw[:, c % 2, :, :], ctx[b, c, :, :, :]).then_inc(s_raw[c % 2], 16)

            def queries(b):
                for twice in range(2):
                    for pair in range(2):
                        sp.dma_start(qraw[NQ * twice:NQ * (twice + 1), pair, :, :],
                                     q_scr[b, 2 * DH * pair:2 * DH * (pair + 1), :, :]).then_inc(s_qin, 16)

            def load_x(t):
                sp.dma_start(xt[:, t % 4, :], x[t, :, :]).then_inc(s_x[t % 4], 16)

            for t in range(min(4, tiles)):
                load_x(t)
            sp.dma_start(ident[:, :], ident_in).then_inc(s_const, 16)
            for n, v in enumerate((bq, bk, bv)):
                sp.dma_start(bias[:, n, :], v).then_inc(s_const, 16)
            sp.dma_start(wq_sb, wq).then_inc(s_wq, 16)
            sp.dma_start(wkv_raw[:, 0, :, :], wk).then_inc(s_wkv[0], 16)
            for t in range(4, tiles):
                sp.wait_ge(s_xn, t - 3)
                load_x(t)
            chunk(0, 0)
            chunk(0, 1)
            sp.dma_start(wkv_raw[:, 1, :, :], wv).then_inc(s_wkv[1], 16)
            for c in range(2, NC):
                sp.wait_ge(s_cx, c - 1)
                chunk(0, c)
            sp.sem_inc(s_oout, 16)
            for slot in s_qout:
                sp.wait_ge(slot, 16 * (QU // 4))
            queries(0)

            def batch(b, last):
                if not last:
                    for c in range(NC):
                        sp.wait_ge(s_cx, b * NC + c + 3)
                        chunk(b + 1, c)
                        if c == 1:
                            sp.wait_ge(s_qb, 8 * b + 8)
                            queries(b + 1)
                sp.wait_ge(s_outr, 2 * b + 2)
                sp.dma_start(o_scr[b, :, :, :], outn[:, :, :]).then_inc(s_oout, 16)

            if batches > 1:
                with sp.Fori(0, batches - 1) as b:
                    batch(b, False)
            v_end = max(u for kind, _, _, _, u, _ in cross_numbered(cross_order(), CROSS_PRO, CROSS_PRO_HI, last=True) if kind == "V")
            sp.wait_ge(s_full, unit(batches - 1, v_end) + 1)
            for dst, src, arrived in prefetch:
                sp.dma_start(dst, src).then_inc(arrived, 16)
            batch(batches - 1, True)
            sp.wait_ge(s_oout, 16 * batches + 16)

        @block.gpsimd
        def _(pool):
            nc.gpsimd.memset(zero[:, :], 0.0).then_inc(s_zero, 1)
            nc.gpsimd.memset(qbh[:, :, :, :].bitcast(F32), 0.0).then_inc(s_zero, 1)
            nc.gpsimd.memset(qbl[:, :, :, :].bitcast(F32), 0.0).then_inc(s_zero, 1)
            pool.dma_start(sel[:, :, :], sel_in[:, 0:2 * P].rearrange("p (a n) -> p a n", a=2)).then_inc(s_sel, 16)
            pool.dma_start(eye2[:, :], sel_in[:, 2 * P:2 * P + NQ]).then_inc(s_sel, 16)
            for u in range(QU):
                pool.wait_ge(s_qs, u + 1)
                b0 = (u // 4) * (QN // NQ)
                pool.dma_start(q_scr[b0:b0 + QN // NQ, :, u % 4, :].rearrange("b p n -> p b n"),
                               qst[:, u % 4, 0:QN].rearrange("p (b n) -> p b n", n=NQ)).then_inc(s_qout[u % 4], 16)

            def item(b, kind, n, i, ahead, u, h):
                if kind == "X" and i >= 2:
                    pool.wait_ge(s_cx, NC * (b + ahead) + i)
                    pool.wait_ge(s_cxh, NC * (b + ahead) + i + 1)
                    nc.gpsimd.tensor_tensor(cxl[:, :, at_keys(i)], raw[:, i % 2, :, :], cxh[:, :, at_keys(i)],
                                            ALU.subtract).then_inc(s_cx, 1)
                elif kind == "Q":
                    if ahead:
                        pool.wait_ge(s_scores, 8 * b + 8)
                    pool.wait_ge(s_qin, 64 * (b + ahead) + 64)
                    if ahead:
                        pool.wait_ge(s_cx, NC * (b + ahead) + NC)
                    for r in range(4):
                        at, q = query_block(r), qraw[DH * r:DH * (r + 1), :, :, :]
                        spread = zero[DH * r:DH * (r + 1), :].unsqueeze(2).unsqueeze(3).to_broadcast([DH, 2, 4, NQ])
                        nc.gpsimd.tensor_tensor(qbh[at], q, spread, ALU.add).then_inc(s_qb, 1)
                        pool.wait_ge(s_qb, 8 * (b + ahead) + 2 * r + 1)
                        nc.gpsimd.tensor_tensor(qbl[at], q, qbh[at], ALU.subtract).then_inc(s_qb, 1)
                        pool.wait_ge(s_qb, 8 * (b + ahead) + 2 * r + 2)

            pool.wait_ge(s_zero, 3)
            item(0, "Q", 0, 0, 0, 0, 0)
            if batches > 1:
                with pool.Fori(0, batches - 1) as b:
                    for step in cross_numbered(cross_order(), CROSS_PRO, CROSS_PRO_HI):
                        item(b, *step)

        @block.scalar
        def _(act):
            def item(b, kind, n, i, ahead, u, h):
                at_bank = u % BANKS
                if kind == "X":
                    act.wait_ge(s_raw[i % 2], 16 * (2 * (b + ahead) + i // 2 + 1))
                    nc.scalar.activation(cxh[:, :, at_keys(i)], raw[:, i % 2, :, :], ACT.Copy).then_inc(s_cxh, 1)
                elif kind == "E":
                    act.wait_ge(s_negmax, 8 * (b + ahead) + n + 1)
                    nc.scalar.activation(probs[:, n % 4, 0:3 * CH].rearrange("p (c n) -> p c n", c=3),
                                         sps[:, 0:3, 0:CH], ACT.Exp, bias=negmax[:, n % 2:n % 2 + 1],
                                         accum_out=rowsum[:, 0, n:n + 1])
                    nc.scalar.activation(probs[:, n % 4, 3 * CH:NK], sps[:, 3, 0:LAST], ACT.Exp,
                                         bias=negmax[:, n % 2:n % 2 + 1],
                                         accum_out=rowsum[:, 1, n:n + 1]).then_inc(s_exp, 1)
                elif kind == "K":
                    act.wait_ge(s_full, unit(b, u) + 1)
                    for pair in range(2):
                        at = half(pair)
                        nc.scalar.activation(kst[at, n % 2, pair, at_keys(i)], work[at, at_bank, 0:CH],
                                             ACT.Identity, bias=bias[at, 1, n:n + 1]).then_inc(s_hi, 1)
                elif kind == "V":
                    m = tile_rows(i)
                    act.wait_ge(s_full, unit(b, u) + 1)
                    nc.scalar.activation(vh[0:m, i, :], work[0:m, at_bank, 0:HW], ACT.Copy).then_inc(s_hi, 1)
                elif kind == "t":
                    m, w = tile_rows(2 * i), 256 * min(2, KT - 2 * i)
                    tn = TU * n + i
                    act.wait_ge(s_pv, 4 * TU * b + tn + 1)
                    act.wait_ge(s_full, unit(b, u) + 1)
                    nc.scalar.activation(pth[0:m, tn % 2, 0:w], work[0:m, at_bank, 0:w], ACT.Copy).then_inc(s_hi, 1)
                elif kind == "O":
                    act.wait_ge(s_pv, 4 * TU * b + TU * (n + 1) + 2)
                    for r in range(4):
                        ins = nc.scalar.activation(outT[32 * r:32 * r + 32, n, :],
                                                   ops[32 * r:32 * r + 32, NQ * r:NQ * (r + 1)], ACT.Copy)
                    ins.then_inc(s_out, 1)
                elif kind == "W":
                    act.wait_ge(s_wkv[n], 16)
                    nc.scalar.activation((wkh, wvh)[n][:, :, :], wkv_raw[:, n, :, :], ACT.Copy).then_inc(s_whi, 1)
                elif kind == "T":
                    act.wait_ge(s_var, n + 1)
                    nc.scalar.activation(rstd[:, n % 2, :], rstd[:, n % 2, :], ACT.Sqrt).then_inc(s_std, 1)
                elif kind == "C":
                    act.wait_ge(s_xT, n + 1)
                    nc.scalar.activation(xnT[:, :, P * n:P * (n + 1)],
                                         ops[:, :].rearrange("p (k n) -> p k n", k=KC),
                                         ACT.Copy).then_inc(s_xTc, 1)
                elif kind == "U":
                    act.wait_ge(s_q, n + 1)
                    if n >= 4:
                        act.wait_ge(s_qout[n % 4], 16 * (n // 4))
                    nc.scalar.activation(qst[:, n % 4, 0:QN], sps[:, n % 4, 0:QN], ACT.Identity,
                                         bias=bqs[:, n % 4:n % 4 + 1], scale=SCALE).then_inc(s_qs, 1)

            act.sem_inc(s_exp, 1)
            act.sem_inc(s_out, 1)
            act.wait_ge(s_const, CONSTS)
            nc.scalar.mul(bqs[:, :], bias[:, 0, :], SCALE).then_inc(s_bqs, 1)
            act.wait_ge(s_bqs, 1)
            for step in prologue:
                item(0, *step)
            if batches > 1:
                with act.Fori(0, batches - 1) as b:
                    for step in cross_numbered(cross_order(), CROSS_PRO, CROSS_PRO_HI):
                        item(b, *step)
            for step in cross_numbered(cross_order(), CROSS_PRO, CROSS_PRO_HI, last=True):
                item(batches - 1, *step)

        @block.vector
        def _(dve):
            def item(b, kind, n, i, ahead, u, h):
                at_bank = u % BANKS
                if kind == "X" and (i < 2 or not ahead):
                    dve.wait_ge(s_cxh, NC * (b + ahead) + i + 1)
                    nc.vector.tensor_tensor(cxl[:, :, at_keys(i)], raw[:, i % 2, :, :], cxh[:, :, at_keys(i)],
                                            ALU.subtract).then_inc(s_cx, 1)
                elif kind == "S":
                    a = n % 2
                    dve.wait_ge(s_scores, 8 * (b + ahead) + n + 1)
                    nc.vector.tensor_reduce(mx[:, a, 0:1], sps[:, 0:3, 0:CH], AX.XY, ALU.max).then_inc(s_mx, 1)
                    nc.vector.tensor_reduce(mx[:, a, 1:2], sps[:, 3, 0:LAST], AX.X, ALU.max).then_inc(s_mx, 1)
                    dve.wait_ge(s_mx, 16 * (b + ahead) + 2 * n + 2)
                    nc.vector.tensor_scalar(negmax[:, a:a + 1], mx[:, a, 0:1], mx[:, a, 1:2], -1.0,
                                            ALU.max, ALU.mult).then_inc(s_negmax, 1)
                elif kind == "K":
                    for pair in range(2):
                        at = half(pair)
                        dve.wait_ge(s_hi, hi_part(b, h) + pair + 1)
                        ins = nc.vector.scalar_tensor_tensor(kst[half(1 - pair), n % 2, pair, at_keys(i)],
                                                             work[at, at_bank, 0:CH], bias[at, 1, n:n + 1],
                                                             kst[at, n % 2, pair, at_keys(i)], ALU.add, ALU.subtract)
                    ins.then_inc(s_evac, 1)
                elif kind == "V":
                    m = tile_rows(i)
                    dve.wait_ge(s_hi, hi_part(b, h) + 1)
                    nc.vector.tensor_tensor(vl[0:m, i, :], work[0:m, at_bank, 0:HW], vh[0:m, i, :],
                                            ALU.subtract).then_inc(s_evac, 1)
                elif kind == "t":
                    m, w = tile_rows(2 * i), 256 * min(2, KT - 2 * i)
                    a = (TU * n + i) % 2
                    dve.wait_ge(s_hi, hi_part(b, h) + 1)
                    nc.vector.tensor_tensor(ptl[0:m, a, 0:w], work[0:m, at_bank, 0:w], pth[0:m, a, 0:w],
                                            ALU.subtract).then_inc(s_evac, 1)
                elif kind == "D":
                    dve.wait_ge(s_exp, 8 * b + 9)
                    nc.vector.tensor_tensor(total[:, :], rowsum[:, 0, :], rowsum[:, 1, :], ALU.add).then_inc(s_tot, 1)
                    dve.wait_ge(s_tot, 2 * b + 1)
                    nc.vector.reciprocal(inv[:, :], total[:, :]).then_inc(s_tot, 1)
                    dve.wait_ge(s_tot, 2 * b + 2)
                    nc.vector.tensor_tensor(diag[:, :, :], eye2[:, :].unsqueeze(1).to_broadcast([P, 8, NQ]),
                                            inv[:, :].unsqueeze(2).to_broadcast([P, 8, NQ]), ALU.mult)\
                      .then_inc(s_diag, 1)
                elif kind == "N":
                    at = (slice(None), slice(2 * n, 2 * n + 2), slice(None))
                    dve.wait_ge(s_oout, 16 * b + 16)
                    dve.wait_ge(s_out, 4 * b + 2 * n + 3)
                    dve.wait_ge(s_full, unit(b, u) + 1)
                    nc.vector.tensor_tensor(outn[at], outT[at],
                                            work[:, at_bank, 0:P].rearrange("p (g n) -> p g n", g=2),
                                            ALU.mult).then_inc(s_evac, 1)
                    dve.wait_ge(s_evac, unit(b, u) + 1)
                    nc.vector.tensor_tensor(outn[at], outn[at],
                                            bias[:, 2, 2 * n:2 * n + 2].unsqueeze(2).to_broadcast([P, 2, NQ]),
                                            ALU.add).then_inc(s_outr, 1)
                elif kind == "W":
                    dve.wait_ge(s_whi, n + 1)
                    nc.vector.tensor_tensor((wkl, wvl)[n][:, :, :], wkv_raw[:, n, :, :], (wkh, wvh)[n][:, :, :],
                                            ALU.subtract).then_inc(s_wlo, 1)
                elif kind == "T":
                    a = n % 2
                    dve.wait_ge(s_x[n % 4], 16 * (n // 4 + 1))
                    nc.vector.bn_stats(stat[:, a, :], xt[:, n % 4, :]).then_inc(s_ln, 1)
                    dve.wait_ge(s_ln, 3 * n + 1)
                    nc.vector.bn_aggr(mv[:, a, :], stat[:, a, :]).then_inc(s_ln, 1)
                    dve.wait_ge(s_ln, 3 * n + 2)
                    nc.vector.tensor_scalar(rstd[:, a, :], mv[:, a, 1:2], EPS, None, ALU.add).then_inc(s_var, 1)
                    dve.wait_ge(s_std, n + 1)
                    nc.vector.reciprocal(rstd[:, a, :], rstd[:, a, :]).then_inc(s_ln, 1)
                    dve.wait_ge(s_ln, 3 * n + 3)
                    if n >= 2:
                        dve.wait_ge(s_xT, n - 1)
                    nc.vector.tensor_scalar(xn[:, a, :], xt[:, n % 4, :], mv[:, a, 0:1], rstd[:, a, :],
                                            ALU.subtract, ALU.mult).then_inc(s_xn, 1)

            dve.wait_ge(s_const, CONSTS)
            for step in prologue:
                if step[:3] == ("V", 0, 0):
                    for slot in s_qout:
                        dve.wait_ge(slot, 16 * (QU // 4))
                item(0, *step)
            dve.wait_ge(s_sel, 32)
            if batches > 1:
                with dve.Fori(0, batches - 1) as b:
                    for step in cross_numbered(cross_order(), CROSS_PRO, CROSS_PRO_HI):
                        item(b, *step)
            for step in cross_numbered(cross_order(), CROSS_PRO, CROSS_PRO_HI, last=True):
                item(batches - 1, *step)

        @block.tensor
        def _(pe):
            def product3(out, lh, ll, rh, rl, start, stop):
                nc.tensor.matmul(out, lh, rh, start=start, stop=False)
                nc.tensor.matmul(out, lh, rl, start=False, stop=False)
                return nc.tensor.matmul(out, ll, rh, start=False, stop=stop)

            def free_bank(b, u):
                if u >= BANKS:
                    pe.wait_ge(s_evac, unit(b, u) - BANKS + 1)

            def item(b, kind, n, i, ahead, u, h):
                at_bank = u % BANKS
                if kind == "S":
                    j = n // 2
                    if n % 2 == 0:
                        pe.wait_ge(s_qb, 8 * (b + ahead) + 8)
                        pe.wait_ge(s_evac, k_done(b, n, u))
                    pe.wait_ge(s_exp, 8 * (b + ahead) + n + 1)
                    for c in range(NC):
                        keys = kst[:, j % 2, n % 2, at_keys(c)]
                        nc.tensor.matmul(sps[:, c, 0:CH], qbh[:, n % 2, j, :], keys, start=True, stop=False)
                        ins = nc.tensor.matmul(sps[:, c, 0:CH], qbl[:, n % 2, j, :], keys, start=False, stop=True)
                    ins.then_inc(s_scores, 1)
                elif kind == "K":
                    free_bank(b, u)
                    pe.wait_ge(s_cx, NC * (b + ahead) + i + 1)
                    if u == 0:
                        pe.wait_ge(s_wlo, 1)
                    for k in range(KC):
                        w = (slice(None), k, slice(P * n, P * (n + 1)))
                        at = (slice(None), k, at_keys(i))
                        ins = product3(work[:, at_bank, 0:CH], wkh[w], wkl[w], cxh[at], cxl[at],
                                       k == 0, k == KC - 1)
                    ins.then_inc(s_full, 1)
                elif kind == "V":
                    m = tile_rows(i)
                    free_bank(b, u)
                    pe.wait_ge(s_cx, NC * (b + ahead) + tile_chunk(i) + 1)
                    if u < CROSS_PRO:
                        pe.wait_ge(s_wlo, 2)
                    for k in range(KC):
                        at = (slice(None), k, slice(P * i, P * i + m))
                        w = (slice(None), k, slice(HW * n, HW * (n + 1)))
                        ins = product3(work[0:m, at_bank, 0:HW], cxh[at], cxl[at], wvh[w], wvl[w],
                                       k == 0, k == KC - 1)
                    ins.then_inc(s_full, 1)
                elif kind == "t":
                    if i == 0:
                        pe.wait_ge(s_exp, 8 * b + 2 * n + 3)
                    free_bank(b, u)
                    for tt in range(min(2, KT - 2 * i)):
                        t = 2 * i + tt
                        m = tile_rows(t)
                        for pp in range(2):
                            at = 256 * tt + P * pp
                            ins = nc.tensor.transpose(work[0:m, at_bank, at:at + P],
                                                      probs[:, (2 * n + pp) % 4, P * t:P * t + m], ident[:, :])
                    ins.then_inc(s_full, 1)
                elif kind == "m":
                    pe.wait_ge(s_evac, unit(b, transposed[n, i]) + 1)
                    if i == 0:
                        pe.wait_ge(s_out, 4 * b + n + 1)
                    for tt in range(min(2, KT - 2 * i)):
                        t = 2 * i + tt
                        m = tile_rows(t)
                        v = (slice(0, m), t, slice(P * (n % 2), P * (n % 2 + 1)))
                        at = (slice(0, m), (TU * n + i) % 2, slice(256 * tt, 256 * (tt + 1)))
                        ins = product3(ops[:, 0:256], vh[v], vl[v], pth[at], ptl[at], t == 0, t == KT - 1)
                    ins.then_inc(s_pv, 1)
                elif kind == "N":
                    pe.wait_ge(s_diag, b + 1)
                    free_bank(b, u)
                    for pp in range(2):
                        ins = nc.tensor.matmul(work[:, at_bank, 0:P], sel[:, pp, :],
                                               diag[:, 4 * n + pp:4 * n + pp + 3:2, :],
                                               start=(pp == 0), stop=(pp == 1))
                    ins.then_inc(s_full, 1)
                elif kind == "C":
                    pe.wait_ge(s_xn, n + 1)
                    if n:
                        pe.wait_ge(s_xTc, n)
                    for k in range(KC):
                        ins = nc.tensor.transpose(ops[:, P * k:P * (k + 1)], xn[:, n % 2, P * k:P * (k + 1)],
                                                  ident[:, :])
                    ins.then_inc(s_xT, 1)
                elif kind == "U":
                    pe.wait_ge(s_wq, 16)
                    pe.wait_ge(s_xTc, (n // 4 + 1) * (QN // P))
                    if n >= 4:
                        pe.wait_ge(s_qs, n - 3)
                    for k in range(KC):
                        ins = nc.tensor.matmul(sps[:, n % 4, 0:QN], wq_sb[:, k, P * (n % 4):P * (n % 4 + 1)],
                                               xnT[:, k, QN * (n // 4):QN * (n // 4 + 1)],
                                               start=(k == 0), stop=(k == KC - 1))
                    ins.then_inc(s_q, 1)

            first_k = next(u for kind, n, i, _, u, _ in prologue if (kind, n, i) == ("K", 0, NC - 1))
            k_end = {n: u for kind, n, i, _, u, _ in cross_numbered(cross_order(), CROSS_PRO, CROSS_PRO_HI) if kind == "K" and i == NC - 1}

            def k_done(b, n, u):
                if u < CROSS_PRO:
                    return first_k + 1
                if n == 2:
                    return unit(b, u) - BANKS
                return unit(b, k_end[n // 2]) + 1

            pe.sem_inc(s_pv, 2)
            pe.wait_ge(s_const, CONSTS)
            for step in prologue:
                if step[0] == "S":
                    pe.wait_ge(s_qs, QU)
                    pe.wait_ge(s_sel, 32)
                item(0, *step)

            if batches > 1:
                transposed = {(n, i): u for kind, n, i, _, u, _ in cross_numbered(cross_order(), CROSS_PRO, CROSS_PRO_HI) if kind == "t"}
                with pe.Fori(0, batches - 1) as b:
                    for step in cross_numbered(cross_order(), CROSS_PRO, CROSS_PRO_HI):
                        item(b, *step)
            transposed = {(n, i): u for kind, n, i, _, u, _ in cross_numbered(cross_order(), CROSS_PRO, CROSS_PRO_HI, last=True) if kind == "t"}
            for step in cross_numbered(cross_order(), CROSS_PRO, CROSS_PRO_HI, last=True):
                item(batches - 1, *step)


SELF_STEPS = [("TQ", 0), ("O1", 1), ("TL", -1), ("S", 0), ("TX", 1), ("LG", -1), ("SM", 0), ("QK", 1), ("TP", 0),
              ("V0", 1), ("O2", 0), ("V1", 1)]
SELF_UNITS = {"TQ": 0, "TL": 1, "O1": 1, "LG": 1, "S": 0, "SM": 0, "TX": 1, "QK": 4, "TP": 4, "V0": 1, "V1": 1, "O2": 1}
RING = 3
SELF_PER = sum(SELF_UNITS.values())
assert SELF_PER % RING == 0


def numbered(kinds, at):
    first = {}
    for kind in kinds:
        first[kind] = at
        at += SELF_UNITS[kind]
    return first, at


SELF_PROLOGUE, _n = numbered(["O1", "TX", "QK", "V0", "V1"], 0)
SELF_START = _n - SELF_UNITS["TL"] - SELF_UNITS["LG"]
SELF_BODY, _n = numbered([kind for kind, _ in SELF_STEPS], SELF_START)
SELF_LAST, _n = numbered([kind for kind, shift in SELF_STEPS if shift < 1], SELF_START)
SELF_TAIL, _n = numbered(["TL", "LG"], _n)
SELF_PIECES = 8


def self_weights(nc, es, wqkv, wo1, wo2):
    KI = SI // P
    base = -(-nc.sbuf_base // 32) * 32
    es.enter_context(nc.sbuf_tensor("room", [P, ROOM], F32))

    def place(name, word, shape, dt):
        assert word + int(np.prod(shape)) <= ROOM
        return nc.alloc_sbuf_tensor_at(name, [P] + shape, dt, offset=base + 4 * word)

    piece = KC * D
    sources = [wqkv[:, :, D * n:D * (n + 1)] for n in range(6)] + [wo2[:, KC * n:KC * (n + 1), :] for n in range(KI // KC)]
    loads, lo = [], []
    for n, src in enumerate([wo1] + sources):
        raw = place(f"sa_raw{n}", piece * n, [KC, D], F32)
        loads.append((raw[:, :, :], src, es.enter_context(nc.semaphore(f"sa_weights{n}"))))
        if n:
            lo.append(place(f"sa_lo{n}", piece * n, [KC, D], F32R))
    return place, loads, lo


def self_attention(nc, x, o_scr, prefetch, lo, bo1, bo2, router, ident_in, x2_scr, xn_scr, lg_scr, tiles):
    with ExitStack() as es:
        def sb(name, shape, dt=F32):
            return es.enter_context(nc.sbuf_tensor(name, shape, dt))

        def sem(name):
            return es.enter_context(nc.semaphore(name))

        KI = SI // P
        wqh = sb("sa_wqh", [P, KC, 3 * SI], F32R)
        woh = sb("sa_woh", [P, KI, D], F32R)
        wo1_sb = prefetch[0][0]
        raw = [dst for dst, _, _ in prefetch[1:]]
        s_weights = [sem for _, _, sem in prefetch]
        router_sb = sb("sa_router", [P, KC, E])
        kbd = sb("sa_kbd", [P, KI, 2 * P])
        qT = sb("sa_qT", [P, KI, P])
        pT = sb("sa_pT", [P, 2, 4, P])
        pc = pT[:, :, :, :].rearrange("p a h n -> p (a h n)").rearrange("p (h n) -> p h n", h=H)
        ident = sb("sa_ident", [P, P])
        bos = sb("sa_bos", [P, 2, D])
        oin = sb("sa_oin", [P, KC, P])
        xin = sb("sa_xin", [P, D])
        xb = sb("sa_xb", [P, D])
        x1 = sb("sa_x1", [P, D])
        x1b = sb("sa_x1b", [P, D])
        xn = sb("sa_xn", [P, D])
        xTh = sb("sa_xTh", [P, KC, P], F32R)
        xTl = sb("sa_xTl", [P, KC, P], F32R)
        rows = sb("sa_rows", [P, 3, SI])
        prob = sb("sa_prob", [P, H, P])
        aTh = sb("sa_aTh", [P, KI, P], F32R)
        aTl = sb("sa_aTl", [P, KI, P], F32R)
        x2 = sb("sa_x2", [P, D])
        xn3 = sb("sa_xn3", [P, D])
        xn3T = sb("sa_xn3T", [P, KC, P])
        lg = sb("sa_lg", [P, E])
        stat = sb("sa_stat", [P, 2, 6])
        mv = sb("sa_mv", [P, 2, 2])
        rstd = sb("sa_rstd", [P, 2, 1])
        idle = sb("sa_idle", [P, 2])
        mx = sb("sa_mx", [P, H])
        tot = sb("sa_tot", [P, 2, H])

        big = es.enter_context(nc.psum_tensor("sa_big", [P, 4, 512], F32))
        ring = es.enter_context(nc.psum_tensor("sa_ring", [P, RING, 512], F32))

        s_const = sem("sa_const")
        s_whi = sem("sa_whi")
        s_wlo = sem("sa_wlo")
        s_zero = sem("sa_zero")
        s_oin = sem("sa_oin_ready")
        s_xin = sem("sa_xin_ready")
        s_xb = sem("sa_xb_ready")
        s_x1b = sem("sa_x1b_ready")
        s_ln = [sem("sa_ln1"), sem("sa_ln3")]
        s_var = [sem("sa_var1"), sem("sa_var3")]
        s_std = [sem("sa_std1"), sem("sa_std3")]
        s_xn = sem("sa_xn_ready")
        s_xn3 = sem("sa_xn3_ready")
        s_xTh = sem("sa_xTh_ready")
        s_full = sem("sa_full")
        s_free = [sem(f"sa_free{i}") for i in range(RING)]
        s_tq = sem("sa_tq")
        s_qT = sem("sa_qT_ready")
        s_kbd = sem("sa_kbd_ready")
        s_s = sem("sa_scores")
        s_sm = sem("sa_softmax")
        s_sub = sem("sa_sub")
        s_exp = sem("sa_exp")
        s_prob = sem("sa_prob_ready")
        s_pv = sem("sa_pv")
        s_aTh = sem("sa_aTh_ready")
        s_aTl = sem("sa_aTl_ready")
        s_x2o = sem("sa_x2_out")
        s_xno = sem("sa_xn_out")
        s_lgo = sem("sa_lg_out")

        CONSTS = 4 * 16
        PROLOGUE, TAIL = -1, tiles

        def steps(t, last):
            for kind, shift in SELF_STEPS:
                if not ((shift < 0 and isinstance(t, int) and t == 0) or (shift > 0 and last)):
                    yield kind, shift

        def first(kind, tb):
            if isinstance(tb, int) and tb == PROLOGUE:
                return SELF_PROLOGUE[kind], 0
            if isinstance(tb, int) and tb >= tiles - 1:
                return (SELF_TAIL if tb == TAIL else SELF_LAST)[kind], tiles - 1
            if isinstance(tb, int) and tb == 0 and kind in ("O1", "TX"):
                return SELF_BODY[kind] + SELF_UNITS["LG"] + (SELF_UNITS["TL"] if kind == "O1" else 0), 0
            return SELF_BODY[kind], tb

        def number(kind, tb, i=0):
            c, n = first(kind, tb)
            return n * SELF_PER + c + i

        def bank(kind, tb, i=0):
            return (first(kind, tb)[0] + i) % RING

        def uses(kind, tb, i=0):
            c, n = first(kind, tb)
            return n * (SELF_PER // RING) + (c + i) // RING

        def filled(eng, kind, tb, i=0):
            eng.wait_ge(s_full, number(kind, tb, i) + 1)

        def emptied(eng, kind, tb, i=0):
            eng.wait_ge(s_free[bank(kind, tb, i)], uses(kind, tb, i) + 1)

        def run(eng, body):
            body(0, tiles == 1)
            if tiles > 2:
                with eng.Fori(1, tiles - 1) as t:
                    body(t, False)
            if tiles > 1:
                body(tiles - 1, True)

        def piece(wq, wo, n):
            return wq[:, :, D * n:D * (n + 1)] if n < 6 else wo[:, KC * (n - 6):KC * (n - 5), :]

        def half(b):
            return slice(NQ * b, NQ * b + NQ)

        block = es.enter_context(nc.Block())

        @block.sync
        def _(sp):
            def inputs(t):
                sp.dma_start(oin[:, :, 0:NQ], o_scr[2 * t, :, :, :]).then_inc(s_oin, 16)
                sp.dma_start(oin[:, :, NQ:P], o_scr[2 * t + 1, :, :, :]).then_inc(s_oin, 16)
                sp.dma_start(xin[:, :], x[t, :, :]).then_inc(s_xin, 16)

            sp.sem_inc(s_lgo, 16)
            inputs(0)
            sp.dma_start(ident[:, :], ident_in).then_inc(s_const, 16)
            sp.dma_start(bos[:, 0, :], bo1.to_broadcast([P, D])).then_inc(s_const, 16)
            sp.dma_start(bos[:, 1, :], bo2.to_broadcast([P, D])).then_inc(s_const, 16)
            sp.dma_start(router_sb[:, :, :], router).then_inc(s_const, 16)

            def logits_out(t, tb):
                emptied(sp, "LG", tb)
                sp.dma_start(lg_scr[t, :, :], lg[:, :]).then_inc(s_lgo, 16)

            def body(t, last):
                if not last:
                    sp.wait_ge(s_var[0], t + 1)
                    inputs(t + 1)
                if not (isinstance(t, int) and t == 0):
                    logits_out(t - 1, t)

            run(sp, body)
            logits_out(tiles - 1, TAIL)
            sp.wait_ge(s_lgo, 16 * tiles + 16)

        @block.gpsimd
        def _(pool):
            nc.gpsimd.memset(prob[:, :, :], 0.0).then_inc(s_zero, 1)
            nc.gpsimd.memset(kbd[:, :, :], 0.0).then_inc(s_zero, 1)

        @block.scalar
        def _(act):
            def root(a, t):
                act.wait_ge(s_var[a], t + 1)
                nc.scalar.activation(rstd[:, a, :], rstd[:, a, :], ACT.Sqrt).then_inc(s_std[a], 1)

            def step(kind, t, tb):
                if kind == "O1":
                    root(0, t)
                elif kind == "TX":
                    filled(act, kind, tb)
                    nc.scalar.activation(xTh[:, :, :], ring[:, bank(kind, tb), :].rearrange("p (k n) -> p k n", k=KC),
                                         ACT.Copy).then_inc(s_xTh, 1)
                elif kind in ("QK", "V0", "V1"):
                    for i in range(SELF_UNITS[kind]):
                        project(kind, tb, i)
                elif kind == "TQ":
                    for i in range(2):
                        act.wait_ge(s_tq, 4 * t + i + 1)
                        nc.scalar.activation(qT[:, 4 * i:4 * i + 4, :],
                                             big[:, i, :].rearrange("p (r n) -> p r n", r=4), ACT.Copy).then_inc(s_qT, 1)
                elif kind == "SM":
                    for b in range(2):
                        act.wait_ge(s_sub, 2 * t + b + 1)
                        nc.scalar.activation(pc[half(b), :, :], pc[half(b), :, :], ACT.Exp, scale=SSCALE)\
                          .then_inc(s_exp, 1)
                elif kind == "LG":
                    filled(act, kind, tb)
                    act.wait_ge(s_lgo, 16 * t + 16)
                    nc.scalar.activation(lg[:, :], ring[:, bank(kind, tb), 0:E], ACT.Copy).then_inc(s_free[bank(kind, tb)], 1)
                elif kind == "TP":
                    for i in range(4):
                        filled(act, kind, tb, i)
                        if i >= 2:
                            act.wait_ge(s_pv, 4 * t + i - 1)
                        nc.scalar.activation(pT[:, i % 2, :, :], ring[:, bank(kind, tb, i), :]
                                             .rearrange("p (h n) -> p h n", h=4), ACT.Copy).then_inc(s_free[bank(kind, tb, i)], 1)
                        if i >= 1:
                            heads_hi(t, i - 1)
                    heads_hi(t, 3)
                elif kind == "O2":
                    root(1, t)
                    emptied(act, kind, tb)
                    act.dma_start(x2_scr[t, :, :], x2[:, :]).then_inc(s_x2o, 16)
                elif kind == "TL":
                    filled(act, kind, tb)
                    act.wait_ge(s_xn3, t + 1)
                    act.dma_start(xn_scr[t, :, :], xn3[:, :]).then_inc(s_xno, 16)
                    nc.scalar.activation(xn3T[:, :, :], ring[:, bank(kind, tb), :].rearrange("p (k n) -> p k n", k=KC),
                                         ACT.Copy).then_inc(s_free[bank(kind, tb)], 1)

            def project(kind, tb, i):
                n = {"QK": 0, "V0": 4, "V1": 5}[kind] + i
                filled(act, kind, tb, i)
                nc.scalar.activation(rows[:, n // 2, D * (n % 2):D * (n % 2 + 1)],
                                     ring[:, bank(kind, tb, i), :], ACT.Copy).then_inc(s_free[bank(kind, tb, i)], 1)

            def heads_hi(t, i):
                act.wait_ge(s_pv, 4 * t + i + 1)
                for hh in range(2):
                    src = big[half(hh), i, :].rearrange("p (r n) -> p r n", r=2)
                    ins = nc.scalar.activation(aTh[half(hh), 2 * i:2 * i + 2, :], src[:, :, P * hh:P * (hh + 1)], ACT.Copy)
                ins.then_inc(s_aTh, 1)

            for n in range(SELF_PIECES):
                act.wait_ge(s_weights[n + 1], 16)
                nc.scalar.activation(piece(wqh, woh, n), raw[n], ACT.Copy).then_inc(s_whi, 1)
                if n == 2:
                    step("O1", 0, PROLOGUE)
                    step("TX", 0, PROLOGUE)
                if 3 <= n < 7:
                    project("QK", PROLOGUE, n - 3)
            step("V0", 0, PROLOGUE)
            step("V1", 0, PROLOGUE)

            def body(t, last):
                for kind, shift in steps(t, last):
                    step(kind, t + shift, t)

            run(act, body)
            step("TL", tiles - 1, TAIL)
            step("LG", tiles - 1, TAIL)
            for s in (s_x2o, s_xno):
                act.wait_ge(s, 16 * tiles)

        @block.vector
        def _(dve):
            def layer_norm(a, t, src, dst, s_dst, out_wait=None):
                nc.vector.bn_stats(stat[:, a, :], src).then_inc(s_ln[a], 1)
                dve.wait_ge(s_ln[a], 3 * t + 1)
                nc.vector.memset(idle[:, a:a + 1], 0.0)
                nc.vector.bn_aggr(mv[:, a, :], stat[:, a, :]).then_inc(s_ln[a], 1)
                dve.wait_ge(s_ln[a], 3 * t + 2)
                nc.vector.tensor_scalar(rstd[:, a, :], mv[:, a, 1:2], EPS, None, ALU.add).then_inc(s_var[a], 1)
                dve.wait_ge(s_std[a], t + 1)
                nc.vector.reciprocal(rstd[:, a, :], rstd[:, a, :]).then_inc(s_ln[a], 1)
                dve.wait_ge(s_ln[a], 3 * t + 3)
                if out_wait is not None:
                    dve.wait_ge(*out_wait)
                nc.vector.tensor_scalar(dst, src, mv[:, a, 0:1], rstd[:, a, :], ALU.subtract, ALU.mult).then_inc(s_dst, 1)

            def step(kind, t, tb):
                if kind == "O1":
                    dve.wait_ge(s_xin, 16 * t + 16)
                    nc.vector.tensor_tensor(xb[:, :], xin[:, :], bos[:, 0, :], ALU.add).then_inc(s_xb, 1)
                    dve.wait_ge(s_xb, t + 1)
                    if not (isinstance(t, int) and t == 0):
                        dve.wait_ge(s_x1b, t)
                    filled(dve, kind, tb)
                    nc.vector.tensor_tensor(x1[:, :], ring[:, bank(kind, tb), :], xb[:, :], ALU.add).then_inc(s_free[bank(kind, tb)], 1)
                    emptied(dve, kind, tb)
                    layer_norm(0, t, x1[:, :], xn[:, :], s_xn)
                elif kind == "TX":
                    dve.wait_ge(s_xTh, t + 1)
                    nc.vector.tensor_tensor(xTl[:, :, :], ring[:, bank(kind, tb), :].rearrange("p (k n) -> p k n", k=KC),
                                            xTh[:, :, :], ALU.subtract).then_inc(s_free[bank(kind, tb)], 1)
                elif kind == "TQ":
                    for i in range(2):
                        dve.wait_ge(s_tq, 4 * t + i + 3)
                        for hh in range(2):
                            ins = nc.vector.tensor_copy(kbd[half(hh), 4 * i:4 * i + 4, P * hh:P * (hh + 1)],
                                                        big[half(hh), 2 + i, :].rearrange("p (r n) -> p r n", r=4))
                        ins.then_inc(s_kbd, 1)
                    nc.vector.tensor_tensor(x1b[:, :], x1[:, :], bos[:, 1, :], ALU.add).then_inc(s_x1b, 1)
                elif kind == "S":
                    dve.wait_ge(s_s, t + 1)
                    nc.vector.tensor_reduce(mx[half(0), :], scores(0), AX.X, ALU.max).then_inc(s_sm, 1)
                elif kind == "SM":
                    for b in range(2):
                        if b:
                            nc.vector.tensor_reduce(mx[half(1), :], scores(1), AX.X, ALU.max).then_inc(s_sm, 1)
                        dve.wait_ge(s_sm, 4 * t + b + 1)
                        nc.vector.tensor_tensor(pc[half(b), :, :], scores(b),
                                                mx[half(b), :].unsqueeze(2).to_broadcast([NQ, H, NQ]),
                                                ALU.subtract).then_inc(s_sub, 1)
                    dve.wait_ge(s_exp, 2 * t + 2)
                    nc.vector.tensor_reduce(tot[:, 0, :], pc[:, :, :], AX.X, ALU.add).then_inc(s_sm, 1)
                    dve.wait_ge(s_sm, 4 * t + 3)
                    nc.vector.reciprocal(tot[:, 1, :], tot[:, 0, :]).then_inc(s_sm, 1)
                    dve.wait_ge(s_sm, 4 * t + 4)
                    for b in range(2):
                        nc.vector.tensor_tensor(prob[half(b), :, half(b)], pc[half(b), :, :],
                                                tot[half(b), 1, :].unsqueeze(2).to_broadcast([NQ, H, NQ]),
                                                ALU.mult).then_inc(s_prob, 1)
                elif kind == "TP":
                    for i in range(4):
                        dve.wait_ge(s_aTh, 4 * t + i + 1)
                        for hh in range(2):
                            src = big[half(hh), i, :].rearrange("p (r n) -> p r n", r=2)
                            at = (half(hh), slice(2 * i, 2 * i + 2), slice(None))
                            ins = nc.vector.tensor_tensor(aTl[at], src[:, :, P * hh:P * (hh + 1)], aTh[at], ALU.subtract)
                        ins.then_inc(s_aTl, 1)
                elif kind == "O2":
                    filled(dve, kind, tb)
                    if not (isinstance(t, int) and t == 0):
                        dve.wait_ge(s_x2o, 16 * t)
                    dve.wait_ge(s_x1b, t + 1)
                    nc.vector.tensor_tensor(x2[:, :], ring[:, bank(kind, tb), :], x1b[:, :], ALU.add).then_inc(s_free[bank(kind, tb)], 1)
                    emptied(dve, kind, tb)
                    layer_norm(1, t, x2[:, :], xn3[:, :], s_xn3,
                               None if isinstance(t, int) and t == 0 else (s_xno, 16 * t))

            def scores(b):
                return big[half(b), :, :].rearrange("p a (h n) -> p (a h) n", h=4)[:, :, half(b)]

            for n in range(SELF_PIECES):
                dve.wait_ge(s_whi, n + 1)
                nc.vector.tensor_tensor(lo[n][:, :, :], raw[n], piece(wqh, woh, n), ALU.subtract).then_inc(s_wlo, 1)
                if n == 2:
                    dve.wait_ge(s_const, CONSTS)
                    step("O1", 0, PROLOGUE)
                    step("TX", 0, PROLOGUE)
            dve.wait_ge(s_zero, 2)

            def body(t, last):
                for kind, shift in steps(t, last):
                    step(kind, t + shift, t)

            run(dve, body)

        @block.tensor
        def _(pe):
            def product3(out, lh, ll, rh, rl, start, stop):
                nc.tensor.matmul(out, lh, rh, start=start, stop=False)
                nc.tensor.matmul(out, lh, rl, start=False, stop=False)
                return nc.tensor.matmul(out, ll, rh, start=False, stop=stop)

            def free_bank(kind, tb, i=0):
                n = uses(kind, tb, i)
                if not (isinstance(n, int) and n == 0):
                    pe.wait_ge(s_free[bank(kind, tb, i)], n)

            def turn4(dst, src):
                for k in range(KC):
                    ins = nc.tensor.transpose(dst[:, P * k:P * (k + 1)], src[:, P * k:P * (k + 1)], ident[:, :])
                return ins

            def step(kind, t, tb):
                if SELF_UNITS[kind]:
                    dst = ring[:, bank(kind, tb), :]
                if kind == "O1":
                    free_bank(kind, tb)
                    pe.wait_ge(s_oin, 32 * t + 32)
                    for k in range(KC):
                        ins = nc.tensor.matmul(dst, oin[:, k, :], wo1_sb[:, k, :], start=(k == 0), stop=(k == KC - 1))
                    ins.then_inc(s_full, 1)
                elif kind == "TX":
                    free_bank(kind, tb)
                    pe.wait_ge(s_xn, t + 1)
                    turn4(dst, xn).then_inc(s_full, 1)
                elif kind in ("QK", "V0", "V1"):
                    emptied(pe, "TX", tb)
                    n0 = {"QK": 0, "V0": 4, "V1": 5}[kind]
                    for i in range(SELF_UNITS[kind]):
                        free_bank(kind, tb, i)
                        n = n0 + i
                        if isinstance(t, int) and t == 0:
                            pe.wait_ge(s_wlo, n + 1)
                        for k in range(KC):
                            w = (slice(None), k, slice(D * n, D * (n + 1)))
                            ins = product3(ring[:, bank(kind, tb, i), :], xTh[:, k, :], xTl[:, k, :], wqh[w], lo[n][:, k, :],
                                           k == 0, k == KC - 1)
                        ins.then_inc(s_full, 1)
                elif kind == "TQ":
                    for i in range(4):
                        emptied(pe, "QK", tb - 1, i)
                        turn4(big[:, i, :], rows[:, i // 2, D * (i % 2):D * (i % 2 + 1)]).then_inc(s_tq, 1)
                elif kind == "S":
                    pe.wait_ge(s_qT, 2 * t + 2)
                    pe.wait_ge(s_kbd, 2 * t + 2)
                    for i in range(4):
                        for r in range(2):
                            ins = nc.tensor.matmul(big[:, i, 256 * r:256 * (r + 1)], qT[:, 2 * i + r, :],
                                                   kbd[:, 2 * i + r, :], start=True, stop=True)
                    ins.then_inc(s_s, 1)
                elif kind == "TP":
                    def turn(i):
                        free_bank(kind, tb, i)
                        turn4(ring[:, bank(kind, tb, i), :],
                              prob[:, 4 * i:4 * i + 4, :].rearrange("p h n -> p (h n)")).then_inc(s_full, 1)

                    def meet(i):
                        emptied(pe, kind, tb, i)
                        for r in range(2):
                            pr = 2 * i + r
                            ins = nc.tensor.matmul(big[:, i, 256 * r:256 * (r + 1)], rows[:, 2, P * pr:P * (pr + 1)],
                                                   pT[:, i % 2, 2 * r:2 * r + 2, :], start=True, stop=True)
                        ins.then_inc(s_pv, 1)

                    pe.wait_ge(s_prob, 2 * t + 2)
                    emptied(pe, "V1", tb - 1)
                    turn(0)
                    for i in range(1, 4):
                        turn(i)
                        meet(i - 1)
                    meet(3)
                elif kind == "O2":
                    if isinstance(t, int) and t == 0:
                        pe.wait_ge(s_wlo, 8)
                    free_bank(kind, tb)
                    pe.wait_ge(s_aTl, 4 * t + 4)
                    for k in range(KI):
                        lo2 = lo[6 + k // KC][:, k % KC, :]
                        ins = product3(dst, aTh[:, k, :], aTl[:, k, :], woh[:, k, :], lo2, k == 0, k == KI - 1)
                    ins.then_inc(s_full, 1)
                elif kind == "TL":
                    free_bank(kind, tb)
                    pe.wait_ge(s_xn3, t + 1)
                    turn4(dst, xn3).then_inc(s_full, 1)
                elif kind == "LG":
                    free_bank(kind, tb)
                    emptied(pe, "TL", tb)
                    for k in range(KC):
                        ins = nc.tensor.matmul(dst[:, 0:E], xn3T[:, k, :], router_sb[:, k, :], start=(k == 0),
                                               stop=(k == KC - 1))
                    ins.then_inc(s_full, 1)

            pe.wait_ge(s_const, CONSTS)
            pe.wait_ge(s_weights[0], 16)
            for kind in SELF_PROLOGUE:
                step(kind, 0, PROLOGUE)

            def body(t, last):
                for kind, shift in steps(t, last):
                    step(kind, t + shift, t)

            run(pe, body)
            step("TL", tiles - 1, TAIL)
            step("LG", tiles - 1, TAIL)


G = 8
SLOTS = E * CAP


class ExpertWeights:

    def __init__(self, nc, es):
        def sb(name, shape, dt=F32):
            return es.enter_context(nc.sbuf_tensor(name, shape, dt))

        def sem(name):
            return es.enter_context(nc.semaphore(name))

        self.raw01 = sb("ex_raw01", [P, 2, 2 * KC * P])
        self.rawo = sb("ex_rawo", [P, 2, D])
        self.w01h = sb("ex_w01h", [P, 2, 2, KC, P], F32R)
        self.w01l = sb("ex_w01l", [P, 2, 2, KC, P], F32R)
        self.woh = sb("ex_woh", [P, 2, D], F32R)
        self.wol = sb("ex_wol", [P, 2, D], F32R)
        self.s_r01 = [sem("ex_r01a"), sem("ex_r01b")]
        self.s_ro = [sem("ex_roa"), sem("ex_rob")]
        self.s_h01 = sem("ex_h01")
        self.s_l01 = sem("ex_l01")
        self.s_ho = sem("ex_ho")
        self.s_lo = sem("ex_lo")

    def flat01(self, t, par):
        return t[:, par, :, :, :].rearrange("p a k n -> p (a k n)")


def experts(nc, x2_scr, xn_scr, lg_scr, w01, wout, tri_in, rowc_in, ident_in, eo_scr, out):
    with ExitStack() as es:
        def sb(name, shape, dt=F32):
            return es.enter_context(nc.sbuf_tensor(name, shape, dt))

        xeh = sb("mo_xeh", [P, KC, E, ROWS], F32R)
        xel = sb("mo_xel", [P, KC, E, ROWS], F32R)
        gates = sb("mo_gates", [P, G, SLOTS])
        ident = sb("mo_ident", [P, P])
        w = ExpertWeights(nc, es)
        route(nc, xn_scr, lg_scr, tri_in, rowc_in, ident_in, w01, wout, xeh, xel, gates, ident, w)
        run_experts(nc, x2_scr, w01, wout, eo_scr, xeh, xel, gates, ident, w, out)


def route(nc, xn_scr, lg_scr, tri_in, rowc_in, ident_in, w01, wout, xeh, xel, gates, ident, w):
    with ExitStack() as es:
        def sb(name, shape, dt=F32):
            return es.enter_context(nc.sbuf_tensor(name, shape, dt))

        def sem(name):
            return es.enter_context(nc.semaphore(name))

        GE = [P, G, E]
        lg = sb("ro_lg", GE)
        xn = sb("ro_xn", [P, G, D])
        tri = sb("ro_tri", [P, 2, P])
        rowc = sb("ro_rowc", [P, E + CAP])
        top = sb("ro_top", [P, 2, G])
        ex = sb("ro_ex", GE)
        raw = sb("ro_raw", GE)
        rest = sb("ro_rest", GE)
        eq = sb("ro_eq", GE)
        cand = sb("ro_cand", GE)
        pick = sb("ro_pick", [P, G])
        mask = sb("ro_mask", [P, 2, G, E])
        kept = sb("ro_kept", [P, 2, G, E])
        pos = sb("ro_pos", [P, 2, G])
        slot1 = sb("ro_slot1", [P, 2, G, CAP])
        small = sb("ro_small", [P, 2, G])
        scaled = sb("ro_scaled", [P, 2, G, E])
        parts = sb("ro_parts", [P, 2, G, SLOTS])
        disp = sb("ro_disp", [P, G, SLOTS])
        pp = es.enter_context(nc.psum_tensor("ro_pp", [P, 2, 512], F32))
        pd = es.enter_context(nc.psum_tensor("ro_pd", [P, 4, 512], F32))

        s_in = sem("ro_in")
        s_xn = sem("ro_xn_in")
        s_v = sem("ro_v")
        s_d = sem("ro_d")
        s_ex = sem("ro_ex_ready")
        s_m = sem("ro_m")
        s_p = sem("ro_p")
        s_gates = sem("ro_gates")
        s_slot = sem("ro_slot")
        s_first = sem("ro_first")
        s_disp = sem("ro_disp_ready")
        s_x = sem("ro_x")
        s_xh = sem("ro_xh")
        s_xl = sem("ro_xl")
        block = es.enter_context(nc.Block())

        def over(a, n):
            return a.unsqueeze(2).to_broadcast([P, G, n])

        @block.sync
        def _(sp):
            sp.dma_start(lg[:, :, :], lg_scr.rearrange("g p e -> p g e")).then_inc(s_in, 16)
            sp.dma_start(rowc[:, :], rowc_in).then_inc(s_in, 16)
            sp.dma_start(tri[:, :, :], tri_in).then_inc(s_in, 16)
            sp.dma_start(ident[:, :], ident_in).then_inc(s_in, 16)
            sp.dma_start(xn[:, :, :], xn_scr.rearrange("g p m -> p g m")).then_inc(s_xn, 16)
            for n in range(2):
                sp.dma_start(w.raw01[:, n, :], w01[n, :, :]).then_inc(w.s_r01[n], 16)
                sp.dma_start(w.rawo[:, n, :], wout[n, :, :]).then_inc(w.s_ro[n], 16)

        def part(eng, i, g):
            return eng.tensor_tensor(parts[:, i, g, :].rearrange("p (e c) -> p e c", e=E),
                                     scaled[:, i, g, :].unsqueeze(2).to_broadcast([P, E, CAP]),
                                     slot1[:, i, g, :].unsqueeze(1).to_broadcast([P, E, CAP]), ALU.mult)

        @block.gpsimd
        def _(pool):
            pool.wait_ge(s_slot, 1)
            for g in range(G):
                part(nc.gpsimd, 0, g).then_inc(s_first, 1)
            pool.wait_ge(w.s_h01, 1)
            nc.gpsimd.tensor_tensor(w.flat01(w.w01l, 0), w.raw01[:, 0, :], w.flat01(w.w01h, 0), ALU.subtract)\
              .then_inc(w.s_l01, 1)
            pool.wait_ge(w.s_ho, 1)
            nc.gpsimd.tensor_tensor(w.wol[:, 0, :], w.rawo[:, 0, :], w.woh[:, 0, :], ALU.subtract).then_inc(w.s_lo, 1)
            pool.wait_ge(w.s_h01, 2)
            nc.gpsimd.tensor_tensor(w.flat01(w.w01l, 1), w.raw01[:, 1, :], w.flat01(w.w01h, 1), ALU.subtract)\
              .then_inc(w.s_l01, 1)

        def rows_of(n, k):
            return pd[:, n % 4, 256 * k:256 * (k + 1)].rearrange("p (e c) -> p e c", e=E)

        @block.scalar
        def _(act):
            act.wait_ge(s_d, 1)
            nc.scalar.activation(ex[:, :, :], ex[:, :, :], ACT.Exp).then_inc(s_ex, 1)
            for n in range(2):
                act.wait_ge(w.s_r01[n], 16)
                nc.scalar.activation(w.flat01(w.w01h, n), w.raw01[:, n, :], ACT.Copy).then_inc(w.s_h01, 1)
                if n == 0:
                    act.wait_ge(w.s_ro[0], 16)
                    nc.scalar.activation(w.woh[:, 0, :], w.rawo[:, 0, :], ACT.Copy).then_inc(w.s_ho, 1)
            for n in range(2 * G):
                g, kk = n // 2, n % 2
                act.wait_ge(s_x, n + 1)
                for k in range(2):
                    ins = nc.scalar.activation(xeh[:, 2 * kk + k, :, CAP * g:CAP * (g + 1)], rows_of(n, k), ACT.Copy)
                ins.then_inc(s_xh, 1)

        @block.vector
        def _(dve):
            steps = [0]

            def after():
                dve.wait_ge(s_v, steps[0])

            def do(ins):
                steps[0] += 1
                ins.then_inc(s_v, 1)

            v = nc.vector
            em8 = rowc[:, 0:E].unsqueeze(1).to_broadcast(GE)
            dve.wait_ge(s_in, 64)
            do(v.tensor_reduce(pick[:, :], lg[:, :, :], AX.X, ALU.max))
            after()
            v.tensor_tensor(ex[:, :, :], lg[:, :, :], over(pick[:, :], E), ALU.subtract).then_inc(s_d, 1)
            dve.wait_ge(s_ex, 1)
            do(v.tensor_reduce(small[:, 0, :], ex[:, :, :], AX.X, ALU.add))
            after()
            do(v.reciprocal(small[:, 1, :], small[:, 0, :]))
            after()
            do(v.tensor_tensor(raw[:, :, :], ex[:, :, :], over(small[:, 1, :], E), ALU.mult))
            after()
            for i, src in enumerate((raw, rest)):
                if i:
                    do(v.tensor_tensor(cand[:, :, :], raw[:, :, :], mask[:, 0, :, :], ALU.mult))
                    after()
                    do(v.tensor_tensor(rest[:, :, :], raw[:, :, :], cand[:, :, :], ALU.subtract))
                    after()
                do(v.tensor_reduce(top[:, i, :], src[:, :, :], AX.X, ALU.max))
                after()
                do(v.tensor_tensor(eq[:, :, :], src[:, :, :], over(top[:, i, :], E), ALU.is_equal))
                after()
                do(v.tensor_tensor(cand[:, :, :], eq[:, :, :], em8, ALU.mult))
                after()
                do(v.tensor_reduce(pick[:, :], cand[:, :, :], AX.X, ALU.min))
                after()
                v.tensor_tensor(mask[:, i, :, :], over(pick[:, :], E), em8, ALU.is_equal).then_inc(s_m, 1)
                dve.wait_ge(s_m, i + 1)
            for i in range(2):
                dve.wait_ge(s_p, i + 1)
                p = pp[:, i, 0:G * E].rearrange("p (g e) -> p g e", g=G)
                v.scalar_tensor_tensor(kept[:, i, :, :].rearrange("p g e -> p (g e)"), pp[:, i, 0:G * E], float(CAP),
                                       mask[:, i, :, :].rearrange("p g e -> p (g e)"), ALU.is_lt, ALU.mult)\
                 .then_inc(s_m, 1)
                dve.wait_ge(s_m, i + 3)
                do(v.tensor_tensor(cand[:, :, :], p, kept[:, i, :, :], ALU.mult))
                after()
                do(v.tensor_reduce(pos[:, i, :], cand[:, :, :], AX.X, ALU.add))
                after()
                do(v.tensor_tensor(slot1[:, i, :, :], rowc[:, E:E + CAP].unsqueeze(1).to_broadcast([P, G, CAP]),
                                   over(pos[:, i, :], CAP), ALU.is_equal))
                v.tensor_tensor(scaled[:, i, :, :], kept[:, i, :, :], over(top[:, i, :], E), ALU.mult).then_inc(s_slot, 1)
            after()
            dve.wait_ge(s_slot, 2)
            for g in range(G):
                do(part(v, 1, g))
            for g in range(G):
                dve.wait_ge(s_first, g + 1)
                if g == 0:
                    after()
                v.tensor_tensor(gates[:, g, :], parts[:, 0, g, :], parts[:, 1, g, :], ALU.add).then_inc(s_gates, 1)
                if g:
                    dve.wait_ge(s_gates, g)
                    v.tensor_scalar(disp[:, g - 1, :], gates[:, g - 1, :], 0.0, None, ALU.not_equal).then_inc(s_disp, 1)
            dve.wait_ge(s_gates, G)
            v.tensor_scalar(disp[:, G - 1, :], gates[:, G - 1, :], 0.0, None, ALU.not_equal).then_inc(s_disp, 1)
            for n in range(2 * G):
                g, kk = n // 2, n % 2
                dve.wait_ge(s_xh, n + 1)
                for k in range(2):
                    at = (slice(None), 2 * kk + k, slice(None), slice(CAP * g, CAP * (g + 1)))
                    ins = v.tensor_tensor(xel[at], rows_of(n, k), xeh[at], ALU.subtract)
                ins.then_inc(s_xl, 1)

        @block.tensor
        def _(pe):
            pe.wait_ge(s_in, 64)
            pe.wait_ge(s_m, 1)
            nc.tensor.matmul(pp[:, 0, 0:G * E], tri[:, 0, :], mask[:, 0, :, :].rearrange("p g e -> p (g e)"),
                             start=True, stop=True).then_inc(s_p, 1)
            pe.wait_ge(s_m, 3)
            nc.tensor.matmul(pp[:, 1, 0:G * E], tri[:, 0, :], mask[:, 1, :, :].rearrange("p g e -> p (g e)"),
                             start=True, stop=False)
            nc.tensor.matmul(pp[:, 1, 0:G * E], tri[:, 1, :], kept[:, 0, :, :].rearrange("p g e -> p (g e)"),
                             start=False, stop=True).then_inc(s_p, 1)
            pe.wait_ge(s_xn, 16)
            for n in range(2 * G):
                g, kk = n // 2, n % 2
                pe.wait_ge(s_disp, g + 1)
                if n >= 4:
                    pe.wait_ge(s_xl, n - 3)
                for k in range(2):
                    m = P * (2 * kk + k)
                    ins = nc.tensor.matmul(pd[:, n % 4, 256 * k:256 * (k + 1)], xn[:, g, m:m + P], disp[:, g, :],
                                           start=True, stop=True)
                ins.then_inc(s_x, 1)


def run_experts(nc, x2_scr, w01, wout, eo_scr, xeh, xel, gates, ident, w, out):
    with ExitStack() as es:
        def sb(name, shape, dt=F32):
            return es.enter_context(nc.sbuf_tensor(name, shape, dt))

        def sem(name):
            return es.enter_context(nc.semaphore(name))

        combT = sb("ex_combT", [P, 2, G, P])
        gelu = sb("ex_gelu", [P, 2, ROWS])
        hid = sb("ex_hid", [P, 2, ROWS])
        hh = sb("ex_hh", [P, 2, ROWS], F32R)
        hl = sb("ex_hl", [P, 2, ROWS], F32R)
        eo = sb("ex_eo", [P, 2, D])
        eog = sb("ex_eog", [P, 2, G, D])
        x2 = sb("ex_x2", [P, G, D])
        banks = es.enter_context(nc.psum_tensor("ex_banks", [P, 8, 512], F32))
        up = banks[:, 0:2, :]
        acc = banks[:, 2:4, :]
        comb = banks[:, 4:8, :]

        s_up = sem("ex_up_full")
        s_gelu = sem("ex_gelu_ready")
        s_hh = sem("ex_hh_ready")
        s_hl = sem("ex_hl_ready")
        s_down = sem("ex_down")
        s_eo = sem("ex_eo_ready")
        s_eoo = sem("ex_eo_out")
        s_eog = [sem("ex_eog0"), sem("ex_eog1"), sem("ex_eog2")]
        s_x2 = sem("ex_x2_in")
        s_t = sem("ex_t")
        s_tc = sem("ex_tc")
        s_c = sem("ex_c")
        s_sum = sem("ex_sum")
        s_out = sem("ex_out")

        def pieces(eng, e, last, step):
            half = e * (FC // 2)
            step(half, 1, e, False, False, False, False)
            with eng.Fori(1, FC // 2 - 1) as j:
                step(half + j, 0, e, False, False, False, False)
                step(half + j, 1, e, False, False, False, False)
            step(half + (FC // 2 - 1), 0, e, False, False, last, False)
            step(half + (FC // 2 - 1), 1, e, False, True, last, last)
            if not last:
                step(half + FC // 2, 0, e + 1, True, False, False, False)

        def all_pieces(eng, step):
            step(0, 0, 0, True, False, False, False)
            with eng.Fori(0, E - 1) as e:
                pieces(eng, e, False, step)
            pieces(eng, E - 1, True, step)

        block = es.enter_context(nc.Block())

        @block.sync
        def _(sp):
            def step(half, par, e, head, tail, no_next2, no_next):
                n = half * 2 + par
                if not no_next2:
                    sp.wait_ge(w.s_l01, n + 1)
                    sp.dma_start(w.raw01[:, par, :], w01[n + 2, :, :]).then_inc(w.s_r01[par], 16)
                    sp.wait_ge(w.s_lo, n + 1)
                    sp.dma_start(w.rawo[:, par, :], wout[n + 2, :, :]).then_inc(w.s_ro[par], 16)

            all_pieces(sp, step)
            sp.wait_ge(s_eo, 2 * E)
            for g in range(G // 2):
                sp.dma_start(eog[P - CAP:P, 1, g:G:G // 2, :], eo[CAP * g:CAP * (g + 1), :, :]).then_inc(s_eog[2], 16)
            for g in range(0, G, 2):
                sp.wait_ge(s_sum, g + 1)
                sp.dma_start(out[g, :, :], x2[:, g, :]).then_inc(s_out, 16)
            sp.wait_ge(s_out, 16 * G)

        @block.gpsimd
        def _(pool):
            pool.dma_start(x2[:, :, :], x2_scr.rearrange("g p m -> p g m")).then_inc(s_x2, 16)
            for e in range(E - 1):
                pool.wait_ge(s_eoo, 32 * e + 64)
                q = CAP * (e % 4)
                pool.dma_start(eog[q:q + CAP, e // 4, :, :], eo_scr[e, :, :].rearrange("(g c) m -> c g m", c=CAP))\
                    .then_inc(s_eog[e // 4], 16)

        @block.scalar
        def _(act):
            def hi01(par, count):
                act.wait_ge(w.s_r01[par], count)
                nc.scalar.activation(w.flat01(w.w01h, par), w.raw01[:, par, :], ACT.Copy).then_inc(w.s_h01, 1)

            def hio(par, count):
                act.wait_ge(w.s_ro[par], count)
                nc.scalar.activation(w.woh[:, par, :], w.rawo[:, par, :], ACT.Copy).then_inc(w.s_ho, 1)

            def step(half, par, e, head, tail, no_next2, no_next):
                n = half * 2 + par
                earlier = head and not isinstance(e, int)
                act.wait_ge(s_up, n + 1)
                nc.scalar.activation(gelu[:, par, :], up[:, par, 0:ROWS], ACT.Gelu_apprx_tanh).then_inc(s_gelu, 1)
                if not no_next2:
                    hi01(par, half * 16 + 32)
                if earlier:
                    act.wait_ge(s_down, n + 1)
                    act.wait_ge(s_eoo, 32 * e)
                    nc.scalar.activation(eo[:, 0, :], acc[:, 0, :], ACT.Copy).then_inc(s_eo, 1)
                if not no_next:
                    act.wait_ge(s_down, n + 1)
                    hio(1 - par, half * 16 + 16 * (1 + par))
                if earlier:
                    act.wait_ge(s_eo, 2 * e)
                    for r in range(2):
                        act.dma_start(eo_scr[e - 1, P * r:P * (r + 1), :], eo[:, r, :]).then_inc(s_eoo, 16)

            act.sem_inc(s_eoo, 32)
            for i in range(4):
                act.wait_ge(s_t, i + 1)
                nc.scalar.activation(combT[:, :, 2 * i:2 * i + 2, :].rearrange("p h g n -> p g h n"),
                                     comb[:, i, :].rearrange("p (g h n) -> p g h n", g=2, h=2), ACT.Copy)\
                  .then_inc(s_tc, 1)
            all_pieces(act, step)
            act.wait_ge(s_down, E * FC + 1)
            act.wait_ge(s_eoo, 32 * E)
            nc.scalar.activation(eo[:, 0, :], acc[:, 0, :], ACT.Copy).then_inc(s_eo, 1)
            for g in range(1, G, 2):
                act.wait_ge(s_sum, g + 1)
                act.dma_start(out[g, :, :], x2[:, g, :]).then_inc(s_out, 16)

        @block.vector
        def _(dve):
            def lo01(par, count):
                dve.wait_ge(w.s_h01, count)
                nc.vector.tensor_tensor(w.flat01(w.w01l, par), w.raw01[:, par, :], w.flat01(w.w01h, par), ALU.subtract)\
                  .then_inc(w.s_l01, 1)

            def loo(par, count):
                dve.wait_ge(w.s_ho, count)
                nc.vector.tensor_tensor(w.wol[:, par, :], w.rawo[:, par, :], w.woh[:, par, :], ALU.subtract)\
                  .then_inc(w.s_lo, 1)

            def step(half, par, e, head, tail, no_next2, no_next):
                n = half * 2 + par
                dve.wait_ge(s_gelu, n + 1)
                nc.vector.tensor_tensor(hid[:, par, :], gelu[:, par, :], up[:, par, ROWS:2 * ROWS], ALU.mult)
                nc.vector.tensor_tensor(hh[:, par, :], gelu[:, par, :], up[:, par, ROWS:2 * ROWS], ALU.mult)\
                  .then_inc(s_hh, 1)
                dve.wait_ge(s_hh, n + 2)
                nc.vector.tensor_tensor(hl[:, par, :], hid[:, par, :], hh[:, par, :], ALU.subtract).then_inc(s_hl, 1)
                if not no_next2:
                    lo01(par, n + 3)
                if head and not isinstance(e, int):
                    dve.wait_ge(s_down, n + 1)
                    dve.wait_ge(s_eoo, 32 * e)
                    nc.vector.tensor_copy(eo[:, 1, :], acc[:, 1, :]).then_inc(s_eo, 1)
                if not no_next:
                    loo(1 - par, n + 2)

            dve.sem_inc(s_hh, 1)
            all_pieces(dve, step)
            dve.wait_ge(s_down, E * FC + 1)
            dve.wait_ge(s_eoo, 32 * E)
            nc.vector.tensor_copy(eo[:, 1, :], acc[:, 1, :]).then_inc(s_eo, 1)
            dve.wait_ge(s_x2, 16)
            for g in range(G):
                dve.wait_ge(s_c, g + 1)
                nc.vector.tensor_tensor(x2[:, g, :], x2[:, g, :], banks[:, g, :], ALU.add).then_inc(s_sum, 1)

        @block.tensor
        def _(pe):
            def product3(out, lh, ll, rh, rl, start, stop):
                nc.tensor.matmul(out, lh, rh, start=start, stop=False)
                nc.tensor.matmul(out, lh, rl, start=False, stop=False)
                return nc.tensor.matmul(out, ll, rh, start=False, stop=stop)

            def first_products(n, par, e):
                pe.wait_ge(w.s_l01, n + 1)
                for a in range(2):
                    for k in range(KC):
                        ins = product3(up[:, par, ROWS * a:ROWS * (a + 1)], w.w01h[:, par, a, k, :],
                                       w.w01l[:, par, a, k, :], xeh[:, k, e, :], xel[:, k, e, :], k == 0, k == KC - 1)
                ins.then_inc(s_up, 1)

            def step(half, par, e, head, tail, no_next2, no_next):
                n = half * 2 + par
                if not no_next:
                    pe.wait_ge(s_hh, n + 1)
                    first_products(n + 1, 1 - par, e + 1 if tail else e)
                if head and not isinstance(e, int):
                    pe.wait_ge(s_eo, 2 * e)
                pe.wait_ge(w.s_lo, n + 1)
                pe.wait_ge(s_hl, n + 1)
                for r in range(2):
                    at = (slice(None), par, slice(P * r, P * (r + 1)))
                    ins = product3(acc[:, r, :], hh[at], hl[at], w.woh[:, par, :], w.wol[:, par, :], head, tail)
                ins.then_inc(s_down, 1)

            pe.sem_inc(s_down, 1)
            for i in range(4):
                for j in range(4):
                    g, h = 2 * i + j // 2, j % 2
                    ins = nc.tensor.transpose(comb[:, i, P * j:P * (j + 1)], gates[:, g, P * h:P * (h + 1)], ident[:, :])
                ins.then_inc(s_t, 1)
            first_products(0, 0, 0)
            all_pieces(pe, step)
            pe.wait_ge(s_tc, 4)
            pe.wait_ge(s_eog[0], 64)
            for g in range(G):
                if g == 2:
                    pe.wait_ge(s_eo, 2 * E)
                nc.tensor.matmul(banks[:, g, :], combT[:, 0, g, :], eog[:, 0, g, :], start=True, stop=False)
            pe.wait_ge(s_eog[1], 48)
            pe.wait_ge(s_eog[2], 16 * (G // 2))
            for g in range(G):
                nc.tensor.matmul(banks[:, g, :], combT[:, 1, g, :], eog[:, 1, g, :], start=False, stop=True)\
                  .then_inc(s_c, 1)


def perceiver_layer(nc, x, ctx, xwq, xbq, xwk, xbk, xwv, xbv, xwo, xbo, wqkv, wo, bo, router, w01, wout,
                    ident, heads, tri, rowc, out):
    batches = ctx.shape[0]
    tiles = batches * NQ // P

    def scratch(name, shape):
        return nc.dram_tensor(name, shape, F32, kind="Internal").ap()

    q_scr = scratch("q_scratch", (batches, P, 4, NQ))
    o_scr = scratch("o_scratch", (batches, P, 4, NQ))
    x2_scr = scratch("x2_scratch", (tiles, P, D))
    xn_scr = scratch("xn_scratch", (tiles, P, D))
    lg_scr = scratch("lg_scratch", (tiles, P, E))
    eo_scr = scratch("eo_scratch", (E, ROWS, D))
    with ExitStack() as es:
        room, weights, weights_lo = self_weights(nc, es, wqkv, xwo, wo)
        cross_attention(nc, x, ctx, xwq, xbq, xwk, xbk, xwv, xbv, ident, heads, q_scr, o_scr, batches, room, weights)
        self_attention(nc, x, o_scr, weights, weights_lo, xbo, bo, router, ident, x2_scr, xn_scr, lg_scr, tiles)
    experts(nc, x2_scr, xn_scr, lg_scr, w01, wout, tri, rowc, ident, eo_scr, out)


def by_rows(w):
    return np.ascontiguousarray(w.reshape(-1, P, w.shape[1]).transpose(1, 0, 2))


def by_column(b):
    return np.ascontiguousarray(b.reshape(-1, P).T)


def constants():
    ident = np.eye(P, dtype=np.float32)
    heads = np.zeros((P, 2, P), np.float32)
    for pair in range(2):
        for h in range(2):
            at = DH * (2 * pair + h)
            heads[NQ * h:NQ * (h + 1), pair, at:at + DH] = 1
    eye2 = np.concatenate([np.eye(NQ), np.eye(NQ)]).astype(np.float32)
    heads = np.concatenate([heads.reshape(P, 2 * P), eye2], axis=1)
    tri = np.stack([np.triu(np.ones((P, P)), 1), np.ones((P, P))], axis=1).astype(np.float32)
    rowc = np.tile(np.concatenate([np.arange(E) - E, np.arange(CAP)]).astype(np.float32), (P, 1))
    return ident, heads, tri, rowc


def lay_out(x, ctx_1024, L0_xattn_wq, L0_xattn_bq, L0_xattn_wk, L0_xattn_bk, L0_xattn_wv, L0_xattn_bv, L0_xattn_wo,
            L0_xattn_bo, L0_attn_Wq, L0_attn_Wkv, L0_attn_Wo, L0_attn_bo, L0_ffn_router_w, L0_ffn_w0_kernel,
            L0_ffn_w1_kernel, L0_ffn_wo_kernel):
    b = ctx_1024.shape[0]
    ctx = np.zeros((b, NC * CH, D), np.float32)
    ctx[:, :NK] = ctx_1024
    ctx = np.ascontiguousarray(ctx.reshape(b, NC, CH, KC, P).transpose(0, 1, 4, 3, 2))
    hidden = L0_ffn_w0_kernel.shape[2]
    w01 = np.zeros((E, FC * P, 2, D), np.float32)
    w01[:, :hidden, 0] = L0_ffn_w0_kernel.transpose(0, 2, 1)
    w01[:, :hidden, 1] = L0_ffn_w1_kernel.transpose(0, 2, 1)
    w01 = np.ascontiguousarray(w01.reshape(E, FC, P, 2, KC, P).transpose(0, 1, 5, 3, 4, 2)).reshape(E * FC, P, 2 * KC * P)
    wout = np.zeros((E, FC * P, D), np.float32)
    wout[:, :hidden] = L0_ffn_wo_kernel
    ident, heads, tri, rowc = constants()
    return {
        "x": x.reshape(-1, P, D), "ctx": ctx,
        "xwq": by_rows(L0_xattn_wq.T), "xbq": by_column(L0_xattn_bq),
        "xwk": by_rows(L0_xattn_wk.T), "xbk": by_column(L0_xattn_bk),
        "xwv": by_rows(L0_xattn_wv.T), "xbv": by_column(L0_xattn_bv),
        "xwo": by_rows(L0_xattn_wo.T), "xbo": L0_xattn_bo.reshape(1, D),
        "wqkv": by_rows(np.concatenate([L0_attn_Wq, L0_attn_Wkv], axis=1)),
        "wo": by_rows(L0_attn_Wo), "bo": L0_attn_bo.reshape(1, D), "router": by_rows(L0_ffn_router_w),
        "w01": w01, "wout": wout.reshape(E * FC, P, D),
        "ident": ident, "heads": heads, "tri": tri, "rowc": rowc,
    }


def kernel(**inputs):
    from concourse import bacc
    from concourse.bass_utils import run_bass_kernel_spmd

    inputs = {name: np.asarray(a) for name, a in inputs.items()}
    arrays = lay_out(**inputs)
    nc = bacc.Bacc("TRN2", target_bir_lowering=False, num_devices=1)
    arrays = {f"in_{name}": np.ascontiguousarray(a) for name, a in arrays.items()}
    args = [nc.dram_tensor(name, a.shape, mybir.dt.from_np(a.dtype), kind="ExternalInput").ap()
            for name, a in arrays.items()]
    shape = inputs["x"].shape
    out = nc.dram_tensor("out_x", (shape[0] * shape[1] // P, P, D), F32, kind="ExternalOutput").ap()
    perceiver_layer(nc, *args, out)
    got = run_bass_kernel_spmd(nc, [arrays], core_ids=[0])
    return got.results[0]["out_x"].reshape(shape)
```
